# Optimizing a Trainium2 kernel written in Bass

```python
import numpy as np
import jax
import jax.numpy as jnp

def _softmax(x, axis=-1):
    return jax.nn.softmax(x, axis=axis)

def _gelu(x):
    return jax.nn.gelu(x, approximate=True)

def _silu(x):
    return jax.nn.silu(x)

def _sigmoid(x):
    return jax.nn.sigmoid(x)

def _layernorm(x, axis=-1, eps=1e-05):
    m = jnp.mean(x, axis=axis, keepdims=True)
    v = jnp.var(x, axis=axis, keepdims=True)
    return (x - m) / jnp.sqrt(v + eps)

def _scatter_add(tgt, idx, src, axis=0):
    return tgt.at[idx].add(src)

def _segment_sum(src, seg, n):
    return jax.ops.segment_sum(src, seg, n)
kernel_name = 'mk_gnn_resnorm_d4_gnn_r64_d4fde3'

def setup_inputs(seed: int=0):
    np.random.seed(seed)
    _w = jnp.asarray

    def _rec_inputs():
        import jax
        import jax.numpy as jnp
        _gk = jax.random.key(seed)
        x = -0.000202 + 1 * jax.random.normal(jax.random.fold_in(_gk, 1), (50000, 128), jnp.float32)
        src = jax.random.randint(jax.random.fold_in(_gk, 2), (12500,), 0, 50000, jnp.int32)
        dst = jax.random.randint(jax.random.fold_in(_gk, 3), (12500,), 0, 50000, jnp.int32)
        _o = jnp.argsort(dst, stable=True)
        src = src[_o]
        dst = dst[_o]
        edge_attr_128 = -8.16379e-05 + 0.999858 * jax.random.normal(jax.random.fold_in(_gk, 12), (12500, 128), jnp.float32)
        edge_weight = jax.random.uniform(jax.random.fold_in(_gk, 14), (12500,), jnp.float32, 0.0, 0.999998)
        return (x, src, dst, edge_attr_128, edge_weight)
    x, src, dst, edge_attr_128, edge_weight = _rec_inputs()

    def _L0_gnn_setup():
        import jax, jax.numpy as jnp
        import numpy as np
        N_NODES = 50000
        N_EDGES = 12500
        NODE_DIM = 128
        EDGE_DIM = 128
        OUT_FEATS = 128
        key = jax.random.key(seed)
        k1, k2, k3, k4, k5, k6 = jax.random.split(key, 6)
        node_features = jax.random.normal(k1, (N_NODES, NODE_DIM), dtype=jnp.float32)
        edge_features = jax.random.normal(k2, (N_EDGES, EDGE_DIM), dtype=jnp.float32)
        src = jax.random.randint(k3, (N_EDGES,), 0, N_NODES, dtype=jnp.int32)
        dst = jax.random.randint(k4, (N_EDGES,), 0, N_NODES, dtype=jnp.int32)
        in_dim = 2 * NODE_DIM + EDGE_DIM
        W = jax.random.normal(k5, (OUT_FEATS, in_dim), dtype=jnp.float32) / np.sqrt(in_dim)
        b = jax.random.normal(k6, (OUT_FEATS,), dtype=jnp.float32) * 0.01
        return {'node_features': node_features, 'edge_features': edge_features, 'src': src, 'dst': dst, 'W': W, 'b': b}
    _L0_gnn_all = _L0_gnn_setup()
    _L0_gnn_in = {k: v for k, v in _L0_gnn_all.items() if k in ('W', 'b')}
    del _L0_gnn_all

    def _L1_gnn_setup():
        import jax, jax.numpy as jnp
        import numpy as np
        N = 625
        E = 10000
        IN = 128
        H = 8
        F = 16
        NEG_SLOPE = 0.2
        BN_EPS = 1e-05
        SOFTMAX_EPS = 1e-16

        def _gat_layer(x, src, dst, W, att_src, att_dst, bias, bn_gamma, bn_beta):
            n = x.shape[0]
            xp = (x @ W).reshape(n, H, F)
            a_s = jnp.einsum('nhf,hf->nh', xp, att_src)
            a_d = jnp.einsum('nhf,hf->nh', xp, att_dst)
            e = jax.nn.leaky_relu(a_s[src] + a_d[dst], NEG_SLOPE)
            m = jax.ops.segment_max(e, dst, num_segments=n)
            m = jnp.where(jnp.isfinite(m), m, 0.0)
            p = jnp.exp(e - m[dst])
            s = jax.ops.segment_sum(p, dst, num_segments=n)
            alpha = p / (s[dst] + SOFTMAX_EPS)
            msg = alpha[:, :, None] * xp[src]
            out = jax.ops.segment_sum(msg, dst, num_segments=n)
            h = out.reshape(n, H * F) + bias
            mean = h.mean(axis=0)
            var = h.var(axis=0)
            h = (h - mean) * jax.lax.rsqrt(var + BN_EPS) * bn_gamma + bn_beta
            h = jax.nn.relu(h)
            return h + x
        key = jax.random.key(seed)
        ks = jax.random.split(key, 7)
        x = jax.random.normal(ks[0], (N, IN), dtype=jnp.float32)
        edge_index = jax.random.randint(ks[1], (2, E), 0, N, dtype=jnp.int32)
        W = jax.random.normal(ks[2], (IN, H * F), dtype=jnp.float32) * (1.0 / np.sqrt(IN))
        att_src = jax.random.normal(ks[3], (H, F), dtype=jnp.float32) * (1.0 / np.sqrt(F))
        att_dst = jax.random.normal(ks[4], (H, F), dtype=jnp.float32) * (1.0 / np.sqrt(F))
        bias = jnp.zeros((H * F,), dtype=jnp.float32)
        bn_gamma = jnp.ones((H * F,), dtype=jnp.float32)
        bn_beta = jnp.zeros((H * F,), dtype=jnp.float32)
        return {'x': x, 'edge_index': edge_index, 'W': W, 'att_src': att_src, 'att_dst': att_dst, 'bias': bias, 'bn_gamma': bn_gamma, 'bn_beta': bn_beta}
    _L1_gnn_all = _L1_gnn_setup()
    _L1_gnn_in = {k: v for k, v in _L1_gnn_all.items() if k in ('W', 'att_src', 'att_dst', 'bias', 'bn_gamma', 'bn_beta')}
    del _L1_gnn_all

    def _L2_gnn_setup():
        import jax, jax.numpy as jnp
        import numpy as np
        N_NODES = 50000
        N_EDGES = 9375
        D = 128
        D_OUT = 128
        key = jax.random.key(seed)
        ks = jax.random.split(key, 6)
        features = jax.random.normal(ks[0], (N_NODES, D), dtype=jnp.float32)
        edge_index = jax.random.randint(ks[1], (2, N_EDGES), 0, N_NODES, dtype=jnp.int64)

        def xavier(k, shape):
            gain = float(np.sqrt(2.0))
            fan_out, fan_in = shape
            bound = gain * float(np.sqrt(6.0 / (fan_in + fan_out)))
            return jax.random.uniform(k, shape, jnp.float32, -bound, bound)
        W_neigh = xavier(ks[2], (D, D))
        b_neigh = jnp.zeros((D,), jnp.float32)
        W_edge = xavier(ks[3], (D, 2 * D))
        b_edge = jnp.zeros((D,), jnp.float32)
        W_lin = xavier(ks[4], (D_OUT, 2 * D))
        b_lin = jnp.zeros((D_OUT,), jnp.float32)
        return {'features': features, 'edge_index': edge_index, 'W_neigh': W_neigh, 'b_neigh': b_neigh, 'W_edge': W_edge, 'b_edge': b_edge, 'W_lin': W_lin, 'b_lin': b_lin}
    _L2_gnn_all = _L2_gnn_setup()
    _L2_gnn_in = {k: v for k, v in _L2_gnn_all.items() if k in ('W_neigh', 'b_neigh', 'W_edge', 'b_edge', 'W_lin', 'b_lin')}
    del _L2_gnn_all

    def _L3_gnn_setup():
        import jax, jax.numpy as jnp
        import numpy as np
        N_NODES = 30000
        DEGREE = 16
        N_EDGES = N_NODES * DEGREE
        F = 128
        F_OUT = 128
        ONSET = 0.8
        CUTOFF = 1.0

        def _ssp(x):
            return jax.nn.softplus(x) - jnp.log(2.0).astype(x.dtype)

        def _smooth_cutoff(d):
            t = (d - ONSET) / (CUTOFF - ONSET)
            ramp = 0.5 * (jnp.cos(jnp.float32(np.pi) * t) + 1.0)
            return jnp.where(d < ONSET, 1.0, jnp.where(d > CUTOFF, 0.0, ramp))
        key = jax.random.key(seed)
        ks = jax.random.split(key, 10)
        h = jax.random.normal(ks[0], (N_NODES, F), dtype=jnp.float32)
        edge_feat = jax.random.normal(ks[1], (N_EDGES, F), dtype=jnp.float32)
        dist = jax.random.uniform(ks[2], (N_EDGES,), dtype=jnp.float32)
        src = jax.random.randint(ks[3], (N_EDGES,), 0, N_NODES, dtype=jnp.int32)
        dst = jnp.repeat(jnp.arange(N_NODES, dtype=jnp.int32), DEGREE)
        s = 1.0 / np.sqrt(F)
        W1 = jax.random.normal(ks[4], (F, F), dtype=jnp.float32) * s
        b1 = jnp.zeros((F,), dtype=jnp.float32)
        W2 = jax.random.normal(ks[5], (F, F), dtype=jnp.float32) * s
        b2 = jnp.zeros((F,), dtype=jnp.float32)
        W3 = jax.random.normal(ks[6], (F, F_OUT), dtype=jnp.float32) * s
        b3 = jnp.zeros((F_OUT,), dtype=jnp.float32)
        return {'h': h, 'edge_feat': edge_feat, 'dist': dist, 'src': src, 'dst': dst, 'W1': W1, 'b1': b1, 'W2': W2, 'b2': b2, 'W3': W3, 'b3': b3}
    _L3_gnn_all = _L3_gnn_setup()
    _L3_gnn_in = {k: v for k, v in _L3_gnn_all.items() if k in ('W1', 'b1', 'W2', 'b2', 'W3', 'b3')}
    del _L3_gnn_all
    return {'x': x, 'src': src, 'dst': dst, 'edge_attr_128': edge_attr_128, 'edge_weight': edge_weight, 'L0_gnn_W': _L0_gnn_in['W'], 'L0_gnn_b': _L0_gnn_in['b'], 'L1_gnn_W': _L1_gnn_in['W'], 'L1_gnn_att_src': _L1_gnn_in['att_src'], 'L1_gnn_att_dst': _L1_gnn_in['att_dst'], 'L1_gnn_bias': _L1_gnn_in['bias'], 'L1_gnn_bn_gamma': _L1_gnn_in['bn_gamma'], 'L1_gnn_bn_beta': _L1_gnn_in['bn_beta'], 'L2_gnn_W_neigh': _L2_gnn_in['W_neigh'], 'L2_gnn_b_neigh': _L2_gnn_in['b_neigh'], 'L2_gnn_W_edge': _L2_gnn_in['W_edge'], 'L2_gnn_b_edge': _L2_gnn_in['b_edge'], 'L2_gnn_W_lin': _L2_gnn_in['W_lin'], 'L2_gnn_b_lin': _L2_gnn_in['b_lin'], 'L3_gnn_W1': _L3_gnn_in['W1'], 'L3_gnn_b1': _L3_gnn_in['b1'], 'L3_gnn_W2': _L3_gnn_in['W2'], 'L3_gnn_b2': _L3_gnn_in['b2'], 'L3_gnn_W3': _L3_gnn_in['W3'], 'L3_gnn_b3': _L3_gnn_in['b3']}

def reference(x, src, dst, edge_attr_128, edge_weight, L0_gnn_W, L0_gnn_b, L1_gnn_W, L1_gnn_att_src, L1_gnn_att_dst, L1_gnn_bias, L1_gnn_bn_gamma, L1_gnn_bn_beta, L2_gnn_W_neigh, L2_gnn_b_neigh, L2_gnn_W_edge, L2_gnn_b_edge, L2_gnn_W_lin, L2_gnn_b_lin, L3_gnn_W1, L3_gnn_b1, L3_gnn_W2, L3_gnn_b2, L3_gnn_W3, L3_gnn_b3):
    import jax
    import jax.numpy as jnp

    def _L0_gnn_ref(node_features, edge_features, src, dst, W, b):
        import jax, jax.numpy as jnp
        import numpy as np
        N_NODES = 50000
        N_EDGES = 12500
        NODE_DIM = 128
        EDGE_DIM = 128
        OUT_FEATS = 128
        agg_src = jax.ops.segment_sum(node_features[src], dst, num_segments=N_NODES)
        agg_edge = jax.ops.segment_sum(edge_features, dst, num_segments=N_NODES)
        h = jnp.concatenate([node_features, agg_src, agg_edge], axis=1)
        h = h @ W.T + b
        return jax.nn.relu(h)

    def _L1_gnn_ref(x, edge_index, W, att_src, att_dst, bias, bn_gamma, bn_beta):
        import jax, jax.numpy as jnp
        import numpy as np
        N = 625
        E = 10000
        IN = 128
        H = 8
        F = 16
        NEG_SLOPE = 0.2
        BN_EPS = 1e-05
        SOFTMAX_EPS = 1e-16

        def _gat_layer(x, src, dst, W, att_src, att_dst, bias, bn_gamma, bn_beta):
            n = x.shape[0]
            xp = (x @ W).reshape(n, H, F)
            a_s = jnp.einsum('nhf,hf->nh', xp, att_src)
            a_d = jnp.einsum('nhf,hf->nh', xp, att_dst)
            e = jax.nn.leaky_relu(a_s[src] + a_d[dst], NEG_SLOPE)
            m = jax.ops.segment_max(e, dst, num_segments=n)
            m = jnp.where(jnp.isfinite(m), m, 0.0)
            p = jnp.exp(e - m[dst])
            s = jax.ops.segment_sum(p, dst, num_segments=n)
            alpha = p / (s[dst] + SOFTMAX_EPS)
            msg = alpha[:, :, None] * xp[src]
            out = jax.ops.segment_sum(msg, dst, num_segments=n)
            h = out.reshape(n, H * F) + bias
            mean = h.mean(axis=0)
            var = h.var(axis=0)
            h = (h - mean) * jax.lax.rsqrt(var + BN_EPS) * bn_gamma + bn_beta
            h = jax.nn.relu(h)
            return h + x
        n = x.shape[0]
        loops = jnp.arange(n, dtype=edge_index.dtype)
        src = jnp.concatenate([edge_index[0], loops])
        dst = jnp.concatenate([edge_index[1], loops])
        return _gat_layer(x, src, dst, W, att_src, att_dst, bias, bn_gamma, bn_beta)

    def _L2_gnn_ref(features, edge_index, W_neigh, b_neigh, W_edge, b_edge, W_lin, b_lin):
        import jax, jax.numpy as jnp
        import numpy as np
        N_NODES = 50000
        N_EDGES = 9375
        D = 128
        D_OUT = 128
        n = features.shape[0]
        dst = edge_index[0]
        src = edge_index[1]
        h = features @ W_neigh.T + b_neigh
        h_src = h[src]
        edge_feats = jnp.abs(h[dst] - h_src)
        new_h = jnp.concatenate([h_src, edge_feats], axis=-1) @ W_edge.T + b_edge
        seg_sum = jax.ops.segment_sum(new_h, dst, num_segments=n)
        cnt = jax.ops.segment_sum(jnp.ones((dst.shape[0],), jnp.float32), dst, num_segments=n)[:, None]
        s = (h + seg_sum) / jnp.maximum(cnt, 1.0)
        z = jnp.concatenate([features, s], axis=-1) @ W_lin.T + b_lin
        return z

    def _L3_gnn_ref(h, edge_feat, dist, src, dst, W1, b1, W2, b2, W3, b3):
        import jax, jax.numpy as jnp
        import numpy as np
        N_NODES = 30000
        DEGREE = 16
        N_EDGES = N_NODES * DEGREE
        F = 128
        F_OUT = 128
        ONSET = 0.8
        CUTOFF = 1.0

        def _ssp(x):
            return jax.nn.softplus(x) - jnp.log(2.0).astype(x.dtype)

        def _smooth_cutoff(d):
            t = (d - ONSET) / (CUTOFF - ONSET)
            ramp = 0.5 * (jnp.cos(jnp.float32(np.pi) * t) + 1.0)
            return jnp.where(d < ONSET, 1.0, jnp.where(d > CUTOFF, 0.0, ramp))
        N, Fdim = h.shape
        gamma = jnp.float32(Fdim)
        muk = jnp.linspace(0.0, 1.0, Fdim, dtype=jnp.float32)
        bf = jnp.exp(-gamma * (dist[:, None] - muk) ** 2)
        bf = _ssp(bf @ W1 + b1)
        bf = _ssp(bf @ W2 + b2)
        cut = _smooth_cutoff(dist)[:, None]
        msg = h[src] * edge_feat * bf * cut
        node_h = jax.ops.segment_prod(msg, dst, num_segments=N)
        return _ssp(node_h @ W3 + b3)
    edge_index = jnp.stack([src, dst])
    x = _layernorm(x + _L0_gnn_ref(x, edge_attr_128, src, dst, L0_gnn_W, L0_gnn_b), axis=-1)
    x = _layernorm(x + _L1_gnn_ref(x, edge_index, L1_gnn_W, L1_gnn_att_src, L1_gnn_att_dst, L1_gnn_bias, L1_gnn_bn_gamma, L1_gnn_bn_beta), axis=-1)
    x = _layernorm(x + _L2_gnn_ref(x, edge_index, L2_gnn_W_neigh, L2_gnn_b_neigh, L2_gnn_W_edge, L2_gnn_b_edge, L2_gnn_W_lin, L2_gnn_b_lin), axis=-1)
    x = _layernorm(x + _L3_gnn_ref(x, edge_attr_128, edge_weight, src, dst, L3_gnn_W1, L3_gnn_b1, L3_gnn_W2, L3_gnn_b2, L3_gnn_W3, L3_gnn_b3), axis=-1)
    return x

_drawn_inputs = setup_inputs


def setup_inputs(seed=0):
    import zlib

    import numpy as np

    out = dict(_drawn_inputs(seed))
    spreads = {'L1_gnn_bias': (0.0, 0.8),
     'L1_gnn_bn_gamma': (1.0, 0.2),
     'L1_gnn_bn_beta': (0.0, 0.1),
     'L2_gnn_b_neigh': (0.0, 0.1),
     'L2_gnn_b_edge': (0.0, 0.532),
     'L2_gnn_b_lin': (0.0, 0.1),
     'L3_gnn_b1': (0.0, 0.8),
     'L3_gnn_b2': (0.0, 0.8),
     'L3_gnn_b3': (0.0, 0.1)}
    factors = {'edge_weight': 3.587,
     'L0_gnn_b': 8.0,
     'L1_gnn_att_dst': 3.036,
     'L3_gnn_W1': 3.287,
     'L3_gnn_W2': 3.163}
    for name, (base, spread) in spreads.items():
        noise = np.random.default_rng([zlib.crc32(name.encode()), seed]).standard_normal(out[name].shape)
        drawn = base * np.exp(spread * noise) if base else spread * noise
        out[name] = jnp.asarray(drawn.astype(out[name].dtype))
    for name, factor in factors.items():
        out[name] = (out[name] * factor).astype(out[name].dtype)
    return out
```

```python
from contextlib import ExitStack, contextmanager

import concourse.bass as bass
from concourse import mybir

F32 = mybir.dt.float32
BF16 = mybir.dt.bfloat16
I32 = mybir.dt.int32
ALU = mybir.AluOpType
ACT = mybir.ActivationFunctionType
AX = mybir.AxisListType

D = 128
NT = 4
ROWS = 128 * NT
GT = 4
GE = 128 * GT
LN_EPS = 1e-5
BN_EPS = 1e-5
SLOPE = 0.2
SOFTMAX_EPS = 1e-16
NEG = -3.0e38
LOADS = 8
PER_STEP = 4
SKIP = float(1 << 20)


def shapes(n, edge_tiles, pads):
    full = n // ROWS
    rest = n - full * ROWS
    tail_t = next((t for t in range(1, NT + 1) if rest % t == 0 and rest // t <= 128), 0) if rest else 0
    hi = n // 128 + 1
    return {
        "n": n,
        "pads": pads,
        "et": edge_tiles,
        "ep": edge_tiles * 128,
        "hi": hi,
        "hc": -(-hi // 128),
        "full": full,
        "tail_t": tail_t,
        "tail_p": rest // tail_t if rest else 0,
        "eg": edge_tiles // GT,
        "tail_e": edge_tiles % GT,
    }


@contextmanager
def stage(nc):
    used = []

    def semaphore(name):
        used.append(nc.alloc_semaphore(name))
        return used[-1]

    with ExitStack() as ctx:
        yield ctx, semaphore
        if used:
            nc.clear_and_free_semaphores(used)
            nc.all_engine_barrier()


def rounds(engine, full, slots, body, tail=None):
    whole = full // slots
    if whole:
        with engine.Fori(0, whole) as r:
            for s in range(slots):
                body(r * slots + s, s, r)
    for g in range(whole * slots, full):
        body(g, g % slots, g // slots)
    if tail is not None:
        tail(full, full % slots, full // slots)


def staggered(engine, full, tail, slots, parts, warm=None):
    groups = full + (1 if tail else 0)
    most = max(lag for lag, *_ in parts)
    start = most + (warm or slots)
    turns = max((full - start) // slots, 0)

    def step(k, r=0):
        for lag, body, size, tail_size in parts:
            g = k - lag
            if 0 <= g < groups:
                whole = g < full
                body(g + r * slots, g % slots, g // slots + r, size if whole else tail_size)

    for k in range(start):
        step(k)
    if turns:
        with engine.Fori(0, turns) as r:
            for k in range(start, start + slots):
                step(k, r)
    for k in range(start + turns * slots, groups + most):
        step(k)


def reused(g, slots=2):
    return not isinstance(g, int) or g >= slots


def edge_groups(engine, sh, *parts, slots=2):
    staggered(engine, sh["eg"], sh["tail_e"] > 0, slots, [(lag, body, GT, sh["tail_e"]) for lag, body in parts])


def edge_rings(engine, sh, *parts):
    edge_groups(engine, sh, *parts, slots=4)


def both_groups(engine, sh, edge_parts, node_parts):
    edges, nodes = sh["eg"] + (sh["tail_e"] > 0), sh["full"] + (sh["tail_t"] > 0)
    edge_most = max([lag for lag, *_ in edge_parts], default=0)
    node_most = max([lag for lag, _ in node_parts], default=0)
    turn = 4 if edge_parts else LOADS // PER_STEP

    def step(k, r=0):
        for i in range(PER_STEP):
            for lag, body, before in edge_parts:
                g = k - lag
                if before == i and 0 <= g < edges:
                    body(g + r * turn, g % 4, g // 4 + r * (turn // 4), GT if g < sh["eg"] else sh["tail_e"])
            for lag, body in node_parts:
                g = k * PER_STEP + i - lag
                if 0 <= g < nodes:
                    body(g + r * (turn * PER_STEP), g % LOADS, g // LOADS + r * (turn * PER_STEP // LOADS),
                         (128, NT) if g < sh["full"] else (sh["tail_p"], sh["tail_t"]))

    steps, first, whole = 0, 0, []
    if edge_parts:
        steps, first = edges + edge_most, edge_most + 4
        whole.append(sh["eg"])
    if node_parts:
        steps = max(steps, -(-(nodes + node_most) // PER_STEP))
        first = max(first, -(-(node_most + LOADS) // PER_STEP))
        whole.append(sh["full"] // PER_STEP)
    turns = max((min(whole, default=0) - first) // turn, 0)
    for k in range(min(first, steps)):
        step(k)
    if turns:
        with engine.Fori(0, turns) as r:
            for k in range(first, first + turn):
                step(k, r)
    for k in range(first + turns * turn, steps):
        step(k)


def run_stages(nc, sh, edge_stage=None, node_stage=None):
    with nc.Block() as block:
        def drive(engine, name):
            programs = [stage_[name](engine) if stage_ and name in stage_ else ([], None)
                        for stage_ in (edge_stage, node_stage)]
            (edge_parts, edge_end), (node_parts, node_end) = programs
            both_groups(engine, sh, edge_parts, node_parts)
            if edge_end:
                edge_end()
            if node_end:
                node_end()

        @block.sync
        def _(sp):
            drive(sp, "sync")

        @block.tensor
        def _(pe):
            drive(pe, "tensor")

        @block.scalar
        def _(act):
            drive(act, "scalar")

        @block.vector
        def _(dve):
            drive(dve, "vector")

        @block.gpsimd
        def _(pool):
            drive(pool, "gpsimd")


def row_numbers(pool, ring, k, tiles, numbers, g, made):
    pool.tensor_copy(ring[:, k, 0:tiles], numbers[:, bass.ds(g * GT, tiles)]).then_inc(made, 1)


def node_rows(table, g, size):
    p, t = size
    return table[bass.ds(g * ROWS, p * t), :].rearrange("(p r) f -> p r f", r=t)


def edge_rows(table, g, tiles, first=0, columns=slice(None)):
    return table[bass.ds(g * GE + first, tiles * 128), columns].rearrange("(t p) f -> p t f", p=128)


def constants(nc, ctx, semaphore, sh):
    c = {}

    def sb(name, shape, dt):
        c[name] = ctx.enter_context(nc.sbuf_tensor(name, shape, dt))
        return c[name]

    width = max(sh["hi"], 129)
    sb("iota_i", [128, width], I32)
    sb("part_i", [128, 1], I32)
    sb("iota", [128, width], F32)
    sb("part", [128, 1], F32)
    sb("ident", [128, 128], F32)
    sb("identb", [128, 128], BF16)
    sb("before", [128, 128], F32)
    sb("above", [128, 128], F32)
    sb("onesb", [128, 128], BF16)
    sb("ones", [128, 128], F32)
    sb("zerosb", [128, width], BF16)
    sb("ln_eps", [128, 1], F32)
    sb("ln_eps4", [128, 1], F32)
    iota_made = semaphore("iota_made")
    iota_cast = semaphore("iota_cast")
    with nc.Block() as block:
        @block.gpsimd
        def _(pool):
            pool.iota(c["iota_i"][:, :], pattern=[[1, width]], base=0, channel_multiplier=0).then_inc(iota_made, 1)
            pool.iota(c["part_i"][:, :], pattern=[[0, 1]], base=0, channel_multiplier=1).then_inc(iota_made, 1)

        @block.vector
        def _(dve):
            dve.wait_ge(iota_made, 2)
            dve.tensor_copy(c["iota"][:, :], c["iota_i"][:, :]).then_inc(iota_cast, 1)
            dve.tensor_copy(c["part"][:, :], c["part_i"][:, :]).then_inc(iota_cast, 1)
            dve.memset(c["onesb"][:, :], 1.0)
            dve.memset(c["ones"][:, :], 1.0)
            dve.memset(c["zerosb"][:, :], 0.0)
            dve.memset(c["ln_eps"][:, :], LN_EPS)
            dve.memset(c["ln_eps4"][:, :], LN_EPS / 4)
            dve.wait_ge(iota_cast, 2)
            row, col = c["iota"][:, 0:128], c["part"][:, 0:1]
            dve.tensor_scalar(c["ident"][:, :], row, col, None, ALU.is_equal)
            dve.tensor_scalar(c["identb"][:, :], row, col, None, ALU.is_equal)
            dve.tensor_scalar(c["before"][:, :], row, col, None, ALU.is_lt)
            dve.tensor_scalar(c["above"][:, :], row, col, None, ALU.is_gt)
    return c


def sort_positions(nc, c, sh, tag, key_cols, key_flat, pos, count_table=None):
    with stage(nc) as (ctx, semaphore):
        def sb(name, shape, dt):
            return ctx.enter_context(nc.sbuf_tensor(f"{tag}_{name}", shape, dt))

        def ps(name):
            return ctx.enter_context(nc.psum_tensor(f"{tag}_{name}", [128, 512], F32))

        def sem(name):
            return semaphore(f"{tag}_{name}")

        hi = sh["hi"]
        key_i = sb("key_i", [128, sh["et"]], I32)
        low_i = sb("low_i", [128, sh["et"]], I32)
        high_i = sb("high_i", [128, sh["et"]], I32)
        key = sb("key", [128, sh["et"]], F32)
        low = sb("low", [128, sh["et"]], F32)
        high = sb("high", [128, sh["et"]], F32)
        hot_low = sb("hot_low", [128, sh["et"] * 128], BF16)
        hot_high = sb("hot_high", [128, sh["et"] * hi], BF16)
        count = sb("count", [128, sh["hc"] * 128], F32)
        running = sb("running", [128, hi], F32)
        before_row = sb("before_row", [128, 1], F32)
        first = sb("first", [128, hi], F32)
        key_row = sb("key_row", [128, 2, GE], I32)
        low_row = sb("low_row", [128, 2, GE], I32)
        hot_row = sb("hot_row", [128, 2, GE], F32)
        table = sb("table", [128, 2, hi], F32)
        equal = sb("equal", [128, GE], F32)
        picked = sb("picked", [128, 2, hi], F32)
        from_table = sb("from_table", [128, sh["et"]], F32)
        in_tile = sb("in_tile", [128, sh["et"]], F32)
        count_t = sb("count_t", [128, sh["hc"], 128], F32)
        hist = ps("hist")
        prefix = ps("prefix")
        found = [ps("found0"), ps("found1")]
        turned = ps("turned")

        keys_in = sem("keys_in")
        split = sem("split")
        parts_cast = sem("parts_cast")
        hot_made = sem("hot_made")
        counted = sem("counted")
        count_out = sem("count_out")
        scanned = sem("scanned")
        prefixed = sem("prefixed")
        prefix_out = sem("prefix_out")
        first_made = sem("first_made")
        row_in = [sem("row_in0"), sem("row_in1")]
        row_free = sem("row_free")
        row_low = sem("row_low")
        row_hot = sem("row_hot")
        table_updated = sem("table_updated")
        table_out = sem("table_out")
        looked_up = sem("looked_up")
        found_free = sem("found_free")
        turned_done = sem("turned_done")
        turned_out = sem("turned_out")
        count_stored = sem("count_stored")
        zeroed = sem("zeroed")
        summed = sem("summed")

        def lows(t):
            return hot_low[:, bass.ds(t * 128, 128)]

        def highs(t):
            return hot_high[:, bass.ds(t * hi, hi)]

        with nc.Block() as block:
            @block.sync
            def _(sp):
                sp.dma_start(key_i[:, :], key_cols).then_inc(keys_in, 16)

                def load(g, s, r, tiles):
                    sp.wait_ge(row_free, g + 1)
                    w = tiles * 128
                    sp.dma_start(key_row[:, s, 0:w],
                                 key_flat[bass.ds(g * GE, w)].rearrange("(a n) -> a n", a=1)
                                 .to_broadcast([128, w])).then_inc(row_in[s], 16)
                edge_groups(sp, sh, (0, load))
                if count_table is not None:
                    sp.wait_ge(turned_out, 1)
                    sp.dma_start(count_table.rearrange("(c h l) -> h c l", h=128, l=128), count_t[:, :, :]) \
                        .then_inc(count_stored, 16)
                    sp.wait_ge(count_stored, 16)

            @block.tensor
            def _(pe):
                pe.matmul(hist[:, 0:hi], c["zerosb"][:, 0:128], c["zerosb"][:, 0:hi], start=True, stop=True,
                          skip_group_check=True)

                def add(t, s, r):
                    pe.wait_ge(hot_made, t + 1)
                    pe.matmul(hist[:, 0:hi], lows(t), highs(t), start=False, stop=True,
                              skip_group_check=True).then_inc(counted, 1)
                rounds(pe, sh["et"], 2, add)
                pe.wait_ge(scanned, 1)
                pe.matmul(prefix[:, 0:1], c["above"][:, :], running[:, hi - 1:hi], start=True, stop=True) \
                    .then_inc(prefixed, 1)
                if count_table is not None:
                    pe.wait_ge(count_out, 1)
                    for k in range(sh["hc"]):
                        last = pe.transpose(turned[:, k * 128:(k + 1) * 128], count[:, k * 128:(k + 1) * 128],
                                            c["ident"][:, :])
                    last.then_inc(turned_done, 1)
                pe.wait_ge(first_made, 1)
                pe.matmul(hist[:, 0:hi], c["ident"][:, :], first[:, :], start=True, stop=True,
                          skip_group_check=True).then_inc(table_updated, 1)

                def look_up(g, s, r, tiles):
                    pe.wait_ge(row_hot, g + 1)
                    for j in range(tiles):
                        t = g * GT + j
                        pe.wait_ge(table_out, t + 1)
                        pe.matmul(hist[:, 0:hi], lows(t), highs(t), start=False, stop=True,
                                  skip_group_check=True).then_inc(table_updated, 1)
                        pe.wait_ge(found_free, t + 1)
                        pe.matmul(found[j % 2][:, 0:hi], hot_row[:, s, j * 128:(j + 1) * 128],
                                  table[:, j % 2, :], start=True, stop=True).then_inc(looked_up, 1)
                edge_groups(pe, sh, (0, look_up))

            @block.scalar
            def _(act):
                act.wait_ge(counted, sh["et"])
                act.wait_ge(zeroed, 1)
                act.activation(count[:, 0:hi], hist[:, 0:hi], ACT.Copy).then_inc(count_out, 1)
                act.wait_ge(prefixed, 1)
                act.activation(before_row[:, :], prefix[:, 0:1], ACT.Copy, bias=1.0).then_inc(prefix_out, 1)
                if count_table is not None:
                    act.wait_ge(turned_done, 1)
                    act.activation(count_t[:, :, :].rearrange("p c l -> p (c l)"), turned[:, 0:sh["hc"] * 128],
                                   ACT.Copy).then_inc(turned_out, 1)

                def take(t, s, r):
                    act.wait_ge(table_updated, t + 1)
                    if not isinstance(t, int) or t >= 2:
                        act.wait_ge(looked_up, t - 1)
                    act.activation(table[:, s, :], hist[:, 0:hi], ACT.Copy).then_inc(table_out, 1)
                take(0, 0, 0)
                take(1, 1, 0)
                rounds(act, sh["et"] - 2, 2, lambda t, s, r: take(t + 2, s, r))

            @block.vector
            def _(dve):
                dve.sem_inc(row_free, 2)
                dve.sem_inc(found_free, 2)
                dve.memset(count[:, :], 0.0).then_inc(zeroed, 1)
                dve.wait_ge(keys_in, 16)
                dve.tensor_copy(key[:, :], key_i[:, :]).then_inc(split, 1)
                dve.tensor_scalar(low_i[:, :], key_i[:, :], 127, None, ALU.bitwise_and).then_inc(split, 1)
                dve.tensor_scalar(high_i[:, :], key_i[:, :], 7, None, ALU.arith_shift_right).then_inc(split, 1)
                dve.wait_ge(split, 3)
                dve.tensor_copy(low[:, :], low_i[:, :]).then_inc(parts_cast, 1)
                dve.tensor_copy(high[:, :], high_i[:, :]).then_inc(parts_cast, 1)
                dve.wait_ge(parts_cast, 2)

                def make(t, s, r):
                    dve.tensor_scalar(lows(t), c["iota"][:, 0:128], low[:, bass.ds(t, 1)], None, ALU.is_equal)
                    dve.tensor_scalar(highs(t), c["iota"][:, 0:hi], high[:, bass.ds(t, 1)], None, ALU.is_equal) \
                        .then_inc(hot_made, 1)
                rounds(dve, sh["et"], 2, make)
                dve.wait_ge(count_out, 1)
                dve.tensor_tensor_scan(running[:, :], c["ones"][:, 0:1].to_broadcast([128, hi]), count[:, 0:hi],
                                       0.0, ALU.mult, ALU.add).then_inc(scanned, 1)
                dve.wait_ge(prefix_out, 1)
                dve.wait_ge(scanned, 1)
                dve.scalar_tensor_tensor(first[:, :], running[:, :], before_row[:, 0:1], count[:, 0:hi],
                                         ALU.add, ALU.subtract).then_inc(first_made, 1)

                def rank(g, s, r, tiles):
                    w = tiles * 128
                    dve.wait_ge(row_in[s], r * 16 + 16)
                    dve.tensor_scalar(low_row[:, s, 0:w], key_row[:, s, 0:w], 127, None, ALU.bitwise_and) \
                        .then_inc(row_low, 1)
                    dve.wait_ge(row_low, g + 1)
                    dve.tensor_scalar(hot_row[:, s, 0:w], low_row[:, s, 0:w], c["part"][:, 0:1], None,
                                      ALU.is_equal).then_inc(row_hot, 1)
                    dve.wait_ge(found_free, g * GT + 2)
                    for j in range(tiles):
                        t = g * GT + j
                        last = dve.scalar_tensor_tensor(
                            equal[:, j * 128:(j + 1) * 128], key_row[:, s, j * 128:(j + 1) * 128],
                            key[:, bass.ds(t, 1)], c["before"][:, :], ALU.is_equal, ALU.mult,
                            accum_out=in_tile[:, bass.ds(t, 1)])
                    last.then_inc(row_free, 1)
                    for j in range(tiles):
                        t = g * GT + j
                        dve.wait_ge(looked_up, t + 1)
                        dve.wait_ge(found_free, t + 1)
                        dve.scalar_tensor_tensor(
                            picked[:, j % 2, :], found[j % 2][:, 0:hi], 1.0, highs(t), ALU.mult, ALU.mult,
                            accum_out=from_table[:, bass.ds(t, 1)]).then_inc(found_free, 1)
                edge_groups(dve, sh, (0, rank))
                dve.wait_ge(found_free, sh["et"] + 2)
                dve.wait_ge(row_free, sh["eg"] + (1 if sh["tail_e"] else 0) + 2)
                dve.tensor_tensor(pos[:, :], from_table[:, :], in_tile[:, :], ALU.add).then_inc(summed, 1)
                dve.wait_ge(summed, 1)




ROW = 388
END = 384


def flat(tile):
    return tile.rearrange("p a b -> p (a b)")


def load_weights(nc, ctx, semaphore, c, sh, t):
    w = {}

    def sb(name, shape, dt=F32):
        w[name] = ctx.enter_context(nc.sbuf_tensor("w_" + name, shape, dt))
        return w[name]

    def sem(name):
        return semaphore("w_" + name)

    squares = ["w0x", "w0s", "w0e", "w1", "w2n", "w2n_t", "w2e_a", "w2e_b", "w2l_a", "w2l_b", "l3w1", "l3w2", "l3w3"]
    columns = ["b2n", "b2e", "l3b1", "bias1", "gamma", "beta", "neg_mu"]
    rows = ["b0", "b2l", "l3b2", "l3b3", "att_s", "att_d"]
    for name in squares:
        sb(name, [128, 128])
    for name in columns:
        sb(name, [128, 1])
    for name in rows:
        sb(name, [128, 128])
    for name in ("b0", "b2l", "l3b2", "l3b3"):
        sb(name + "_m", [128, NT, 128], BF16)
    sb("ws", [128, 128])
    sb("wd", [128, 128])
    sb("wsd", [128, 128])
    sb("w2n_neg", [128, 128])
    sb("part_hi", [128, 128], BF16)
    sb("part_mid", [128, 128], BF16)
    sb("part_lo", [128, 128], BF16)
    sb("rest1", [128, 128])
    sb("rest2", [128, 128])
    sb("weighted", [128, 128])
    sb("per_head", [128, 8])
    loaded, linked = sem("loaded"), sem("linked")
    loads = len(squares) + len(columns) + len(rows)
    with nc.Block() as block:
        @block.sync
        def _(sp):
            for name in squares:
                sp.dma_start(w[name][:, :], t[name]).then_inc(loaded, 16)
            for name in columns:
                sp.dma_start(w[name][:, :], t[name].rearrange("(p a) -> p a", a=1)).then_inc(loaded, 16)
            for name in rows:
                sp.dma_start(w[name][:, :], t[name].rearrange("(a n) -> a n", a=1).to_broadcast([128, 128])) \
                    .then_inc(loaded, 16)

        @block.vector
        def _(dve):
            dve.wait_ge(loaded, 16 * loads)
            done = [0]

            def link(instruction):
                instruction.then_inc(linked, 1)
                done[0] += 1
                dve.wait_ge(linked, done[0])

            for name in ("b0", "b2l", "l3b2", "l3b3"):
                bias_parts(dve, link, w, w[name], w[name + "_m"])
            for att, out in (("att_s", "ws"), ("att_d", "wd")):
                link(dve.tensor_tensor(w["weighted"][:, :], w["w1"][:, :], w[att][:, :], ALU.mult))
                link(dve.tensor_reduce(w["per_head"][:, :], w["weighted"][:, :].rearrange("p (h f) -> p h f", h=8),
                                       AX.X, ALU.add))
                link(dve.tensor_copy(w[out][:, :].rearrange("p (h f) -> p h f", h=8),
                                     w["per_head"][:, :].rearrange("p (h a) -> p h a", a=1).to_broadcast([128, 8, 16])))
            link(dve.tensor_tensor(w["wsd"][:, :], w["ws"][:, :], w["wd"][:, :], ALU.add))
            link(dve.tensor_scalar(w["w2n_neg"][:, :], w["w2n_t"][:, :], -1.0, None, ALU.mult))
    return w


def bias_parts(dve, link, w, row, parts):
    link(dve.tensor_copy(w["part_hi"][:, :], row[:, :]))
    link(dve.tensor_tensor(w["rest1"][:, :], row[:, :], w["part_hi"][:, :], ALU.subtract))
    link(dve.tensor_copy(w["part_mid"][:, :], w["rest1"][:, :]))
    link(dve.tensor_tensor(w["rest2"][:, :], w["rest1"][:, :], w["part_mid"][:, :], ALU.subtract))
    link(dve.tensor_copy(w["part_lo"][:, :], w["rest2"][:, :]))
    link(dve.memset(flat(parts[:, :, :]), 0.0))
    for k, part in enumerate(("part_hi", "part_mid", "part_lo")):
        at = slice(32 * k, 32 * k + 32)
        for j in range(NT):
            last = dve.tensor_scalar(parts[at, j, :], w[part][at, :], 1.0 / 32, None, ALU.mult)
    link(last)


def norm_buffers(nc, ctx, semaphore, tag, eps, slots=2):
    def sb(name, shape):
        return ctx.enter_context(nc.sbuf_tensor(f"{tag}_{name}", shape, F32))

    nm = {"eps": eps, "stats": sb("stats", [128, slots, NT, 6]), "moments": sb("moments", [128, slots, NT, 2]),
          "dev": sb("dev", [128, slots, NT]), "inv": sb("inv", [128, slots, NT])}
    for name in ("stats_made", "moments_made", "dev_made", "inv_made", "carried"):
        nm[name] = semaphore(f"{tag}_{name}")
    return nm


def norm_measure(nm, dve, rows, g, s, p, t):
    norm_stats(nm, dve, rows, s, p, t)
    norm_moments(nm, dve, g, s, p, t)


def norm_stats(nm, dve, rows, s, p, t):
    for j in range(t):
        last = dve.bn_stats(nm["stats"][0:p, s, j, :], rows[:, j, :])
    last.then_inc(nm["stats_made"], 1)


def norm_moments(nm, dve, g, s, p, t):
    dve.wait_ge(nm["stats_made"], g + 1)
    dve.sem_inc(nm["carried"], 1)
    for j in range(t):
        last = dve.bn_aggr(nm["moments"][0:p, s, j, :], nm["stats"][0:p, s, j, :])
    last.then_inc(nm["moments_made"], 1)


def norm_deviation(nm, act, g, s, p, t):
    act.wait_ge(nm["moments_made"], g + 1)
    act.activation(nm["dev"][0:p, s, 0:t], nm["moments"][0:p, s, 0:t, 1], ACT.Sqrt,
                   bias=nm["eps"][0:p, :]).then_inc(nm["dev_made"], 1)


def norm_invert(nm, dve, g, s, p, t):
    dve.wait_ge(nm["dev_made"], g + 1)
    dve.reciprocal(nm["inv"][0:p, s, 0:t], nm["dev"][0:p, s, 0:t]).then_inc(nm["inv_made"], 1)


def norm_scale(nm, dve, out, rows, g, s, p, t):
    dve.wait_ge(nm["inv_made"], g + 1)
    for j in range(t):
        last = dve.tensor_scalar(out[:, j, :], rows[:, j, :], nm["moments"][0:p, s, j, 0:1],
                                 nm["inv"][0:p, s, j:j + 1], ALU.subtract, ALU.mult)
    return last


def edge_rows_stage(nc, ctx, semaphore, c, sh, t, w, pos):
    def sb(name, shape, dt=F32):
        return ctx.enter_context(nc.sbuf_tensor("p_" + name, shape, dt))

    def ps(name):
        return ctx.enter_context(nc.psum_tensor("p_" + name, [128, 512], F32))

    def sem(name):
        return semaphore("p_" + name)

    ends_i = sb("ends_i", [128, 2, sh["et"]], I32)
    ends = sb("ends", [128, sh["et"], 2])
    own_i = sb("own_i", [128, sh["et"]], I32)
    other_i = sb("other_i", [128, sh["et"]], I32)
    dist = sb("dist", [128, sh["et"]])
    ramp = sb("ramp", [128, sh["et"]])
    ramp01 = sb("ramp01", [128, sh["et"]])
    cosine = sb("cosine", [128, sh["et"]])
    halved = sb("halved", [128, sh["et"]])
    cut = sb("cut", [128, sh["et"]])
    half_pi = sb("half_pi", [128, 1])
    half = sb("half", [128, 1])
    pad_row = sb("pad_row", [1, ROW])
    own_at, other_at, put_at = (sb(k, [128, 4, GT], I32) for k in ("own_at", "other_at", "put_at"))
    xs = sb("xs", [128, 4, GT, 128])
    xs_t, ea_t = sb("xs_t", [128, 2, GE]), sb("ea_t", [128, 2, GE])
    ea = sb("ea", [128, 4, GT, 128])
    dist_row = sb("dist_row", [128, 4, GE])
    radial = sb("radial", [128, 2, GE])
    soft1, soft2 = sb("soft1", [128, 2, GE]), sb("soft2", [128, 2, GE])
    hidden = sb("hidden", [128, 2, GE])
    filt = sb("filt", [128, 2, GT, 128])
    row = sb("row", [128, 4, GT, ROW])
    turned_x, turned_e, message = ps("turned_x"), ps("turned_e"), ps("message")
    act1, act2 = ps("act1"), ps("act2")

    ends_in, linked, setup, cos_made, pads_stored = (
        sem(k) for k in ("ends_in", "linked", "setup", "cos_made", "pads_stored"))
    numbers_ready, at_made, put_made, issuing = (
        sem(k) for k in ("numbers_ready", "at_made", "put_made", "issuing"))
    gathered, ea_in, dist_in, stored = (
        [sem(f"{name}{k}") for k in range(4)] for name in ("gathered", "ea_in", "dist_in", "stored"))
    x_turned, x_t_out, message_made, message_out, squared, radial_made = (
        sem(k) for k in ("x_turned", "x_t_out", "message_made", "message_out", "squared", "radial_made"))
    act1_made, abs1, exp1, log1, pos1, hidden_made, act2_made, abs2, exp2, log2, filt_made, row_made = (
        sem(k) for k in ("act1_made", "abs1", "exp1", "log1", "pos1", "hidden_made", "act2_made", "abs2", "exp2",
                         "log2", "filt_made", "row_made"))

    def sync(sp):
        sp.dma_start(ends_i[:, 0, :], t["dst_cols"]).then_inc(ends_in, 16)
        sp.dma_start(ends_i[:, 1, :], t["src_cols"]).then_inc(ends_in, 16)
        sp.dma_start(dist[:, :], t["weight_cols"]).then_inc(ends_in, 16)
        sp.wait_ge(setup, 1)
        sp.dma_start(t["rows_d"][0:1, :], pad_row[:, :]).then_inc(pads_stored, 16)
        sp.dma_start(t["rows_d"][sh["ep"] + 1:sh["ep"] + 2, :], pad_row[:, :]).then_inc(pads_stored, 16)
        sp.dma_start(t["rows_s"][0:1, :], pad_row[:, 0:2]).then_inc(pads_stored, 16)
        sp.dma_start(t["rows_s"][sh["ep"] + 1:sh["ep"] + 2, :], pad_row[:, 0:2]).then_inc(pads_stored, 16)

        def load_distances(g, k, r, tiles):
            n = tiles * 128
            if reused(g, 4):
                sp.wait_ge(squared, g - 3)
            sp.dma_start(dist_row[:, k, 0:n],
                         t["weight_flat"][bass.ds(g * GE, n)].rearrange("(a n) -> a n", a=1)
                         .to_broadcast([128, n])).then_inc(dist_in[k], 16)

        def load_attributes(g, k, r, tiles):
            if reused(g, 4):
                sp.wait_ge(x_turned, g - 3)
                sp.wait_ge(row_made, g - 3)
            sp.dma_start(ea[:, k, 0:tiles, :], edge_rows(t["edge_attr"], g, tiles)).then_inc(ea_in[k], 16)
        return [(0, load_distances, 0), (1, load_attributes, 0)], lambda: sp.wait_ge(pads_stored, 64)

    def gpsimd(pool):
        last_node = pool.to_reg(sh["n"] - 1)
        last_row = pool.to_reg(sh["ep"] + 1)
        pool.wait_ge(numbers_ready, 1)

        def gather(g, k, r, tiles):
            if reused(g, 4):
                pool.wait_ge(gathered[k], r * 32 * GT)
            pool.tensor_copy(own_at[:, k, 0:tiles], own_i[:, bass.ds(g * GT, tiles)]).then_inc(at_made, 1)
            pool.tensor_copy(other_at[:, k, 0:tiles], other_i[:, bass.ds(g * GT, tiles)]).then_inc(at_made, 1)
            pool.wait_ge(at_made, 2 * g + 2)
            if reused(g, 4):
                pool.wait_ge(stored[k], r * 16 * GT)
                pool.wait_ge(x_turned, g - 3)
            pool.sem_inc(issuing, 1)
            for j in range(tiles):
                pool.indirect_dma_start(
                    out=xs[:, k, j, :], out_offset=None, in_=t["x"],
                    in_offset=bass.IndirectOffsetOnAxis(ap=other_at[:, k, j:j + 1], axis=0),
                    bounds_check=last_node, oob_is_err=False).then_inc(gathered[k], 16)
                pool.indirect_dma_start(
                    out=row[:, k, j, 128:256], out_offset=None, in_=t["x"],
                    in_offset=bass.IndirectOffsetOnAxis(ap=own_at[:, k, j:j + 1], axis=0),
                    bounds_check=last_node, oob_is_err=False).then_inc(gathered[k], 16)

        def scatter(g, k, r, tiles):
            if reused(g, 4):
                pool.wait_ge(stored[k], r * 16 * GT)
            pool.tensor_copy(put_at[:, k, 0:tiles], pos[:, bass.ds(g * GT, tiles)]).then_inc(put_made, 1)
            pool.wait_ge(put_made, g + 1)
            pool.wait_ge(row_made, g + 1)
            pool.wait_ge(message_out, g + 1)
            pool.wait_ge(gathered[k], r * 32 * GT + 32 * tiles)
            pool.sem_inc(issuing, 1)
            for j in range(tiles):
                pool.indirect_dma_start(
                    out=t["rows_d"], out_offset=bass.IndirectOffsetOnAxis(ap=put_at[:, k, j:j + 1], axis=0),
                    in_=row[:, k, j, :], in_offset=None,
                    bounds_check=last_row, oob_is_err=False).then_inc(stored[k], 16)

        def finish():
            for k in range(4):
                pool.wait_ge(stored[k], 16 * slot_tiles(sh, k, 4))
        return [(2, gather, 0), (5, scatter, 0)], finish

    def tensor(pe):
        def filter1(g, k, r, tiles):
            s, n = k % 2, tiles * 128
            pe.wait_ge(radial_made, g + 1)
            if reused(g, 1):
                pe.wait_ge(pos1, g)
            pe.matmul(act1[:, 0:n], w["l3w1"][:, :], radial[:, s, 0:n], start=True, stop=True) \
                .then_inc(act1_made, 1)

        def turn(g, k, r, tiles):
            pe.wait_ge(gathered[k], r * 32 * GT + 32 * tiles)
            pe.wait_ge(ea_in[k], r * 16 + 16)
            if reused(g, 1):
                pe.wait_ge(x_t_out, g)
            for j in range(tiles):
                pe.transpose(turned_x[:, j * 128:(j + 1) * 128], xs[:, k, j, :], c["ident"][:, :])
                last = pe.transpose(turned_e[:, j * 128:(j + 1) * 128], ea[:, k, j, :], c["ident"][:, :])
            last.then_inc(x_turned, 1)

        def project(g, k, r, tiles):
            s = k % 2
            pe.wait_ge(x_t_out, g + 1)
            if reused(g, 1):
                pe.wait_ge(message_out, g)
            for j in range(tiles):
                at = slice(j * 128, (j + 1) * 128)
                pe.matmul(message[:, at], xs_t[:, s, at], w["w0s"][:, :], start=True, stop=False)
                last = pe.matmul(message[:, at], ea_t[:, s, at], w["w0e"][:, :], start=False, stop=True)
            last.then_inc(message_made, 1)

        def filter2(g, k, r, tiles):
            s, n = k % 2, tiles * 128
            pe.wait_ge(hidden_made, g + 1)
            if reused(g, 1):
                pe.wait_ge(filt_made, g)
            pe.matmul(act2[:, 0:n], c["onesb"][:, :], flat(w["l3b2_m"][:, 0:tiles, :]), start=True,
                      stop=False, skip_group_check=True)
            for j in range(tiles):
                at = slice(j * 128, (j + 1) * 128)
                last = pe.matmul(act2[:, at], hidden[:, s, at], w["l3w2"][:, :], start=False, stop=True,
                                 skip_group_check=True)
            last.then_inc(act2_made, 1)
        return [(2, turn, 0), (3, project, 1), (2, filter2, 3), (0, filter1, 3)], None

    def scalar(act):
        act.wait_ge(setup, 1)
        act.activation(cosine[:, :], ramp01[:, :], ACT.Sin, bias=half_pi[:, :], scale=-3.14159265358979) \
            .then_inc(cos_made, 1)

        def radial_part(g, k, r, tiles):
            s, n = k % 2, tiles * 128
            act.wait_ge(dist_in[k], r * 16 + 16)
            if reused(g):
                act.wait_ge(act1_made, g - 1)
            act.activation(radial[:, s, 0:n], dist_row[:, k, 0:n], ACT.Square, bias=w["neg_mu"][:, :]) \
                .then_inc(squared, 1)
            act.wait_ge(squared, g + 1)
            act.activation(radial[:, s, 0:n], radial[:, s, 0:n], ACT.Exp, scale=-float(D)).then_inc(radial_made, 1)

        def decay1(g, k, r, tiles):
            s, n = k % 2, tiles * 128
            act.wait_ge(act1_made, g + 1)
            if reused(g):
                act.wait_ge(hidden_made, g - 1)
            act.activation(soft1[:, s, 0:n], act1[:, 0:n], ACT.Abs, bias=w["l3b1"][:, :]).then_inc(abs1, 1)
            act.wait_ge(abs1, g + 1)
            act.activation(soft1[:, s, 0:n], soft1[:, s, 0:n], ACT.Exp, scale=-1.0).then_inc(exp1, 1)

        def decay2(g, k, r, tiles):
            s, n = k % 2, tiles * 128
            act.wait_ge(act2_made, g + 1)
            if reused(g):
                act.wait_ge(filt_made, g - 1)
            act.activation(soft2[:, s, 0:n], act2[:, 0:n], ACT.Abs).then_inc(abs2, 1)
            act.wait_ge(abs2, g + 1)
            act.activation(soft2[:, s, 0:n], soft2[:, s, 0:n], ACT.Exp, scale=-1.0).then_inc(exp2, 1)

        def logs1(g, k, r, tiles):
            s, n = k % 2, tiles * 128
            act.wait_ge(exp1, g + 1)
            act.activation(soft1[:, s, 0:n], soft1[:, s, 0:n], ACT.Ln, scale=0.5, bias=half[:, :]) \
                .then_inc(log1, 1)

        def logs2(g, k, r, tiles):
            s, n = k % 2, tiles * 128
            act.wait_ge(exp2, g + 1)
            act.activation(soft2[:, s, 0:n], soft2[:, s, 0:n], ACT.Ln, scale=0.5, bias=half[:, :]) \
                .then_inc(log2, 1)

        def copies(g, k, r, tiles):
            s, n = k % 2, tiles * 128
            act.wait_ge(x_turned, g + 1)
            if reused(g):
                act.wait_ge(message_made, g - 1)
            act.activation(xs_t[:, s, 0:n], turned_x[:, 0:n], ACT.Copy)
            act.activation(ea_t[:, s, 0:n], turned_e[:, 0:n], ACT.Copy).then_inc(x_t_out, 1)

        def messages(g, k, r, tiles):
            act.wait_ge(message_made, g + 1)
            if reused(g, 4):
                act.wait_ge(stored[k], r * 16 * GT)
            act.activation(row[:, k, 0:tiles, 0:128], message[:, 0:tiles * 128].rearrange("p (t f) -> p t f", f=128),
                           ACT.Copy).then_inc(message_out, 1)
        return [(4, messages, 0), (1, decay1, 0), (3, decay2, 0), (0, radial_part, 0), (1, logs1, 1), (3, logs2, 1),
                (2, copies, 2)], None

    def vector(dve):
        done = [0]

        def link(instruction):
            instruction.then_inc(linked, 1)
            done[0] += 1
            dve.wait_ge(linked, done[0])
        dve.memset(pad_row[:, :], -1.0)
        dve.memset(half[:, :], 0.5)
        dve.memset(half_pi[:, :], 3.14159265358979 / 2)
        for k in range(4):
            dve.memset(row[:, k, :, 386:388], 0.0)
        dve.wait_ge(ends_in, 48)
        dve.tensor_scalar(own_i[:, :], ends_i[:, 0, :], sh["n"] - 1, None, ALU.min)
        dve.tensor_scalar(other_i[:, :], ends_i[:, 1, :], sh["n"] - 1, None, ALU.min).then_inc(numbers_ready, 1)
        for k in range(2):
            link(dve.tensor_copy(ends[:, :, k], ends_i[:, k, :]))
        link(dve.tensor_scalar(ramp[:, :], dist[:, :], -0.8, 1.0 / (1.0 - 0.8), ALU.add, ALU.mult))
        dve.tensor_scalar(ramp01[:, :], ramp[:, :], 0.0, 1.0, ALU.max, ALU.min).then_inc(setup, 1)
        dve.wait_ge(cos_made, 1)
        link(dve.tensor_scalar(halved[:, :], cosine[:, :], 0.5, 0.5, ALU.mult, ALU.add))
        link(dve.scalar_tensor_tensor(cut[:, :], dist[:, :], 1.0, halved[:, :], ALU.is_le, ALU.mult))

        def rectify(g, k, r, tiles):
            s, n = k % 2, tiles * 128
            dve.wait_ge(abs1, g + 1)
            if reused(g):
                dve.wait_ge(act2_made, g - 1)
            dve.tensor_scalar(hidden[:, s, 0:n], act1[:, 0:n], w["l3b1"][:, :], 0.0, ALU.add, ALU.max) \
                .then_inc(pos1, 1)

        def hide(g, k, r, tiles):
            s, n = k % 2, tiles * 128
            dve.wait_ge(pos1, g + 1)
            dve.wait_ge(log1, g + 1)
            dve.tensor_tensor(hidden[:, s, 0:n], hidden[:, s, 0:n], soft1[:, s, 0:n], ALU.add) \
                .then_inc(hidden_made, 1)

        def filters(g, k, r, tiles):
            s, n = k % 2, tiles * 128
            dve.wait_ge(log2, g + 1)
            if reused(g):
                dve.wait_ge(row_made, g - 1)
            dve.scalar_tensor_tensor(flat(filt[:, s, 0:tiles, :]), act2[:, 0:n], 0.0, soft2[:, s, 0:n],
                                     ALU.max, ALU.add).then_inc(filt_made, 1)

        def fill(g, k, r, tiles):
            s = k % 2
            dve.wait_ge(filt_made, g + 1)
            dve.wait_ge(ea_in[k], r * 16 + 16)
            if reused(g, 4):
                dve.wait_ge(stored[k], r * 16 * GT)
            for j in range(tiles):
                dve.scalar_tensor_tensor(row[:, k, j, 256:384], ea[:, k, j, :], cut[:, bass.ds(g * GT + j, 1)],
                                         filt[:, s, j, :], ALU.mult, ALU.mult)
            dve.tensor_copy(row[:, k, 0:tiles, END:END + 2], ends[:, bass.ds(g * GT, tiles), :]) \
                .then_inc(row_made, 1)
        return [(1, rectify, 0), (1, hide, 1), (3, filters, 2), (4, fill, 3)], None
    return {"sync": sync, "gpsimd": gpsimd, "tensor": tensor, "scalar": scalar, "vector": vector}


def dense_stage(nc, ctx, semaphore, c, sh, tag, src, dst, weight, bias_m, eps, gram=None):
    def sb(name, shape, dt=F32):
        return ctx.enter_context(nc.sbuf_tensor(f"{tag}_{name}", shape, dt))

    def ps(name):
        return ctx.enter_context(nc.psum_tensor(f"{tag}_{name}", [128, 512], F32))

    def sem(name):
        return semaphore(f"{tag}_{name}")

    groups = sh["full"] + (1 if sh["tail_t"] else 0)
    x = sb("x", [128, LOADS, NT, 128])
    x_t = sb("x_t", [128, 2, ROWS])
    u = sb("u", [128, 4, NT, 128])
    y = sb("y", [128, 4, NT, 128])
    turned, summed = [ps("turned")], [ps("summed")]
    norm = norm_buffers(nc, ctx, semaphore, tag + "_norm", eps, 4)
    x_in = [sem(f"x_in{k}") for k in range(LOADS)]
    y_stored = [sem(f"y_stored{s}") for s in range(LOADS)]
    x_turned, x_t_out, sum_made, u_made, y_made = (
        sem(k) for k in ("x_turned", "x_t_out", "sum_made", "u_made", "y_made"))
    if gram:
        ym = sb("ym", [128, 4, NT, 129])
        kept_inv = sb("kept_inv", [128, 4, NT])
        counts = sb("counts", [128, groups, NT])
        alone = sb("alone", [128, groups, NT])
        gram_ps = ps("gram")
        counts_in, alone_made, kept_made, ym_made, gram_added = (
            sem(k) for k in ("counts_in", "alone_made", "kept_made", "ym_made", "gram_added"))
    else:
        turned.append(ps("turned1"))
        summed.append(ps("summed1"))
    banks = len(turned)

    def view(bank, p, t):
        return bank[:, 0:t * 128].rearrange("p (t f) -> p t f", f=128)[:, :, 0:p]

    def sync(sp):
        if gram:
            n_full = sh["full"] * ROWS
            sp.dma_start(counts[:, 0:sh["full"], :],
                         gram[0][0:n_full].rearrange("(g p r) -> p g r", p=128, r=NT)).then_inc(counts_in, 16)
            if sh["tail_t"]:
                sp.dma_start(counts[0:sh["tail_p"], sh["full"], 0:sh["tail_t"]],
                             gram[0][n_full:sh["n"]].rearrange("(p r) -> p r", r=sh["tail_t"])).then_inc(counts_in, 16)

        def load(g, k, r, size):
            p, t = size
            if reused(g, LOADS):
                sp.wait_ge(u_made, g - LOADS + 1)
            sp.dma_start(x[0:p, k, 0:t, :], node_rows(src, g, size)).then_inc(x_in[k], 16)

        def store(g, k, r, size):
            p, t = size
            sp.wait_ge(y_made, g + 1)
            sp.dma_start(node_rows(dst, g, size), y[0:p, k % 4, 0:t, :]).then_inc(y_stored[k], 16)

        def finish():
            for k in range(LOADS):
                sp.wait_ge(y_stored[k], 16 * len(range(k, groups, LOADS)))
        return [(0, load), (6, store)], finish

    def tensor(pe):
        if gram:
            pe.matmul(gram_ps[:, 0:129], c["zerosb"][:, 0:128], c["zerosb"][:, 0:129], start=True, stop=True,
                      skip_group_check=True)

        def turn(g, k, r, size):
            p, t = size
            pe.wait_ge(x_in[k], r * 16 + 16)
            if reused(g, banks):
                pe.wait_ge(x_t_out, g + 1 - banks)
            bank = turned[k % banks]
            for j in range(t):
                last = pe.transpose(bank[:, j * 128:j * 128 + p], x[0:p, k, j, :], c["ident"][0:p, 0:p])
            last.then_inc(x_turned, 1)

        def project(g, k, r, size):
            p, t = size
            bank = summed[k % banks]
            pe.wait_ge(x_t_out, g + 1)
            if reused(g, banks):
                pe.wait_ge(u_made, g + 1 - banks)
            pe.matmul(bank[0:p, 0:t * 128], c["onesb"][:, 0:p], flat(bias_m[:, 0:t, :]), start=True,
                      stop=False, skip_group_check=True)
            for j in range(t):
                last = pe.matmul(bank[0:p, j * 128:(j + 1) * 128], x_t[:, k % 2, j * 128:j * 128 + p],
                                 weight[:, :], start=False, stop=True, skip_group_check=True)
            last.then_inc(sum_made, 1)

        def add_gram(g, k, r, size):
            p, t = size
            pe.wait_ge(ym_made, g + 1)
            for j in range(t):
                last = pe.matmul(gram_ps[:, 0:129], y[0:p, k % 4, j, :], ym[0:p, k % 4, j, :], start=False, stop=True,
                                 skip_group_check=True)
            last.then_inc(gram_added, 1)
        return [(0, turn), *([(5, add_gram)] if gram else []), (1, project)], None

    def scalar(act):
        def copy(g, k, r, size):
            p, t = size
            act.wait_ge(x_turned, g + 1)
            if reused(g):
                act.wait_ge(sum_made, g - 1)
            act.activation(view(x_t[:, k % 2, :], p, t), view(turned[k % banks], p, t), ACT.Copy).then_inc(x_t_out, 1)

        def deviation(g, k, r, size):
            norm_deviation(norm, act, g, k % 4, *size)

        def finish():
            if gram:
                act.wait_ge(gram_added, groups)
                act.activation(gram[1][:, :], gram_ps[:, 0:129], ACT.Copy).then_inc(x_t_out, 1)
        return [(0, copy), (3, deviation)], finish

    def vector(dve):
        if gram:
            dve.wait_ge(counts_in, 32 if sh["tail_t"] else 16)
            dve.tensor_scalar(flat(alone[:, 0:sh["full"], :]), flat(counts[:, 0:sh["full"], :]), 0.0, None,
                              ALU.is_equal).then_inc(alone_made, 1)
            if sh["tail_t"]:
                dve.tensor_scalar(alone[0:sh["tail_p"], sh["full"], 0:sh["tail_t"]],
                                  counts[0:sh["tail_p"], sh["full"], 0:sh["tail_t"]], 0.0, None,
                                  ALU.is_equal).then_inc(alone_made, 1)
            dve.wait_ge(alone_made, 2 if sh["tail_t"] else 1)

        def add(g, k, r, size):
            p, t = size
            dve.wait_ge(sum_made, g + 1)
            dve.scalar_tensor_tensor(flat(u[0:p, k % 4, 0:t, :]), summed[k % banks][0:p, 0:t * 128], 0.0,
                                     flat(x[0:p, k, 0:t, :]), ALU.max, ALU.add).then_inc(u_made, 1)

        def stats(g, k, r, size):
            p, t = size
            dve.wait_ge(u_made, g + 1)
            norm_stats(norm, dve, u[0:p, k % 4, 0:t, :], k % 4, p, t)

        def moments(g, k, r, size):
            norm_moments(norm, dve, g, k % 4, *size)

        def invert(g, k, r, size):
            norm_invert(norm, dve, g, k % 4, *size)

        def scale(g, k, r, size):
            p, t = size
            s = k % 4
            if reused(g, 4):
                dve.wait_ge(y_stored[(k + 4) % LOADS], (r * 16 if k < 4 else r * 16 + 16))
                if gram:
                    dve.wait_ge(gram_added, g - 3)
            norm_scale(norm, dve, y[0:p, s, 0:t, :], u[0:p, s, 0:t, :], g, s, p, t).then_inc(y_made, 1)
            if gram:
                keep = alone[0:p, bass.ds(g, 1), 0:t].rearrange("p a t -> p (a t)")
                dve.tensor_tensor(kept_inv[0:p, s, 0:t], norm["inv"][0:p, s, 0:t], keep, ALU.mult) \
                    .then_inc(kept_made, 1)

        def mask(g, k, r, size):
            p, t = size
            s = k % 4
            dve.tensor_copy(ym[0:p, s, 0:t, 128], alone[0:p, bass.ds(g, 1), 0:t].rearrange("p a t -> p (a t)"))
            dve.wait_ge(kept_made, g + 1)
            for j in range(t):
                last = dve.tensor_scalar(ym[0:p, s, j, 0:128], u[0:p, s, j, :], norm["moments"][0:p, s, j, 0:1],
                                         kept_inv[0:p, s, j:j + 1], ALU.subtract, ALU.mult)
            last.then_inc(ym_made, 1)
        return [(2, add), (4, invert), (2, stats), (4, scale), (2, moments), *([(4, mask)] if gram else [])], None
    return {"sync": sync, "tensor": tensor, "scalar": scalar, "vector": vector}


def last_dense_stage(nc, ctx, semaphore, c, sh, w, src, dst, out):
    def sb(name, shape, dt=F32):
        return ctx.enter_context(nc.sbuf_tensor("d2_" + name, shape, dt))

    def ps(name):
        return ctx.enter_context(nc.psum_tensor("d2_" + name, [128, 512], F32))

    def sem(name):
        return semaphore("d2_" + name)

    groups = sh["full"] + (1 if sh["tail_t"] else 0)
    x = sb("x", [128, LOADS, NT, 128])
    x_t = sb("x_t", [128, 2, ROWS])
    y, u2, y2 = (sb(k, [128, 4, NT, 128]) for k in ("y", "u2", "y2"))
    squares = sb("squares", [128, 2, NT, 128])
    power, dev, inv, power2, dev2, inv2 = (sb(k, [128, 4, NT]) for k in ("power", "dev", "inv", "power2", "dev2", "inv2"))
    turned, summed, row_ps = [ps("turned0"), ps("turned1")], [ps(f"summed{k}") for k in range(4)], ps("row")
    x_in, y_stored, y2_stored = ([sem(f"{name}{k}") for k in range(LOADS)] for name in ("x_in", "y_stored", "y2_stored"))
    (row_made, x_turned, x_t_out, sum_made, power_made, dev_made, inv_made, y_made, u2_made, power2_made, dev2_made,
     inv2_made, y2_made) = (sem(k) for k in (
         "row_made", "x_turned", "x_t_out", "sum_made", "power_made", "dev_made", "inv_made", "y_made", "u2_made",
         "power2_made", "dev2_made", "inv2_made", "y2_made"))

    def view(bank, p, t):
        return bank[:, 0:t * 128].rearrange("p (t f) -> p t f", f=128)[:, :, 0:p]

    def sync(sp):
        def load(g, k, r, size):
            p, t = size
            if reused(g, LOADS):
                sp.wait_ge(x_turned, g - LOADS + 1)
            sp.dma_start(x[0:p, k, 0:t, :], node_rows(src, g, size)).then_inc(x_in[k], 16)

        def store(g, k, r, size):
            p, t = size
            sp.wait_ge(y_made, g + 1)
            sp.dma_start(node_rows(dst, g, size), y[0:p, k % 4, 0:t, :]).then_inc(y_stored[k], 16)

        def store2(g, k, r, size):
            p, t = size
            sp.wait_ge(y2_made, g + 1)
            sp.dma_start(node_rows(out, g, size), y2[0:p, k % 4, 0:t, :]).then_inc(y2_stored[k], 16)

        def finish():
            for k in range(LOADS):
                sp.wait_ge(y_stored[k], 16 * len(range(k, groups, LOADS)))
                sp.wait_ge(y2_stored[k], 16 * len(range(k, groups, LOADS)))
        return [(0, load), (4, store), (6, store2)], finish

    def tensor(pe):
        pe.matmul(row_ps[:, :], c["onesb"][:, :], flat(w["lone_mc"][:, :, :]), start=True, stop=True) \
            .then_inc(row_made, 1)

        def turn(g, k, r, size):
            p, t = size
            pe.wait_ge(x_in[k], r * 16 + 16)
            if reused(g):
                pe.wait_ge(x_t_out, g - 1)
            for j in range(t):
                last = pe.transpose(turned[k % 2][:, j * 128:j * 128 + p], x[0:p, k, j, :], c["ident"][0:p, 0:p])
            last.then_inc(x_turned, 1)

        def project(g, k, r, size):
            p, t = size
            bank = summed[k % 4]
            pe.wait_ge(x_t_out, g + 1)
            if reused(g, 4):
                pe.wait_ge(y_made, g - 3)
            pe.matmul(bank[0:p, 0:t * 128], c["onesb"][:, 0:p], flat(w["bz_mc"][:, 0:t, :]), start=True,
                      stop=False, skip_group_check=True)
            for j in range(t):
                last = pe.matmul(bank[0:p, j * 128:(j + 1) * 128], x_t[:, k % 2, j * 128:j * 128 + p],
                                 w["wz"][:, :], start=False, stop=True, skip_group_check=True)
            last.then_inc(sum_made, 1)
        return [(0, turn), (1, project)], None

    def scalar(act):
        def copy(g, k, r, size):
            p, t = size
            act.wait_ge(x_turned, g + 1)
            if reused(g):
                act.wait_ge(sum_made, g - 1)
            act.activation(view(x_t[:, k % 2, :], p, t), view(turned[k % 2], p, t), ACT.Copy).then_inc(x_t_out, 1)

        def measure(g, k, r, size):
            p, t = size
            s = k % 4
            act.wait_ge(sum_made, g + 1)
            if reused(g, 1):
                act.wait_ge(power_made, g)
            for j in range(t):
                last = act.activation(squares[0:p, 0, j, :], summed[s][0:p, j * 128:(j + 1) * 128], ACT.Square,
                                      accum_out=power[0:p, s, j:j + 1])
            last.then_inc(power_made, 1)

        def measure2(g, k, r, size):
            p, t = size
            s = k % 4
            act.wait_ge(u2_made, g + 1)
            if reused(g, 1):
                act.wait_ge(power2_made, g)
            for j in range(t):
                last = act.activation(squares[0:p, 1, j, :], u2[0:p, s, j, :], ACT.Square,
                                      accum_out=power2[0:p, s, j:j + 1])
            last.then_inc(power2_made, 1)

        def deviation(g, k, r, size):
            p, t = size
            act.wait_ge(power_made, g + 1)
            act.activation(dev[0:p, k % 4, 0:t], power[0:p, k % 4, 0:t], ACT.Sqrt, bias=c["ln_eps"][0:p, :],
                           scale=1.0 / D).then_inc(dev_made, 1)

        def deviation2(g, k, r, size):
            p, t = size
            act.wait_ge(power2_made, g + 1)
            act.activation(dev2[0:p, k % 4, 0:t], power2[0:p, k % 4, 0:t], ACT.Sqrt, bias=c["ln_eps"][0:p, :],
                           scale=1.0 / D).then_inc(dev2_made, 1)
        return [(2, measure), (0, copy), (2, deviation), (4, measure2), (4, deviation2)], None

    def vector(dve):
        dve.wait_ge(row_made, 1)

        def invert(g, k, r, size):
            p, t = size
            dve.wait_ge(dev_made, g + 1)
            dve.reciprocal(inv[0:p, k % 4, 0:t], dev[0:p, k % 4, 0:t]).then_inc(inv_made, 1)

        def scale(g, k, r, size):
            p, t = size
            s = k % 4
            if reused(g, 4):
                dve.wait_ge(y_stored[(k + 4) % LOADS], (r * 16 if k < 4 else r * 16 + 16))
                dve.wait_ge(u2_made, g - 3)
            dve.wait_ge(inv_made, g + 1)
            for j in range(t):
                last = dve.tensor_scalar(y[0:p, s, j, :], summed[s][0:p, j * 128:(j + 1) * 128],
                                         inv[0:p, s, j:j + 1], None, ALU.mult)
            last.then_inc(y_made, 1)

        def add(g, k, r, size):
            p, t = size
            s = k % 4
            dve.wait_ge(y_made, g + 1)
            if reused(g, 4):
                dve.wait_ge(y2_made, g - 3)
            dve.tensor_tensor(flat(u2[0:p, s, 0:t, :]), row_ps[0:p, 0:t * 128], flat(y[0:p, s, 0:t, :]), ALU.add) \
                .then_inc(u2_made, 1)

        def invert2(g, k, r, size):
            p, t = size
            dve.wait_ge(dev2_made, g + 1)
            dve.reciprocal(inv2[0:p, k % 4, 0:t], dev2[0:p, k % 4, 0:t]).then_inc(inv2_made, 1)

        def scale2(g, k, r, size):
            p, t = size
            s = k % 4
            if reused(g, 4):
                dve.wait_ge(y2_stored[(k + 4) % LOADS], (r * 16 if k < 4 else r * 16 + 16))
            dve.wait_ge(inv2_made, g + 1)
            for j in range(t):
                last = dve.tensor_scalar(y2[0:p, s, j, :], u2[0:p, s, j, :], inv2[0:p, s, j:j + 1], None, ALU.mult)
            last.then_inc(y2_made, 1)
        return [(3, invert), (5, invert2), (3, scale), (5, scale2), (3, add)], None
    return {"sync": sync, "tensor": tensor, "scalar": scalar, "vector": vector}


def sorted_order(nc, ctx, c, sh, tag, table, first_column):
    o = {}

    def keep(name, shape, dt):
        o[name] = ctx.enter_context(nc.sbuf_tensor(f"{tag}_{name}", shape, dt))

    keep("joined", [128, sh["ep"] + 1], BF16)
    keep("store_at", [128, sh["et"]], I32)
    keep("own_at", [128, sh["et"]], I32)
    keep("other_at", [128, sh["et"]], I32)
    with stage(nc) as (inner, semaphore):
        def sb(name, shape, dt=F32):
            return inner.enter_context(nc.sbuf_tensor(f"{tag}o_{name}", shape, dt))

        def sem(name):
            return semaphore(f"{tag}o_{name}")

        near = [sb(f"near{k}", [128, sh["et"], 2]) for k in range(3)]
        joined_col = sb("joined_col", [128, sh["et"]], BF16)
        more = sb("more", [128, sh["et"]])
        store_f = sb("store_f", [128, sh["et"]])
        bank = [inner.enter_context(nc.psum_tensor(f"{tag}o_bank{k}", [128, 512], F32)) for k in range(2)]
        rows_in, linked, columns_made, spread, copied = (
            sem(k) for k in ("rows_in", "linked", "columns_made", "spread", "copied"))
        with nc.Block() as block:
            @block.sync
            def _(sp):
                for k in range(3):
                    sp.dma_start(near[k][:, :, :], table[k:k + sh["ep"], first_column:first_column + 2]
                                 .rearrange("(t p) f -> p t f", p=128)).then_inc(rows_in, 16)

            @block.vector
            def _(dve):
                done = [0]

                def link(instruction):
                    instruction.then_inc(linked, 1)
                    done[0] += 1
                    dve.wait_ge(linked, done[0])
                dve.wait_ge(rows_in, 48)
                own = near[1][:, :, 0]
                dve.tensor_tensor(joined_col[:, :], near[0][:, :, 0], own, ALU.is_equal).then_inc(columns_made, 1)
                link(dve.tensor_tensor(more[:, :], near[2][:, :, 0], own, ALU.is_equal))
                link(dve.scalar_tensor_tensor(store_f[:, :], more[:, :], SKIP, own, ALU.mult, ALU.add))
                dve.tensor_copy(o["store_at"][:, :], store_f[:, :])
                dve.tensor_scalar(o["own_at"][:, :], own, float(sh["n"] - 1), None, ALU.min)
                dve.tensor_scalar(o["other_at"][:, :], near[1][:, :, 1], float(sh["n"] - 1), None, ALU.min)
                link(dve.memset(o["joined"][:, sh["ep"]:sh["ep"] + 1], 1.0 if sh["pads"] else 0.0))

            @block.tensor
            def _(pe):
                pe.wait_ge(columns_made, 1)

                def spread_out(g, s, r, tiles):
                    if reused(g):
                        pe.wait_ge(copied, g - 1)
                    for j in range(tiles):
                        last = pe.matmul(bank[s][:, j * 128:(j + 1) * 128],
                                         joined_col[:, bass.ds(g * GT + j, 1)].to_broadcast([128, 128]),
                                         c["identb"][:, :], start=True, stop=True)
                    last.then_inc(spread, 1)
                edge_groups(pe, sh, (0, spread_out))

            @block.scalar
            def _(act):
                def copy(g, s, r, tiles):
                    act.wait_ge(spread, g + 1)
                    act.activation(o["joined"][:, bass.ds(g * GE, tiles * 128)], bank[s][:, 0:tiles * 128],
                                   ACT.Copy).then_inc(copied, 1)
                edge_groups(act, sh, (0, copy))
    return o


def layer0_ends(nc, c, sh, t, w, o, ends_t):
    with stage(nc) as (ctx, semaphore):
        def sb(name, shape, dt=F32):
            return ctx.enter_context(nc.sbuf_tensor("e0_" + name, shape, dt))

        def sem(name):
            return semaphore("e0_" + name)

        rows = sb("rows", [128, 2, GT, 256])
        total = sb("total", [128, 2, GE])
        x_t = sb("x_t", [128, 2, GE])
        u = sb("u", [128, 2, GT, 128])
        y = sb("y", [128, 2, GT, 128])
        at = sb("at", [128, 2, GT], I32)
        message_t, turned, summed, y_turned = (ctx.enter_context(nc.psum_tensor("e0_" + k, [128, 512], F32))
                                               for k in ("message_t", "turned", "summed", "y_turned"))
        norm = norm_buffers(nc, ctx, semaphore, "e0_norm", c["ln_eps"])
        rows_in = [sem("rows_in0"), sem("rows_in1")]
        kept = [sem("kept0"), sem("kept1")]
        scattered = [sem("scattered0"), sem("scattered1")]
        message_turned, x_turned, total_made, x_t_out, sum_made, u_made, y_made, at_made, y_turn_made, y_t_out, issuing = (
            sem(k) for k in ("message_turned", "x_turned", "total_made", "x_t_out", "sum_made", "u_made", "y_made",
                             "at_made", "y_turn_made", "y_t_out", "issuing"))

        with nc.Block() as block:
            @block.sync
            def _(sp):
                def load(g, s, r, tiles):
                    if reused(g):
                        sp.wait_ge(u_made, g - 1)
                    sp.dma_start(rows[:, s, 0:tiles, :], edge_rows(t["rows_d"], g, tiles, 1, slice(0, 256))) \
                        .then_inc(rows_in[s], 16)

                def keep(g, s, r, tiles):
                    sp.wait_ge(y_made, g + 1)
                    sp.dma_start(edge_rows(t["x1_ends"], g, tiles), y[:, s, 0:tiles, :]).then_inc(kept[s], 16)
                edge_groups(sp, sh, (0, load), (2, keep))
                for s in range(2):
                    sp.wait_ge(kept[s], 16 * slot_groups(sh, s))

            @block.gpsimd
            def _(pool):
                last_node = pool.to_reg(sh["n"] - 1)

                def scatter(g, s, r, tiles):
                    pool.wait_ge(at_made, g + 1)
                    pool.wait_ge(y_made, g + 1)
                    pool.sem_inc(issuing, 1)
                    for j in range(tiles):
                        pool.indirect_dma_start(
                            out=t["x1"], out_offset=bass.IndirectOffsetOnAxis(ap=at[:, s, j:j + 1], axis=0),
                            in_=y[:, s, j, :], in_offset=None, bounds_check=last_node, oob_is_err=False) \
                            .then_inc(scattered[s], 16)
                edge_groups(pool, sh, (0, scatter))
                for s in range(2):
                    pool.wait_ge(scattered[s], 16 * slot_tiles(sh, s))

            @block.tensor
            def _(pe):
                def turn(g, s, r, tiles):
                    pe.wait_ge(rows_in[s], r * 16 + 16)
                    if reused(g, 1):
                        pe.wait_ge(total_made, g)
                    for j in range(tiles):
                        last = pe.transpose(message_t[:, j * 128:(j + 1) * 128], rows[:, s, j, 0:128], c["ident"][:, :])
                    last.then_inc(message_turned, 1)
                    if reused(g, 1):
                        pe.wait_ge(x_t_out, g)
                    for j in range(tiles):
                        last = pe.transpose(turned[:, j * 128:(j + 1) * 128], rows[:, s, j, 128:256], c["ident"][:, :])
                    last.then_inc(x_turned, 1)

                def project(g, s, r, tiles):
                    pe.wait_ge(x_t_out, g + 1)
                    pe.wait_ge(total_made, g + 1)
                    if reused(g, 1):
                        pe.wait_ge(u_made, g)
                    pe.matmul(summed[:, 0:tiles * 128], c["onesb"][:, :], flat(w["b0_m"][:, 0:tiles, :]), start=True,
                              stop=False, skip_group_check=True)
                    for j in range(tiles):
                        cols = slice(j * 128, (j + 1) * 128)
                        pe.matmul(summed[:, cols], x_t[:, s, cols], w["w0x"][:, :], start=False, stop=True,
                                  skip_group_check=True)
                        last = pe.matmul(summed[:, cols], total[:, s, cols], c["ident"][:, :], start=False, stop=True,
                                         skip_group_check=True)
                    last.then_inc(sum_made, 1)

                def turn_y(g, s, r, tiles):
                    pe.wait_ge(y_made, g + 1)
                    if reused(g, 1):
                        pe.wait_ge(y_t_out, g)
                    for j in range(tiles):
                        last = pe.transpose(y_turned[:, j * 128:(j + 1) * 128], y[:, s, j, :], c["ident"][:, :])
                    last.then_inc(y_turn_made, 1)
                edge_groups(pe, sh, (0, turn), (1, project), (3, turn_y))

            @block.scalar
            def _(act):
                def copy(g, s, r, tiles):
                    n = tiles * 128
                    act.wait_ge(x_turned, g + 1)
                    if reused(g):
                        act.wait_ge(sum_made, g - 1)
                    act.activation(x_t[:, s, 0:n], turned[:, 0:n], ACT.Copy).then_inc(x_t_out, 1)

                def copy_y(g, s, r, tiles):
                    act.wait_ge(y_turn_made, g + 1)
                    act.activation(ends_t[:, bass.ds(g * GE, tiles * 128)], y_turned[:, 0:tiles * 128], ACT.Copy) \
                        .then_inc(y_t_out, 1)
                edge_groups(act, sh, (0, copy), (1, lambda g, s, r, tiles: norm_deviation(norm, act, g, s, 128, tiles)),
                            (3, copy_y))

            @block.vector
            def _(dve):
                def sum_up(g, s, r, tiles):
                    n = tiles * 128
                    dve.wait_ge(message_turned, g + 1)
                    if reused(g, 1):
                        dve.wait_ge(total_made, g)
                    if reused(g):
                        dve.wait_ge(sum_made, g - 1)
                    dve.tensor_tensor_scan(
                        total[:, s, 0:n], o["joined"][:, bass.ds(g * GE, n)], message_t[:, 0:n],
                        total[:, 1 - s, GE - 1:GE] if reused(g, 1) else 0.0, ALU.mult, ALU.add).then_inc(total_made, 1)

                def measure(g, s, r, tiles):
                    dve.wait_ge(sum_made, g + 1)
                    if reused(g):
                        dve.wait_ge(y_made, g - 1)
                    dve.scalar_tensor_tensor(
                        u[:, s, 0:tiles, :], summed[:, 0:tiles * 128].rearrange("p (t f) -> p t f", f=128), 0.0,
                        rows[:, s, 0:tiles, 128:256], ALU.max, ALU.add).then_inc(u_made, 1)
                    dve.wait_ge(u_made, g + 1)
                    norm_measure(norm, dve, u[:, s, 0:tiles, :], g, s, 128, tiles)

                def scale(g, s, r, tiles):
                    if reused(g):
                        dve.wait_ge(kept[s], r * 16)
                        dve.wait_ge(scattered[s], r * 16 * GT)
                        dve.wait_ge(y_turn_made, g - 1)
                    dve.tensor_copy(at[:, s, 0:tiles], o["store_at"][:, bass.ds(g * GT, tiles)]).then_inc(at_made, 1)
                    norm_invert(norm, dve, g, s, 128, tiles)
                    norm_scale(norm, dve, y[:, s, 0:tiles, :], u[:, s, 0:tiles, :], g, s, 128, tiles).then_inc(y_made, 1)
                edge_groups(dve, sh, (0, sum_up), (1, measure), (2, scale))


def slot_groups(sh, s, slots=2):
    return len(range(s, sh["eg"] + (1 if sh["tail_e"] else 0), slots))


def slot_tiles(sh, s, slots=2):
    return sum(sh["tail_e"] if g == sh["eg"] else GT for g in range(s, sh["eg"] + (1 if sh["tail_e"] else 0), slots))


def spread_back(nc, c, sh, w, o, ends_t, scores):
    with stage(nc) as (ctx, semaphore):
        def sem(name):
            return semaphore("sb_" + name)

        kept = ctx.enter_context(nc.sbuf_tensor("sb_kept", [128, 2, GE], F32))
        last = ctx.enter_context(nc.sbuf_tensor("sb_last", [128, 2, GE], BF16))
        score = [ctx.enter_context(nc.psum_tensor(f"sb_score{k}", [128, 512], F32)) for k in range(2)]
        scored, last_made, kept_made, spread = sem("scored"), sem("last_made"), sem("kept_made"), sem("spread")
        groups = [(g, sh["tail_e"] if g == sh["eg"] else GT) for g in range(sh["eg"] + (1 if sh["tail_e"] else 0))][::-1]
        with nc.Block() as block:
            @block.tensor
            def _(pe):
                for k, (g, tiles) in enumerate(groups):
                    if k >= 2:
                        pe.wait_ge(kept_made, k - 1)
                    pe.matmul(score[k % 2][:, 0:tiles * 128], w["wd"][:, :], ends_t[:, g * GE:g * GE + tiles * 128],
                              start=True, stop=True).then_inc(scored, 1)

            @block.vector
            def _(dve):
                for k, (g, tiles) in enumerate(groups):
                    n, first = tiles * 128, g * GE
                    dve.wait_ge(scored, k + 1)
                    if k >= 2:
                        dve.wait_ge(spread, k - 1)
                    mark_last(dve, last[:, k % 2, 0:n], o, first, n).then_inc(last_made, 1)
                    dve.wait_ge(last_made, k + 1)
                    dve.tensor_tensor(kept[:, k % 2, 0:n], score[k % 2][:, 0:n], last[:, k % 2, 0:n], ALU.mult) \
                        .then_inc(kept_made, 1)
                    dve.wait_ge(kept_made, k + 1)
                    if k:
                        dve.wait_ge(spread, k)
                    dve.tensor_tensor_scan(
                        backwards(scores, first, n), backwards(o["joined"], first + 1, n),
                        backwards(kept, (k % 2) * GE, n, flat(kept[:, :, :])),
                        scores[:, first + n:first + n + 1] if k else 0.0, ALU.mult, ALU.add).then_inc(spread, 1)


def backwards(tensor, first, n, view=None):
    view = tensor[:, :] if view is None else view
    stop = first - 1 if first else None
    return view[:, first + n - 1:stop:-1]


def mark_last(dve, out, o, first, n):
    return dve.tensor_scalar(out, o["joined"][:, bass.ds(first + 1, n)], -1.0, 1.0, ALU.mult, ALU.add)


def attention(nc, c, sh, t, w, o, ends_t, scores, sums):
    with stage(nc) as (ctx, semaphore):
        def sb(name, shape=None, dt=F32):
            return ctx.enter_context(nc.sbuf_tensor("at_" + name, shape or [128, GE], dt))

        def sem(name):
            return semaphore("at_" + name)

        groups = sh["eg"] + (1 if sh["tail_e"] else 0)
        gather_at = sb("gather_at", [128, 2, GT], I32)
        xs = sb("xs", [128, 2, GT, 128])
        xs_t = sb("xs_t", [128, 2, GE])
        raw, logit, leak, fall, restart = (sb(k) for k in ("raw", "logit", "leak", "fall", "restart"))
        peak = sb("peak", [128, 2, GE + 1])
        step, below, up, down = (sb(k, [128, 2, GE]) for k in ("step", "below", "up", "down"))
        total, mixed = sb("total", [128, 2, GE]), sb("mixed", [128, 2, GE])
        weighted, mine, scaled = sb("weighted"), sb("mine"), sb("scaled")
        last = sb("last", [128, 2, GE], BF16)
        own, lift = leak, raw
        decay, p, keep_old, keep_own = step, below, up, down
        whole = inverse = scaled
        old = both = result = weighted
        sum_parts, square_parts = sb("sum_parts", [128, groups]), sb("square_parts", [128, groups])
        turned, score, own_score, squares, value0, value1, own_value0, own_value1 = (
            ctx.enter_context(nc.psum_tensor("at_" + k, [128, 512], F32))
            for k in ("turned", "score", "own_score", "squares", "value0", "value1", "own_value0", "own_value1"))
        value, own_value = [value0, value1], [own_value0, own_value1]
        gathered = [sem("gathered0"), sem("gathered1")]
        names = ("at_made x_turned x_t_out score_made value_made own_made leak_made raw_made logit_made own_out restart_made "
                 "peak_made carry_made fall_made step_made decay_made below_made p_made total_made weighted_made "
                 "mixed_made lift_made up_made keeps_made scaled_made whole_made inverse_made old_made mine_made "
                 "both_made result_made last_made summed squared issuing finished")
        S = {k: sem(k) for k in names.split()}

        with nc.Block() as block:
            @block.gpsimd
            def _(pool):
                last_node = pool.to_reg(sh["n"] - 1)

                def gather(g, s, r, tiles):
                    if reused(g):
                        pool.wait_ge(gathered[s], r * 16 * GT)
                    row_numbers(pool, gather_at, s, tiles, o["other_at"], g, S["at_made"])
                    pool.wait_ge(S["at_made"], g + 1)
                    if reused(g):
                        pool.wait_ge(S["x_turned"], g - 1)
                    pool.sem_inc(S["issuing"], 1)
                    for j in range(tiles):
                        pool.indirect_dma_start(
                            out=xs[:, s, j, :], out_offset=None, in_=t["x1"],
                            in_offset=bass.IndirectOffsetOnAxis(ap=gather_at[:, s, j:j + 1], axis=0),
                            bounds_check=last_node, oob_is_err=False).then_inc(gathered[s], 16)
                edge_groups(pool, sh, (0, gather))
                for s in range(2):
                    pool.wait_ge(gathered[s], 16 * slot_tiles(sh, s))

            @block.tensor
            def _(pe):
                def turn(g, s, r, tiles):
                    pe.wait_ge(gathered[s], r * 16 * GT + 16 * tiles)
                    if reused(g, 1):
                        pe.wait_ge(S["x_t_out"], g)
                    for j in range(tiles):
                        last_ = pe.transpose(turned[:, j * 128:(j + 1) * 128], xs[:, s, j, :], c["ident"][:, :])
                    last_.then_inc(S["x_turned"], 1)

                def project(g, s, r, tiles):
                    n = tiles * 128
                    ends = ends_t[:, bass.ds(g * GE, n)]
                    pe.wait_ge(S["x_t_out"], g + 1)
                    if reused(g, 1):
                        pe.wait_ge(S["raw_made"], g)
                    pe.matmul(score[:, 0:n], w["ws"][:, :], xs_t[:, s, 0:n], start=True, stop=True) \
                        .then_inc(S["score_made"], 1)
                    if reused(g, 1):
                        pe.wait_ge(S["leak_made"], g)
                    pe.matmul(own_score[:, 0:n], w["wsd"][:, :], ends, start=True, stop=True).then_inc(S["own_made"], 1)
                    if reused(g):
                        pe.wait_ge(S["mine_made"], g - 1)
                    pe.matmul(value[s][:, 0:n], w["w1"][:, :], xs_t[:, s, 0:n], start=True, stop=True)
                    pe.matmul(own_value[s][:, 0:n], w["w1"][:, :], ends, start=True, stop=True) \
                        .then_inc(S["value_made"], 1)
                edge_groups(pe, sh, (0, turn), (1, project))

            @block.scalar
            def _(act):
                def copy(g, s, r, tiles):
                    n = tiles * 128
                    act.wait_ge(S["x_turned"], g + 1)
                    if reused(g):
                        act.wait_ge(S["value_made"], g - 1)
                    act.activation(xs_t[:, s, 0:n], turned[:, 0:n], ACT.Copy).then_inc(S["x_t_out"], 1)

                def masks(g, s, r, tiles):
                    n = tiles * 128
                    if reused(g, 1):
                        act.wait_ge(S["step_made"], g)
                    act.activation(restart[:, 0:n], o["joined"][:, bass.ds(g * GE, n)], ACT.Copy, scale=-NEG, bias=NEG) \
                        .then_inc(S["restart_made"], 1)
                    if reused(g):
                        act.wait_ge(S["summed"], g - 1)
                    act.activation(last[:, s, 0:n], o["joined"][:, bass.ds(g * GE + 1, n)], ACT.Copy, scale=-1.0, bias=1.0) \
                        .then_inc(S["last_made"], 1)
                    act.wait_ge(S["own_made"], g + 1)
                    if reused(g, 1):
                        act.wait_ge(S["lift_made"], g)
                    act.activation(leak[:, 0:n], own_score[:, 0:n], ACT.Copy, scale=SLOPE).then_inc(S["own_out"], 1)

                def exps(g, s, r, tiles):
                    n = tiles * 128
                    act.wait_ge(S["step_made"], g + 1)
                    act.activation(decay[:, s, 0:n], step[:, s, 0:n], ACT.Exp).then_inc(S["decay_made"], 1)
                    act.wait_ge(S["below_made"], g + 1)
                    act.activation(p[:, s, 0:n], below[:, s, 0:n], ACT.Exp).then_inc(S["p_made"], 1)
                    act.wait_ge(S["lift_made"], g + 1)
                    if reused(g):
                        act.wait_ge(S["old_made"], g - 1)
                        act.wait_ge(S["whole_made"], g - 1)
                    act.activation(up[:, s, 0:n], lift[:, 0:n], ACT.Relu)
                    act.activation(down[:, s, 0:n], lift[:, 0:n], ACT.Relu, scale=-1.0).then_inc(S["up_made"], 1)
                    act.wait_ge(S["up_made"], g + 1)
                    act.activation(keep_old[:, s, 0:n], up[:, s, 0:n], ACT.Exp, scale=-1.0)
                    act.activation(keep_own[:, s, 0:n], down[:, s, 0:n], ACT.Exp, scale=-1.0).then_inc(S["keeps_made"], 1)

                def square(g, s, r, tiles):
                    act.wait_ge(S["summed"], g + 1)
                    if reused(g, 1):
                        act.wait_ge(S["squared"], g)
                    act.activation(squares[:, 0:tiles * 128], scores[:, bass.ds(g * GE, tiles * 128)], ACT.Square,
                                   accum_out=square_parts[:, bass.ds(g, 1)]).then_inc(S["squared"], 1)
                edge_groups(act, sh, (0, copy), (1, masks), (1, exps), (3, square))

            @block.vector
            def _(dve):
                def weigh(g, s, r, tiles):
                    n = tiles * 128
                    dve.wait_ge(S["score_made"], g + 1)
                    if reused(g, 1):
                        dve.wait_ge(S["up_made"], g)
                    dve.tensor_tensor(raw[:, 0:n], score[:, 0:n], scores[:, bass.ds(g * GE, n)], ALU.add) \
                        .then_inc(S["raw_made"], 1)
                    dve.wait_ge(S["raw_made"], g + 1)
                    if reused(g, 1):
                        dve.wait_ge(S["below_made"], g)
                    dve.scalar_tensor_tensor(logit[:, 0:n], raw[:, 0:n], SLOPE, raw[:, 0:n], ALU.mult, ALU.max) \
                        .then_inc(S["logit_made"], 1)
                    dve.wait_ge(S["own_out"], g + 1)
                    dve.tensor_tensor(own[:, 0:n], own_score[:, 0:n], leak[:, 0:n], ALU.max).then_inc(S["leak_made"], 1)
                    dve.wait_ge(S["restart_made"], g + 1)
                    dve.wait_ge(S["logit_made"], g + 1)
                    if reused(g, 1):
                        dve.wait_ge(S["carry_made"], g + 1)
                    else:
                        dve.memset(peak[:, 0, 0:1], 0.0).then_inc(S["carry_made"], 1)
                        dve.wait_ge(S["carry_made"], 1)
                    dve.tensor_tensor_scan(peak[:, s, 1:n + 1], restart[:, 0:n], logit[:, 0:n], peak[:, s, 0:1],
                                           ALU.add, ALU.max).then_inc(S["peak_made"], 1)
                    dve.wait_ge(S["peak_made"], g + 1)
                    dve.tensor_copy(peak[:, 1 - s, 0:1], peak[:, s, n:n + 1]).then_inc(S["carry_made"], 1)
                    if reused(g, 1):
                        dve.wait_ge(S["step_made"], g)
                    if reused(g):
                        dve.wait_ge(S["mixed_made"], g - 1)
                    dve.tensor_tensor(fall[:, 0:n], peak[:, s, 0:n], peak[:, s, 1:n + 1], ALU.subtract) \
                        .then_inc(S["fall_made"], 1)
                    dve.tensor_tensor(below[:, s, 0:n], logit[:, 0:n], peak[:, s, 1:n + 1], ALU.subtract) \
                        .then_inc(S["below_made"], 1)
                    dve.wait_ge(S["fall_made"], g + 1)
                    dve.scalar_tensor_tensor(step[:, s, 0:n], fall[:, 0:n], 0.0, restart[:, 0:n], ALU.min, ALU.add) \
                        .then_inc(S["step_made"], 1)
                    dve.wait_ge(S["leak_made"], g + 1)
                    dve.tensor_tensor(lift[:, 0:n], own[:, 0:n], peak[:, s, 1:n + 1], ALU.subtract) \
                        .then_inc(S["lift_made"], 1)

                def mix(g, s, r, tiles):
                    n = tiles * 128
                    dve.wait_ge(S["decay_made"], g + 1)
                    dve.wait_ge(S["p_made"], g + 1)
                    if reused(g, 1):
                        dve.wait_ge(S["result_made"], g)
                        dve.wait_ge(S["summed"], g)
                    dve.tensor_tensor_scan(total[:, s, 0:n], decay[:, s, 0:n], p[:, s, 0:n],
                                           total[:, 1 - s, GE - 1:GE] if reused(g, 1) else 0.0, ALU.mult, ALU.add) \
                        .then_inc(S["total_made"], 1)
                    dve.wait_ge(S["value_made"], g + 1)
                    dve.tensor_tensor(weighted[:, 0:n], value[s][:, 0:n], p[:, s, 0:n], ALU.mult) \
                        .then_inc(S["weighted_made"], 1)
                    dve.wait_ge(S["keeps_made"], g + 1)
                    dve.tensor_tensor(mine[:, 0:n], own_value[s][:, 0:n], keep_own[:, s, 0:n], ALU.mult) \
                        .then_inc(S["mine_made"], 1)
                    dve.wait_ge(S["weighted_made"], g + 1)
                    dve.tensor_tensor_scan(mixed[:, s, 0:n], decay[:, s, 0:n], weighted[:, 0:n],
                                           mixed[:, 1 - s, GE - 1:GE] if reused(g, 1) else 0.0, ALU.mult, ALU.add) \
                        .then_inc(S["mixed_made"], 1)
                    dve.wait_ge(S["total_made"], g + 1)
                    dve.tensor_tensor(scaled[:, 0:n], total[:, s, 0:n], keep_old[:, s, 0:n], ALU.mult) \
                        .then_inc(S["scaled_made"], 1)
                    dve.wait_ge(S["mixed_made"], g + 1)
                    dve.tensor_tensor(old[:, 0:n], mixed[:, s, 0:n], keep_old[:, s, 0:n], ALU.mult) \
                        .then_inc(S["old_made"], 1)
                    dve.wait_ge(S["scaled_made"], g + 1)
                    dve.scalar_tensor_tensor(whole[:, 0:n], scaled[:, 0:n], SOFTMAX_EPS, keep_own[:, s, 0:n],
                                             ALU.add, ALU.add).then_inc(S["whole_made"], 1)
                    dve.wait_ge(S["old_made"], g + 1)
                    dve.wait_ge(S["mine_made"], g + 1)
                    dve.tensor_tensor(both[:, 0:n], old[:, 0:n], mine[:, 0:n], ALU.add).then_inc(S["both_made"], 1)
                    dve.wait_ge(S["whole_made"], g + 1)
                    dve.reciprocal(inverse[:, 0:n], whole[:, 0:n]).then_inc(S["inverse_made"], 1)
                    dve.wait_ge(S["both_made"], g + 1)
                    dve.wait_ge(S["inverse_made"], g + 1)
                    dve.tensor_tensor(result[:, 0:n], both[:, 0:n], inverse[:, 0:n], ALU.mult) \
                        .then_inc(S["result_made"], 1)
                    dve.wait_ge(S["result_made"], g + 1)
                    dve.wait_ge(S["last_made"], g + 1)
                    dve.scalar_tensor_tensor(scores[:, bass.ds(g * GE, n)], result[:, 0:n], 1.0, last[:, s, 0:n],
                                             ALU.mult, ALU.mult, accum_out=sum_parts[:, bass.ds(g, 1)]) \
                        .then_inc(S["summed"], 1)
                edge_groups(dve, sh, (0, weigh), (1, mix))
                dve.wait_ge(S["summed"], groups)
                dve.wait_ge(S["squared"], groups)
                dve.tensor_reduce(sums[:, 0:1], sum_parts[:, :], AX.X, ALU.add)
                dve.tensor_reduce(sums[:, 1:2], square_parts[:, :], AX.X, ALU.add).then_inc(S["finished"], 1)


def batch_norm(nc, c, sh, w, gram, sums, out):
    with stage(nc) as (ctx, semaphore):
        def sb(name, shape):
            return ctx.enter_context(nc.sbuf_tensor("bn_" + name, shape, F32))

        def sem(name):
            return semaphore("bn_" + name)

        gw, mean, squares, mean2, var = sb("gw", [128, 128]), *(sb(k, [128, 1]) for k in ("mean", "squares", "mean2", "var"))
        total, total2, dev, inv = (sb(k, [128, 1]) for k in ("total", "total2", "dev", "inv"))
        moved, centre, scale, shift, bn_eps = (sb(k, [128, 1]) for k in ("moved", "centre", "scale", "shift", "bn_eps"))
        scale_all, shift_all, shift_row = sb("scale_all", [128, 128]), sb("shift_all", [128, 128]), sb("shift_row", [128, 128])
        a, b = (ctx.enter_context(nc.psum_tensor("bn_" + k, [128, 512], F32)) for k in ("a", "b"))
        linked, product, product_out, reduced, reduced_out, var_made, dev_made, columns, spread = (
            sem(k) for k in ("linked", "product", "product_out", "reduced", "reduced_out", "var_made", "dev_made", "columns", "spread"))
        with nc.Block() as block:
            @block.tensor
            def _(pe):
                pe.matmul(a[:, 0:128], gram[:, 0:128], w["w1"][:, :], start=True, stop=True).then_inc(product, 1)
                pe.wait_ge(product_out, 1)
                pe.matmul(b[:, 0:1], gw[:, :], c["ones"][:, 0:1], start=True, stop=True)
                pe.matmul(b[:, 1:2], w["w1"][:, :], gram[:, 128:129], start=True, stop=True).then_inc(reduced, 1)
                pe.wait_ge(columns, 1)
                pe.matmul(a[:, 128:256], scale_all[:, :], c["ident"][:, :], start=True, stop=True)
                pe.matmul(a[:, 256:384], shift_all[:, :], c["ident"][:, :], start=True, stop=True).then_inc(spread, 1)

            @block.scalar
            def _(act):
                act.wait_ge(var_made, 1)
                act.activation(dev[:, :], var[:, :], ACT.Sqrt, bias=bn_eps[:, :]).then_inc(dev_made, 1)

            @block.vector
            def _(dve):
                done = [0]

                def link(instruction):
                    instruction.then_inc(linked, 1)
                    done[0] += 1
                    dve.wait_ge(linked, done[0])
                dve.memset(bn_eps[:, :], BN_EPS)
                dve.wait_ge(product, 1)
                dve.tensor_tensor(gw[:, :], a[:, 0:128], w["w1"][:, :], ALU.mult).then_inc(product_out, 1)
                dve.wait_ge(reduced, 1)
                dve.tensor_tensor(total[:, :], b[:, 1:2], sums[:, 0:1], ALU.add)
                link(dve.tensor_tensor(total2[:, :], b[:, 0:1], sums[:, 1:2], ALU.add))
                dve.tensor_scalar(mean[:, :], total[:, :], 1.0 / sh["n"], None, ALU.mult)
                link(dve.tensor_scalar(squares[:, :], total2[:, :], 1.0 / sh["n"], None, ALU.mult))
                link(dve.tensor_tensor(mean2[:, :], mean[:, :], mean[:, :], ALU.mult))
                link(dve.tensor_tensor(centre[:, :], squares[:, :], mean2[:, :], ALU.subtract))
                dve.tensor_scalar(var[:, :], centre[:, :], 0.0, None, ALU.max).then_inc(var_made, 1)
                dve.wait_ge(dev_made, 1)
                link(dve.reciprocal(inv[:, :], dev[:, :]))
                link(dve.tensor_tensor(scale[:, :], inv[:, :], w["gamma"][:, :], ALU.mult))
                link(dve.tensor_tensor(moved[:, :], mean[:, :], w["bias1"][:, :], ALU.add))
                link(dve.tensor_tensor(mean2[:, :], w["bias1"][:, :], moved[:, :], ALU.subtract))
                link(dve.scalar_tensor_tensor(shift[:, :], mean2[:, :], scale[:, 0:1], w["beta"][:, :], ALU.mult, ALU.add))
                dve.tensor_scalar(out["scale"][:, :], scale[:, :], 0.5, None, ALU.mult)
                link(dve.tensor_scalar(out["shift"][:, :], shift[:, :], 0.5, None, ALU.mult))
                dve.tensor_scalar(scale_all[:, :], c["ones"][:, :], out["scale"][:, :], None, ALU.mult)
                dve.tensor_scalar(shift_all[:, :], c["ones"][:, :], out["shift"][:, :], None, ALU.mult) \
                    .then_inc(columns, 1)
                dve.wait_ge(spread, 1)
                link(dve.tensor_tensor(out["w1"][:, :], a[:, 128:256], w["w1"][:, :], ALU.mult))
                link(dve.tensor_copy(shift_row[:, :], a[:, 256:384]))
                bias_parts(dve, link, w, shift_row, out["shift_m"])


def layer1_ends(nc, c, sh, t, o, mixed, bn):
    with stage(nc) as (ctx, semaphore):
        def sb(name, shape, dt=F32):
            return ctx.enter_context(nc.sbuf_tensor("e1_" + name, shape, dt))

        def sem(name):
            return semaphore("e1_" + name)

        rows = sb("rows", [128, 2, GT, 128])
        active = sb("active", [128, 2, GE])
        u, y = sb("u", [128, 2, GT, 128]), sb("y", [128, 2, GT, 128])
        at = sb("at", [128, 2, GT], I32)
        turned = [ctx.enter_context(nc.psum_tensor(f"e1_turned{k}", [128, 512], F32)) for k in range(2)]
        norm = norm_buffers(nc, ctx, semaphore, "e1_norm", c["ln_eps4"])
        rows_in = [sem("rows_in0"), sem("rows_in1")]
        scattered = [sem("scattered0"), sem("scattered1")]
        active_made, turn_made, u_made, y_made, at_made, issuing = (
            sem(k) for k in ("active_made", "turn_made", "u_made", "y_made", "at_made", "issuing"))
        with nc.Block() as block:
            @block.sync
            def _(sp):
                def load(g, s, r, tiles):
                    if reused(g):
                        sp.wait_ge(u_made, g - 1)
                    sp.dma_start(rows[:, s, 0:tiles, :], edge_rows(t["x1_ends"], g, tiles)).then_inc(rows_in[s], 16)
                edge_groups(sp, sh, (0, load))

            @block.scalar
            def _(act):
                def activate(g, s, r, tiles):
                    n = tiles * 128
                    if reused(g):
                        act.wait_ge(turn_made, g - 1)
                    act.activation(active[:, s, 0:n], mixed[:, bass.ds(g * GE, n)], ACT.Relu,
                                   bias=bn["shift"][:, :], scale=bn["scale"][:, :]).then_inc(active_made, 1)
                edge_groups(act, sh, (0, activate), (1, lambda g, s, r, tiles: norm_deviation(norm, act, g, s, 128, tiles)))

            @block.tensor
            def _(pe):
                def turn(g, s, r, tiles):
                    pe.wait_ge(active_made, g + 1)
                    if reused(g):
                        pe.wait_ge(u_made, g - 1)
                    for j in range(tiles):
                        last = pe.transpose(turned[s][:, j * 128:(j + 1) * 128], active[:, s, j * 128:(j + 1) * 128],
                                            c["ident"][:, :])
                    last.then_inc(turn_made, 1)
                edge_groups(pe, sh, (0, turn))

            @block.vector
            def _(dve):
                def measure(g, s, r, tiles):
                    dve.wait_ge(turn_made, g + 1)
                    dve.wait_ge(rows_in[s], r * 16 + 16)
                    if reused(g):
                        dve.wait_ge(y_made, g - 1)
                    dve.tensor_tensor(flat(u[:, s, 0:tiles, :]), turned[s][:, 0:tiles * 128],
                                      flat(rows[:, s, 0:tiles, :]), ALU.add).then_inc(u_made, 1)
                    dve.wait_ge(u_made, g + 1)
                    norm_measure(norm, dve, u[:, s, 0:tiles, :], g, s, 128, tiles)

                def scale(g, s, r, tiles):
                    if reused(g):
                        dve.wait_ge(scattered[s], r * 16 * GT)
                    dve.tensor_copy(at[:, s, 0:tiles], o["store_at"][:, bass.ds(g * GT, tiles)]).then_inc(at_made, 1)
                    norm_invert(norm, dve, g, s, 128, tiles)
                    norm_scale(norm, dve, y[:, s, 0:tiles, :], u[:, s, 0:tiles, :], g, s, 128, tiles).then_inc(y_made, 1)
                edge_groups(dve, sh, (0, measure), (1, scale))

            @block.gpsimd
            def _(pool):
                scatter_rows(pool, sh, t["x2"], y, at, y_made, at_made, issuing, scattered)


def scatter_rows(pool, sh, table, y, at, y_made, at_made, issuing, scattered):
    last_node = pool.to_reg(sh["n"] - 1)

    def scatter(g, s, r, tiles):
        pool.wait_ge(at_made, g + 1)
        pool.wait_ge(y_made, g + 1)
        pool.sem_inc(issuing, 1)
        for j in range(tiles):
            pool.indirect_dma_start(
                out=table, out_offset=bass.IndirectOffsetOnAxis(ap=at[:, s, j:j + 1], axis=0),
                in_=y[:, s, j, :], in_offset=None, bounds_check=last_node, oob_is_err=False) \
                .then_inc(scattered[s], 16)
    edge_groups(pool, sh, (0, scatter))
    for s in range(2):
        pool.wait_ge(scattered[s], 16 * slot_tiles(sh, s))


def build_pairs(nc, c, sh, t, pos):
    with stage(nc) as (ctx, semaphore):
        def sb(name, shape, dt=F32):
            return ctx.enter_context(nc.sbuf_tensor("pr_" + name, shape, dt))

        def sem(name):
            return semaphore("pr_" + name)

        ends_i = sb("ends_i", [128, 2, sh["et"]], I32)
        pair = sb("pair", [128, 2, GT, 2])
        put_at = sb("put_at", [128, 2, GT], I32)
        ends_in, pair_made, issuing = sem("ends_in"), sem("pair_made"), sem("issuing")
        stored = [sem("stored0"), sem("stored1")]
        with nc.Block() as block:
            @block.sync
            def _(sp):
                sp.dma_start(ends_i[:, 0, :], t["src_cols"]).then_inc(ends_in, 16)
                sp.dma_start(ends_i[:, 1, :], t["dst_cols"]).then_inc(ends_in, 16)

            @block.vector
            def _(dve):
                dve.wait_ge(ends_in, 32)

                def make(g, s, r, tiles):
                    if reused(g):
                        dve.wait_ge(stored[s], r * 16 * GT)
                    dve.tensor_copy(pair[:, s, 0:tiles, :],
                                    ends_i[:, :, bass.ds(g * GT, tiles)].rearrange("p k t -> p t k"))
                    dve.tensor_copy(put_at[:, s, 0:tiles], pos[:, bass.ds(g * GT, tiles)]).then_inc(pair_made, 1)
                edge_groups(dve, sh, (0, make))

            @block.gpsimd
            def _(pool):
                last_row = pool.to_reg(sh["ep"] + 1)

                def scatter(g, s, r, tiles):
                    pool.wait_ge(pair_made, g + 1)
                    pool.sem_inc(issuing, 1)
                    for j in range(tiles):
                        pool.indirect_dma_start(
                            out=t["rows_s"], out_offset=bass.IndirectOffsetOnAxis(ap=put_at[:, s, j:j + 1], axis=0),
                            in_=pair[:, s, j, :], in_offset=None,
                            bounds_check=last_row, oob_is_err=False).then_inc(stored[s], 16)
                edge_groups(pool, sh, (0, scatter))
                for s in range(2):
                    pool.wait_ge(stored[s], 16 * slot_tiles(sh, s))


def compose(nc, ctx, c, w):
    def keep(name, shape, dt=F32):
        w[name] = ctx.enter_context(nc.sbuf_tensor("w_" + name, shape, dt))

    keep("wz", [128, 128])
    keep("bz_mc", [128, NT, 128], BF16)
    keep("lone_mc", [128, NT, 128], BF16)
    keep("lone_m", [128, NT, 128], BF16)
    with stage(nc) as (inner, semaphore):
        def sb(name):
            return inner.enter_context(nc.sbuf_tensor("co_" + name, [128, 128], F32))

        def sem(name):
            return semaphore("co_" + name)

        spread, bz, z, size, decayed, logged, lone, raised, whole, centred = (
            sb(k) for k in ("spread", "bz", "z", "size", "decayed", "logged", "lone", "raised", "whole", "centred"))
        total = inner.enter_context(nc.sbuf_tensor("co_total", [128, 1], F32))
        half = inner.enter_context(nc.sbuf_tensor("co_half", [128, 1], F32))
        products = inner.enter_context(nc.psum_tensor("co_products", [128, 512], F32))
        linked, spread_made, product, z_made, log_made, chained = (
            sem(k) for k in ("linked", "spread_made", "product", "z_made", "log_made", "chained"))
        with nc.Block() as block:
            @block.tensor
            def _(pe):
                pe.matmul(products[:, 0:128], w["w2n"][:, :], w["w2l_b"][:, :], start=True, stop=True)
                pe.matmul(products[:, 128:256], c["ones"][:, :], w["l3w3"][:, :], start=True, stop=True)
                pe.wait_ge(spread_made, 1)
                pe.matmul(products[:, 256:384], spread[:, :], w["w2l_b"][:, :], start=True, stop=True) \
                    .then_inc(product, 1)

            @block.scalar
            def _(act):
                act.wait_ge(z_made, 1)
                act.activation(size[:, :], z[:, :], ACT.Abs).then_inc(chained, 1)
                act.wait_ge(chained, 1)
                act.activation(decayed[:, :], size[:, :], ACT.Exp, scale=-1.0).then_inc(chained, 1)
                act.wait_ge(chained, 2)
                act.activation(logged[:, :], decayed[:, :], ACT.Ln, scale=0.5, bias=half[:, :]).then_inc(log_made, 1)

            @block.vector
            def _(dve):
                done = [0]

                def link(instruction):
                    instruction.then_inc(linked, 1)
                    done[0] += 1
                    dve.wait_ge(linked, done[0])
                dve.memset(half[:, :], 0.5)
                dve.tensor_scalar(spread[:, :], c["ones"][:, :], w["b2n"][:, :], None, ALU.mult).then_inc(spread_made, 1)
                dve.wait_ge(product, 1)
                dve.tensor_tensor(z[:, :], products[:, 128:256], w["l3b3"][:, :], ALU.add).then_inc(z_made, 1)
                link(dve.tensor_tensor(raised[:, :], w["w2l_a"][:, :], c["ident"][:, :], ALU.add))
                link(dve.tensor_tensor(whole[:, :], products[:, 0:128], raised[:, :], ALU.add))
                link(dve.tensor_tensor(bz[:, :], products[:, 256:384], w["b2l"][:, :], ALU.add))

                def centre(out, rows):
                    link(dve.tensor_reduce(total[:, :], rows[:, :], AX.X, ALU.add))
                    link(dve.tensor_scalar(total[:, :], total[:, :], 1.0 / D, None, ALU.mult))
                    link(dve.tensor_scalar(out[:, :], rows[:, :], total[:, 0:1], None, ALU.subtract))
                centre(w["wz"], whole)
                centre(centred, bz)
                bias_parts(dve, link, w, centred, w["bz_mc"])
                dve.wait_ge(log_made, 1)
                link(dve.scalar_tensor_tensor(lone[:, :], z[:, :], 0.0, logged[:, :], ALU.max, ALU.add))
                bias_parts(dve, link, w, lone, w["lone_m"])
                centre(centred, lone)
                bias_parts(dve, link, w, centred, w["lone_mc"])


def layer2_ends(nc, c, sh, t, w, o):
    with stage(nc) as (ctx, semaphore):
        def sb(name, shape, dt=F32):
            return ctx.enter_context(nc.sbuf_tensor("e2_" + name, shape, dt))

        def sem(name):
            return semaphore("e2_" + name)

        own_at, other_at, at = (sb(k, [128, 4, GT], I32) for k in ("own_at", "other_at", "at"))
        xa, xb = sb("xa", [128, 4, GT, 128]), sb("xb", [128, 4, GT, 128])
        xa_t, xb_t = sb("xa_t", [128, 2, GE]), sb("xb_t", [128, 2, GE])
        h_other, gap, new_h = sb("h_other", [128, GE]), sb("gap", [128, GE]), sb("new_h", [128, GE])
        seg_sum, count = sb("seg_sum", [128, 2, GE]), sb("count", [128, 2, GE])
        numerator, inverse, mean = sb("numerator", [128, GE]), sb("inverse", [128, GE]), sb("mean", [128, 2, GE])
        u, y = sb("u", [128, 2, GT, 128]), sb("y", [128, 4, GT, 128])
        u2, y2 = sb("u2", [128, 2, GT, 128]), sb("y2", [128, 4, GT, 128])
        turned_a, turned_b, h_ps, gap_ps, own_ps, new_ps, out_ps, lone_ps = (
            ctx.enter_context(nc.psum_tensor("e2_" + k, [128, 512], F32))
            for k in ("turned_a", "turned_b", "h_ps", "gap_ps", "own_ps", "new_ps", "out_ps", "lone_ps"))
        norm, norm2 = norm_buffers(nc, ctx, semaphore, "e2_norm", c["ln_eps"]), norm_buffers(nc, ctx, semaphore, "e2_norm2", c["ln_eps"])
        gathered = [sem(f"gathered{k}") for k in range(4)]
        scattered = [sem(f"scattered{k}") for k in range(4)]
        scattered2 = [sem(f"scattered2{k}") for k in range(4)]
        (at_made, x_turned, x_t_out, h_made, h_out, new_made, new_out, seg_made, count_made, num_made, inv_made,
         mean_made, out_made, u_made, y_made, u2_made, y2_made, lone_made, put_made, issuing) = (sem(k) for k in (
             "at_made", "x_turned", "x_t_out", "h_made", "h_out", "new_made", "new_out", "seg_made", "count_made",
             "num_made", "inv_made", "mean_made", "out_made", "u_made", "y_made", "u2_made", "y2_made", "lone_made",
             "put_made", "issuing"))

        with nc.Block() as block:
            @block.gpsimd
            def _(pool):
                last_node = pool.to_reg(sh["n"] - 1)

                def gather(g, k, r, tiles):
                    if reused(g, 4):
                        pool.wait_ge(gathered[k], r * 32 * GT)
                    row_numbers(pool, own_at, k, tiles, o["own_at"], g, at_made)
                    row_numbers(pool, other_at, k, tiles, o["other_at"], g, at_made)
                    pool.wait_ge(at_made, 2 * g + 2)
                    if reused(g, 4):
                        pool.wait_ge(x_turned, g - 3)
                        pool.wait_ge(u_made, g - 3)
                    pool.sem_inc(issuing, 1)
                    for j in range(tiles):
                        for to, numbers in ((xa, own_at), (xb, other_at)):
                            pool.indirect_dma_start(
                                out=to[:, k, j, :], out_offset=None, in_=t["x2"],
                                in_offset=bass.IndirectOffsetOnAxis(ap=numbers[:, k, j:j + 1], axis=0),
                                bounds_check=last_node, oob_is_err=False).then_inc(gathered[k], 16)

                def scatter(g, k, r, tiles):
                    if reused(g, 4):
                        pool.wait_ge(scattered[k], r * 16 * GT)
                        pool.wait_ge(scattered2[k], r * 16 * GT)
                    row_numbers(pool, at, k, tiles, o["store_at"], g, put_made)
                    pool.wait_ge(put_made, g + 1)
                    pool.wait_ge(y_made, g + 1)
                    pool.sem_inc(issuing, 1)
                    for j in range(tiles):
                        pool.indirect_dma_start(
                            out=t["x3"], out_offset=bass.IndirectOffsetOnAxis(ap=at[:, k, j:j + 1], axis=0),
                            in_=y[:, k, j, :], in_offset=None, bounds_check=last_node, oob_is_err=False) \
                            .then_inc(scattered[k], 16)

                def scatter2(g, k, r, tiles):
                    pool.wait_ge(y2_made, g + 1)
                    pool.sem_inc(issuing, 1)
                    for j in range(tiles):
                        pool.indirect_dma_start(
                            out=t["out"], out_offset=bass.IndirectOffsetOnAxis(ap=at[:, k, j:j + 1], axis=0),
                            in_=y2[:, k, j, :], in_offset=None, bounds_check=last_node, oob_is_err=False) \
                            .then_inc(scattered2[k], 16)
                edge_rings(pool, sh, (0, gather), (4, scatter), (5, scatter2))
                for k in range(4):
                    pool.wait_ge(scattered[k], 16 * slot_tiles(sh, k, 4))
                    pool.wait_ge(scattered2[k], 16 * slot_tiles(sh, k, 4))

            @block.tensor
            def _(pe):
                pe.matmul(lone_ps[:, :], c["onesb"][:, :], flat(w["lone_m"][:, :, :]), start=True, stop=True) \
                    .then_inc(lone_made, 1)

                def turn(g, k, r, tiles):
                    s = k % 2
                    pe.wait_ge(gathered[k], r * 32 * GT + 32 * tiles)
                    if reused(g, 1):
                        pe.wait_ge(x_t_out, g)
                    for j in range(tiles):
                        pe.transpose(turned_a[:, j * 128:(j + 1) * 128], xa[:, k, j, :], c["ident"][:, :])
                        last = pe.transpose(turned_b[:, j * 128:(j + 1) * 128], xb[:, k, j, :], c["ident"][:, :])
                    last.then_inc(x_turned, 1)

                def project(g, k, r, tiles):
                    s = k % 2
                    n = tiles * 128
                    pe.wait_ge(x_t_out, g + 1)
                    if reused(g, 1):
                        pe.wait_ge(h_out, g)
                        pe.wait_ge(num_made, g)
                    pe.matmul(h_ps[:, 0:n], w["w2n_t"][:, :], xb_t[:, s, 0:n], start=True, stop=True)
                    pe.matmul(gap_ps[:, 0:n], w["w2n_t"][:, :], xa_t[:, s, 0:n], start=True, stop=False)
                    pe.matmul(gap_ps[:, 0:n], w["w2n_neg"][:, :], xb_t[:, s, 0:n], start=False, stop=True)
                    pe.matmul(own_ps[:, 0:n], w["w2n_t"][:, :], xa_t[:, s, 0:n], start=True, stop=True) \
                        .then_inc(h_made, 1)

                def edge(g, k, r, tiles):
                    s = k % 2
                    n = tiles * 128
                    pe.wait_ge(h_out, g + 1)
                    if reused(g, 1):
                        pe.wait_ge(new_out, g)
                    pe.matmul(new_ps[:, 0:n], w["w2e_a"][:, :], h_other[:, 0:n], start=True, stop=False)
                    pe.matmul(new_ps[:, 0:n], w["w2e_b"][:, :], gap[:, 0:n], start=False, stop=True) \
                        .then_inc(new_made, 1)

                def combine(g, k, r, tiles):
                    s = k % 2
                    pe.wait_ge(mean_made, g + 1)
                    if reused(g, 1):
                        pe.wait_ge(u_made, g)
                    pe.matmul(out_ps[:, 0:tiles * 128], c["onesb"][:, :], flat(w["b2l_m"][:, 0:tiles, :]), start=True,
                              stop=False, skip_group_check=True)
                    for j in range(tiles):
                        cols = slice(j * 128, (j + 1) * 128)
                        pe.matmul(out_ps[:, cols], xa_t[:, s, cols], w["w2l_a"][:, :], start=False, stop=True,
                                  skip_group_check=True)
                        last = pe.matmul(out_ps[:, cols], mean[:, s, cols], w["w2l_b"][:, :], start=False, stop=True,
                                         skip_group_check=True)
                    last.then_inc(out_made, 1)
                edge_rings(pe, sh, (0, turn), (1, project), (2, combine), (1, edge))

            @block.scalar
            def _(act):
                def copies(g, k, r, tiles):
                    s = k % 2
                    n = tiles * 128
                    act.wait_ge(x_turned, g + 1)
                    if reused(g):
                        act.wait_ge(out_made, g - 1)
                    act.activation(xa_t[:, s, 0:n], turned_a[:, 0:n], ACT.Copy)
                    act.activation(xb_t[:, s, 0:n], turned_b[:, 0:n], ACT.Copy).then_inc(x_t_out, 1)

                def edge(g, k, r, tiles):
                    n = tiles * 128
                    act.wait_ge(h_made, g + 1)
                    if reused(g, 1):
                        act.wait_ge(new_made, g)
                    act.activation(h_other[:, 0:n], h_ps[:, 0:n], ACT.Identity, bias=w["b2n"][:, :])
                    act.activation(gap[:, 0:n], gap_ps[:, 0:n], ACT.Abs).then_inc(h_out, 1)
                    act.wait_ge(new_made, g + 1)
                    if reused(g, 1):
                        act.wait_ge(seg_made, g)
                    act.activation(new_h[:, 0:n], new_ps[:, 0:n], ACT.Identity, bias=w["b2e"][:, :]).then_inc(new_out, 1)
                edge_rings(act, sh, (0, copies), (1, edge),
                           (2, lambda g, k, r, tiles: norm_deviation(norm, act, g, k % 2, 128, tiles)),
                           (3, lambda g, k, r, tiles: norm_deviation(norm2, act, g, k % 2, 128, tiles)))

            @block.vector
            def _(dve):
                dve.wait_ge(lone_made, 1)

                def aggregate(g, k, r, tiles):
                    s = k % 2
                    n = tiles * 128
                    joined = o["joined"][:, bass.ds(g * GE, n)]
                    if reused(g, 1):
                        dve.wait_ge(count_made, g)
                        dve.wait_ge(mean_made, g)
                    dve.tensor_tensor_scan(count[:, s, 0:n], joined, c["ones"][:, 0:1].to_broadcast([128, n]),
                                           count[:, 1 - s, GE - 1:GE] if reused(g, 1) else 0.0,
                                           ALU.mult, ALU.add).then_inc(count_made, 1)
                    dve.wait_ge(count_made, g + 1)
                    dve.reciprocal(inverse[:, 0:n], count[:, s, 0:n]).then_inc(inv_made, 1)
                    dve.wait_ge(new_out, g + 1)
                    if reused(g, 1):
                        dve.wait_ge(seg_made, g)
                    dve.tensor_tensor_scan(seg_sum[:, s, 0:n], joined, new_h[:, 0:n],
                                           seg_sum[:, 1 - s, GE - 1:GE] if reused(g, 1) else 0.0,
                                           ALU.mult, ALU.add).then_inc(seg_made, 1)
                    dve.wait_ge(seg_made, g + 1)
                    dve.wait_ge(h_made, g + 1)
                    dve.scalar_tensor_tensor(numerator[:, 0:n], own_ps[:, 0:n], w["b2n"][:, :], seg_sum[:, s, 0:n],
                                             ALU.add, ALU.add).then_inc(num_made, 1)
                    dve.wait_ge(num_made, g + 1)
                    dve.wait_ge(inv_made, g + 1)
                    if reused(g):
                        dve.wait_ge(out_made, g - 1)
                    dve.tensor_tensor(mean[:, s, 0:n], numerator[:, 0:n], inverse[:, 0:n], ALU.mult) \
                        .then_inc(mean_made, 1)

                def measure(g, k, r, tiles):
                    s = k % 2
                    dve.wait_ge(out_made, g + 1)
                    if reused(g):
                        dve.wait_ge(y_made, g - 1)
                    dve.tensor_tensor(flat(u[:, s, 0:tiles, :]), out_ps[:, 0:tiles * 128],
                                      flat(xa[:, k, 0:tiles, :]), ALU.add).then_inc(u_made, 1)
                    dve.wait_ge(u_made, g + 1)
                    norm_measure(norm, dve, u[:, s, 0:tiles, :], g, s, 128, tiles)

                def scale(g, k, r, tiles):
                    s = k % 2
                    if reused(g):
                        dve.wait_ge(u2_made, g - 1)
                    if reused(g, 4):
                        dve.wait_ge(scattered[k], r * 16 * GT)
                    norm_invert(norm, dve, g, s, 128, tiles)
                    norm_scale(norm, dve, y[:, k, 0:tiles, :], u[:, s, 0:tiles, :], g, s, 128, tiles).then_inc(y_made, 1)

                def measure2(g, k, r, tiles):
                    s = k % 2
                    dve.wait_ge(y_made, g + 1)
                    if reused(g):
                        dve.wait_ge(y2_made, g - 1)
                    dve.tensor_tensor(flat(u2[:, s, 0:tiles, :]), lone_ps[:, 0:tiles * 128],
                                      flat(y[:, k, 0:tiles, :]), ALU.add).then_inc(u2_made, 1)
                    dve.wait_ge(u2_made, g + 1)
                    norm_measure(norm2, dve, u2[:, s, 0:tiles, :], g, s, 128, tiles)

                def scale2(g, k, r, tiles):
                    s = k % 2
                    if reused(g, 4):
                        dve.wait_ge(scattered2[k], r * 16 * GT)
                    norm_invert(norm2, dve, g, s, 128, tiles)
                    norm_scale(norm2, dve, y2[:, k, 0:tiles, :], u2[:, s, 0:tiles, :], g, s, 128, tiles).then_inc(y2_made, 1)
                edge_rings(dve, sh, (0, aggregate), (1, measure), (2, scale), (2, measure2), (3, scale2))


def layer3_ends(nc, c, sh, t, w, o):
    with stage(nc) as (ctx, semaphore):
        def sb(name, shape, dt=F32):
            return ctx.enter_context(nc.sbuf_tensor("e3_" + name, shape, dt))

        def sem(name):
            return semaphore("e3_" + name)

        own_at, other_at, at = (sb(k, [128, 4, GT], I32) for k in ("own_at", "other_at", "at"))
        xa, xb = sb("xa", [128, 4, GT, 128]), sb("xb", [128, 4, GT, 128])
        factor, message = sb("factor", [128, 4, GT, 128]), sb("message", [128, 2, GT, 128])
        times, restart = sb("times", [128, GE]), sb("restart", [128, GE])
        product = sb("product", [128, 2, GE])
        size, decayed, logged = sb("size", [128, GE]), sb("decayed", [128, GE]), sb("logged", [128, GE])
        z, u, y = sb("z", [128, 2, GT, 128]), sb("u", [128, 2, GT, 128]), sb("y", [128, 4, GT, 128])
        half = sb("half", [128, 1])
        turned, out_ps = (ctx.enter_context(nc.psum_tensor("e3_" + k, [128, 512], F32)) for k in ("turned", "out_ps"))
        norm = norm_buffers(nc, ctx, semaphore, "e3_norm", c["ln_eps"])
        gathered = [sem(f"gathered{k}") for k in range(4)]
        factor_in = [sem(f"factor_in{k}") for k in range(4)]
        scattered = [sem(f"scattered{k}") for k in range(4)]
        (at_made, half_made, message_made, message_turned, times_made, restart_made, product_made, out_made, size_made,
         decay_made, log_made, z_made, u_made, y_made, put_made, issuing) = (sem(k) for k in (
             "at_made", "half_made", "message_made", "message_turned", "times_made", "restart_made", "product_made",
             "out_made", "size_made", "decay_made", "log_made", "z_made", "u_made", "y_made", "put_made", "issuing"))

        with nc.Block() as block:
            @block.sync
            def _(sp):
                def load(g, k, r, tiles):
                    if reused(g, 4):
                        sp.wait_ge(message_made, g - 3)
                    sp.dma_start(factor[:, k, 0:tiles, :], edge_rows(t["rows_d"], g, tiles, 1, slice(256, 384))) \
                        .then_inc(factor_in[k], 16)
                edge_rings(sp, sh, (0, load))

            @block.gpsimd
            def _(pool):
                last_node = pool.to_reg(sh["n"] - 1)

                def gather(g, k, r, tiles):
                    if reused(g, 4):
                        pool.wait_ge(gathered[k], r * 32 * GT)
                    row_numbers(pool, own_at, k, tiles, o["own_at"], g, at_made)
                    row_numbers(pool, other_at, k, tiles, o["other_at"], g, at_made)
                    pool.wait_ge(at_made, 2 * g + 2)
                    if reused(g, 4):
                        pool.wait_ge(message_made, g - 3)
                        pool.wait_ge(u_made, g - 3)
                    pool.sem_inc(issuing, 1)
                    for j in range(tiles):
                        for to, numbers in ((xa, own_at), (xb, other_at)):
                            pool.indirect_dma_start(
                                out=to[:, k, j, :], out_offset=None, in_=t["x3"],
                                in_offset=bass.IndirectOffsetOnAxis(ap=numbers[:, k, j:j + 1], axis=0),
                                bounds_check=last_node, oob_is_err=False).then_inc(gathered[k], 16)

                def scatter(g, k, r, tiles):
                    if reused(g, 4):
                        pool.wait_ge(scattered[k], r * 16 * GT)
                    row_numbers(pool, at, k, tiles, o["store_at"], g, put_made)
                    pool.wait_ge(put_made, g + 1)
                    pool.wait_ge(y_made, g + 1)
                    pool.sem_inc(issuing, 1)
                    for j in range(tiles):
                        pool.indirect_dma_start(
                            out=t["out"], out_offset=bass.IndirectOffsetOnAxis(ap=at[:, k, j:j + 1], axis=0),
                            in_=y[:, k, j, :], in_offset=None, bounds_check=last_node, oob_is_err=False) \
                            .then_inc(scattered[k], 16)
                edge_rings(pool, sh, (0, gather), (4, scatter))
                for k in range(4):
                    pool.wait_ge(scattered[k], 16 * slot_tiles(sh, k, 4))

            @block.tensor
            def _(pe):
                def turn(g, k, r, tiles):
                    s = k % 2
                    pe.wait_ge(message_made, g + 1)
                    if reused(g, 1):
                        pe.wait_ge(product_made, g)
                    for j in range(tiles):
                        last = pe.transpose(turned[:, j * 128:(j + 1) * 128], message[:, s, j, :], c["ident"][:, :])
                    last.then_inc(message_turned, 1)

                def project(g, k, r, tiles):
                    s = k % 2
                    pe.wait_ge(product_made, g + 1)
                    if reused(g, 1):
                        pe.wait_ge(z_made, g)
                    pe.matmul(out_ps[:, 0:tiles * 128], c["onesb"][:, :], flat(w["l3b3_m"][:, 0:tiles, :]), start=True,
                              stop=False, skip_group_check=True)
                    for j in range(tiles):
                        cols = slice(j * 128, (j + 1) * 128)
                        last = pe.matmul(out_ps[:, cols], product[:, s, cols], w["l3w3"][:, :], start=False, stop=True,
                                         skip_group_check=True)
                    last.then_inc(out_made, 1)
                edge_rings(pe, sh, (0, turn), (1, project))

            @block.scalar
            def _(act):
                act.wait_ge(half_made, 1)

                def softplus(g, k, r, tiles):
                    n = tiles * 128
                    act.wait_ge(out_made, g + 1)
                    if reused(g, 1):
                        act.wait_ge(decay_made, g)
                    act.activation(size[:, 0:n], out_ps[:, 0:n], ACT.Abs).then_inc(size_made, 1)
                    act.wait_ge(size_made, g + 1)
                    if reused(g, 1):
                        act.wait_ge(log_made, g)
                    act.activation(decayed[:, 0:n], size[:, 0:n], ACT.Exp, scale=-1.0).then_inc(decay_made, 1)
                    act.wait_ge(decay_made, g + 1)
                    if reused(g, 1):
                        act.wait_ge(z_made, g)
                    act.activation(logged[:, 0:n], decayed[:, 0:n], ACT.Ln, scale=0.5, bias=half[:, :]) \
                        .then_inc(log_made, 1)
                edge_rings(act, sh, (0, softplus), (1, lambda g, k, r, tiles: norm_deviation(norm, act, g, k % 2, 128, tiles)))

            @block.vector
            def _(dve):
                dve.memset(half[:, :], 0.5).then_inc(half_made, 1)

                def multiply(g, k, r, tiles):
                    s = k % 2
                    dve.wait_ge(gathered[k], r * 32 * GT + 32 * tiles)
                    dve.wait_ge(factor_in[k], r * 16 + 16)
                    if reused(g):
                        dve.wait_ge(message_turned, g - 1)
                    dve.tensor_tensor(flat(message[:, s, 0:tiles, :]), flat(xb[:, k, 0:tiles, :]),
                                      flat(factor[:, k, 0:tiles, :]), ALU.mult).then_inc(message_made, 1)

                def product_up(g, k, r, tiles):
                    s = k % 2
                    n = tiles * 128
                    dve.wait_ge(message_turned, g + 1)
                    if reused(g, 1):
                        dve.wait_ge(product_made, g)
                    dve.tensor_tensor(times[:, 0:n], turned[:, 0:n], o["joined"][:, bass.ds(g * GE, n)], ALU.mult) \
                        .then_inc(times_made, 1)
                    dve.wait_ge(times_made, g + 1)
                    dve.tensor_tensor(restart[:, 0:n], turned[:, 0:n], times[:, 0:n], ALU.subtract) \
                        .then_inc(restart_made, 1)
                    dve.wait_ge(restart_made, g + 1)
                    if reused(g):
                        dve.wait_ge(out_made, g - 1)
                    dve.tensor_tensor_scan(product[:, s, 0:n], times[:, 0:n], restart[:, 0:n],
                                           product[:, 1 - s, GE - 1:GE] if reused(g, 1) else 1.0,
                                           ALU.mult, ALU.add).then_inc(product_made, 1)

                def measure(g, k, r, tiles):
                    s = k % 2
                    dve.wait_ge(out_made, g + 1)
                    dve.wait_ge(log_made, g + 1)
                    if reused(g):
                        dve.wait_ge(u_made, g - 1)
                    dve.scalar_tensor_tensor(flat(z[:, s, 0:tiles, :]), out_ps[:, 0:tiles * 128], 0.0,
                                             logged[:, 0:tiles * 128], ALU.max, ALU.add).then_inc(z_made, 1)
                    dve.wait_ge(z_made, g + 1)
                    if reused(g):
                        dve.wait_ge(y_made, g - 1)
                    dve.tensor_tensor(flat(u[:, s, 0:tiles, :]), flat(z[:, s, 0:tiles, :]),
                                      flat(xa[:, k, 0:tiles, :]), ALU.add).then_inc(u_made, 1)
                    dve.wait_ge(u_made, g + 1)
                    norm_measure(norm, dve, u[:, s, 0:tiles, :], g, s, 128, tiles)

                def scale(g, k, r, tiles):
                    s = k % 2
                    if reused(g, 4):
                        dve.wait_ge(scattered[k], r * 16 * GT)
                    norm_invert(norm, dve, g, s, 128, tiles)
                    norm_scale(norm, dve, y[:, k, 0:tiles, :], u[:, s, 0:tiles, :], g, s, 128, tiles).then_inc(y_made, 1)
                edge_rings(dve, sh, (0, multiply), (1, product_up), (2, measure), (3, scale))


def program(nc, t, n, edge_tiles, pads):
    sh = shapes(n, edge_tiles, pads)
    with stage(nc) as (ctx, semaphore):
        c = constants(nc, ctx, semaphore, sh)
        w = load_weights(nc, ctx, semaphore, c, sh, t)
        pos_d = ctx.enter_context(nc.sbuf_tensor("pos_d", [128, sh["et"]], I32))
        pos_s = ctx.enter_context(nc.sbuf_tensor("pos_s", [128, sh["et"]], I32))
        gram = ctx.enter_context(nc.sbuf_tensor("gram", [128, 129], F32))
        sums = ctx.enter_context(nc.sbuf_tensor("sums", [128, 2], F32))
        bn = {"scale": ctx.enter_context(nc.sbuf_tensor("scale", [128, 1], F32)),
              "shift": ctx.enter_context(nc.sbuf_tensor("shift", [128, 1], F32)),
              "w1": ctx.enter_context(nc.sbuf_tensor("w1_scaled", [128, 128], F32)),
              "shift_m": ctx.enter_context(nc.sbuf_tensor("shift_m", [128, NT, 128], BF16))}
        sort_positions(nc, c, sh, "by_dst", t["dst_cols"], t["dst_flat"], pos_d, t["cnt"])
        with stage(nc) as (inner, inner_semaphore):
            run_stages(nc, sh, edge_rows_stage(nc, inner, inner_semaphore, c, sh, t, w, pos_d),
                       dense_stage(nc, inner, inner_semaphore, c, sh, "d0", t["x"], t["x1"], w["w0x"], w["b0_m"],
                                   c["ln_eps"], gram=(t["cnt"], gram)))
        o = sorted_order(nc, ctx, c, sh, "od", t["rows_d"], END)
        with stage(nc) as (inner, semaphore):
            ends_t = inner.enter_context(nc.sbuf_tensor("ends_t", [128, sh["ep"]], F32))
            scores = inner.enter_context(nc.sbuf_tensor("scores", [128, sh["ep"]], F32))
            layer0_ends(nc, c, sh, t, w, o, ends_t)
            spread_back(nc, c, sh, w, o, ends_t, scores)
            attention(nc, c, sh, t, w, o, ends_t, scores, sums)
            batch_norm(nc, c, sh, w, gram, sums, bn)
            with stage(nc) as (inner2, inner_semaphore):
                run_stages(nc, sh, node_stage=dense_stage(nc, inner2, inner_semaphore, c, sh, "d1", t["x1"], t["x2"],
                                                          bn["w1"], bn["shift_m"], c["ln_eps4"]))
            layer1_ends(nc, c, sh, t, o, scores, bn)
        compose(nc, ctx, c, w)
        with stage(nc) as (inner, inner_semaphore):
            run_stages(nc, sh, node_stage=last_dense_stage(nc, inner, inner_semaphore, c, sh, w, t["x2"], t["x3"], t["out"]))
        with stage(nc) as (inner, semaphore):
            sort_positions(nc, c, sh, "by_src", t["src_cols"], t["src_flat"], pos_s)
            build_pairs(nc, c, sh, t, pos_s)
            by_start = sorted_order(nc, inner, c, sh, "os", t["rows_s"], 0)
            layer2_ends(nc, c, sh, t, w, by_start)
        layer3_ends(nc, c, sh, t, w, o)


def kernel(**inputs):
    import numpy as _np
    import concourse.bacc as _bacc
    from concourse import mybir as _mybir
    from concourse.bass_utils import run_bass_kernel_spmd as _run

    nc = _bacc.Bacc("TRN2", target_bir_lowering=False, num_devices=1)
    a = {k: _np.asarray(v) for k, v in inputs.items()}
    n, e = a["x"].shape[0], a["dst"].shape[0]
    tiles = -(-e // 128)
    pad = tiles * 128 - e
    f32 = _mybir.dt.float32
    arrays, t = {}, {}

    def put(name, array):
        arrays[name] = _np.ascontiguousarray(array)
        t[name] = nc.dram_tensor(name, arrays[name].shape, _mybir.dt.from_np(arrays[name].dtype),
                                 kind="ExternalInput").ap()

    beyond = n // 128 * 128 + 127
    for name in ("dst", "src"):
        flat_ = _np.concatenate([a[name], _np.full((pad,), beyond, a[name].dtype)])
        put(name + "_flat", flat_)
        put(name + "_cols", flat_.reshape(tiles, 128).T)
    weight = _np.concatenate([a["edge_weight"], _np.zeros((pad,), a["edge_weight"].dtype)])
    put("weight_flat", weight)
    put("weight_cols", weight.reshape(tiles, 128).T)
    put("edge_attr", _np.concatenate([a["edge_attr_128"], _np.zeros((pad, 128), a["edge_attr_128"].dtype)]))
    put("x", a["x"])
    w0, wl, we = a["L0_gnn_W"].T, a["L2_gnn_W_lin"].T, a["L2_gnn_W_edge"].T
    squares = {"w0x": w0[0:128], "w0s": w0[128:256], "w0e": w0[256:384], "w1": a["L1_gnn_W"],
               "w2n": a["L2_gnn_W_neigh"], "w2n_t": a["L2_gnn_W_neigh"].T, "w2e_a": we[0:128], "w2e_b": we[128:256],
               "w2l_a": wl[0:128], "w2l_b": wl[128:256],
               "l3w1": a["L3_gnn_W1"], "l3w2": a["L3_gnn_W2"], "l3w3": a["L3_gnn_W3"]}
    vectors = {"b0": "L0_gnn_b", "b2n": "L2_gnn_b_neigh", "b2e": "L2_gnn_b_edge", "b2l": "L2_gnn_b_lin",
               "l3b1": "L3_gnn_b1", "l3b2": "L3_gnn_b2", "l3b3": "L3_gnn_b3", "bias1": "L1_gnn_bias",
               "gamma": "L1_gnn_bn_gamma", "beta": "L1_gnn_bn_beta"}
    for name, array in squares.items():
        put(name, array)
    for name, key in vectors.items():
        put(name, a[key])
    put("att_s", a["L1_gnn_att_src"].reshape(128))
    put("att_d", a["L1_gnn_att_dst"].reshape(128))
    put("neg_mu", -_np.linspace(0.0, 1.0, 128, dtype=_np.float32))
    sh = shapes(n, tiles, pad)

    def scratch(name, shape, kind="Internal"):
        t[name] = nc.dram_tensor(name, shape, f32, kind=kind).ap()

    scratch("out", [n, 128], "ExternalOutput")
    for name in ("x1", "x2", "x3"):
        scratch(name, [n, 128])
    scratch("x1_ends", [sh["ep"], 128])
    scratch("cnt", [sh["hc"] * 128 * 128])
    scratch("rows_d", [sh["ep"] + 2, ROW])
    scratch("rows_s", [sh["ep"] + 2, 2])
    program(nc, t, n, tiles, pad)
    r = _run(nc, [arrays], core_ids=[0])
    return r.results[0]["out"]
```

```python
from contextlib import ExitStack, contextmanager

import concourse.bass as bass
from concourse import mybir

F32 = mybir.dt.float32
BF16 = mybir.dt.bfloat16
I32 = mybir.dt.int32
ALU = mybir.AluOpType
ACT = mybir.ActivationFunctionType
AX = mybir.AxisListType

D = 128
NT = 4
ROWS = 128 * NT
GT = 4
GE = 128 * GT
LN_EPS = 1e-5
BN_EPS = 1e-5
SLOPE = 0.2
SOFTMAX_EPS = 1e-16
NEG = -3.0e38
LOADS = 8
PER_STEP = 4
SKIP = float(1 << 20)


def shapes(n, edge_tiles, pads):
    full = n // ROWS
    rest = n - full * ROWS
    tail_t = next((t for t in range(1, NT + 1) if rest % t == 0 and rest // t <= 128), 0) if rest else 0
    hi = n // 128 + 1
    return {
        "n": n,
        "pads": pads,
        "et": edge_tiles,
        "ep": edge_tiles * 128,
        "hi": hi,
        "hc": -(-hi // 128),
        "full": full,
        "tail_t": tail_t,
        "tail_p": rest // tail_t if rest else 0,
        "eg": edge_tiles // GT,
        "tail_e": edge_tiles % GT,
    }


@contextmanager
def stage(nc):
    used = []

    def semaphore(name):
        used.append(nc.alloc_semaphore(name))
        return used[-1]

    with ExitStack() as ctx:
        yield ctx, semaphore
        if used:
            nc.clear_and_free_semaphores(used)
            nc.all_engine_barrier()


def rounds(engine, full, slots, body, tail=None):
    whole = full // slots
    if whole:
        with engine.Fori(0, whole) as r:
            for s in range(slots):
                body(r * slots + s, s, r)
    for g in range(whole * slots, full):
        body(g, g % slots, g // slots)
    if tail is not None:
        tail(full, full % slots, full // slots)


def staggered(engine, full, tail, slots, parts, warm=None):
    groups = full + (1 if tail else 0)
    most = max(lag for lag, *_ in parts)
    start = most + (warm or slots)
    turns = max((full - start) // slots, 0)

    def step(k, r=0):
        for lag, body, size, tail_size in parts:
            g = k - lag
            if 0 <= g < groups:
                whole = g < full
                body(g + r * slots, g % slots, g // slots + r, size if whole else tail_size)

    for k in range(start):
        step(k)
    if turns:
        with engine.Fori(0, turns) as r:
            for k in range(start, start + slots):
                step(k, r)
    for k in range(start + turns * slots, groups + most):
        step(k)


def reused(g, slots=2):
    return not isinstance(g, int) or g >= slots


def edge_groups(engine, sh, *parts, slots=2):
    staggered(engine, sh["eg"], sh["tail_e"] > 0, slots, [(lag, body, GT, sh["tail_e"]) for lag, body in parts])


def edge_rings(engine, sh, *parts):
    edge_groups(engine, sh, *parts, slots=4)


def both_groups(engine, sh, edge_parts, node_parts):
    edges, nodes = sh["eg"] + (sh["tail_e"] > 0), sh["full"] + (sh["tail_t"] > 0)
    edge_most = max([lag for lag, *_ in edge_parts], default=0)
    node_most = max([lag for lag, _ in node_parts], default=0)
    turn = 4 if edge_parts else LOADS // PER_STEP

    def step(k, r=0):
        for i in range(PER_STEP):
            for lag, body, before in edge_parts:
                g = k - lag
                if before == i and 0 <= g < edges:
                    body(g + r * turn, g % 4, g // 4 + r * (turn // 4), GT if g < sh["eg"] else sh["tail_e"])
            for lag, body in node_parts:
                g = k * PER_STEP + i - lag
                if 0 <= g < nodes:
                    body(g + r * (turn * PER_STEP), g % LOADS, g // LOADS + r * (turn * PER_STEP // LOADS),
                         (128, NT) if g < sh["full"] else (sh["tail_p"], sh["tail_t"]))

    steps, first, whole = 0, 0, []
    if edge_parts:
        steps, first = edges + edge_most, edge_most + 4
        whole.append(sh["eg"])
    if node_parts:
        steps = max(steps, -(-(nodes + node_most) // PER_STEP))
        first = max(first, -(-(node_most + LOADS) // PER_STEP))
        whole.append(sh["full"] // PER_STEP)
    turns = max((min(whole, default=0) - first) // turn, 0)
    for k in range(min(first, steps)):
        step(k)
    if turns:
        with engine.Fori(0, turns) as r:
            for k in range(first, first + turn):
                step(k, r)
    for k in range(first + turns * turn, steps):
        step(k)


def run_stages(nc, sh, edge_stage=None, node_stage=None):
    with nc.Block() as block:
        def drive(engine, name):
            programs = [stage_[name](engine) if stage_ and name in stage_ else ([], None)
                        for stage_ in (edge_stage, node_stage)]
            (edge_parts, edge_end), (node_parts, node_end) = programs
            both_groups(engine, sh, edge_parts, node_parts)
            if edge_end:
                edge_end()
            if node_end:
                node_end()

        @block.sync
        def _(sp):
            drive(sp, "sync")

        @block.tensor
        def _(pe):
            drive(pe, "tensor")

        @block.scalar
        def _(act):
            drive(act, "scalar")

        @block.vector
        def _(dve):
            drive(dve, "vector")

        @block.gpsimd
        def _(pool):
            drive(pool, "gpsimd")


def row_numbers(pool, ring, k, tiles, numbers, g, made):
    pool.tensor_copy(ring[:, k, 0:tiles], numbers[:, bass.ds(g * GT, tiles)]).then_inc(made, 1)


def node_rows(table, g, size):
    p, t = size
    return table[bass.ds(g * ROWS, p * t), :].rearrange("(p r) f -> p r f", r=t)


def edge_rows(table, g, tiles, first=0, columns=slice(None)):
    return table[bass.ds(g * GE + first, tiles * 128), columns].rearrange("(t p) f -> p t f", p=128)


def constants(nc, ctx, semaphore, sh):
    c = {}

    def sb(name, shape, dt):
        c[name] = ctx.enter_context(nc.sbuf_tensor(name, shape, dt))
        return c[name]

    width = max(sh["hi"], 129)
    sb("iota_i", [128, width], I32)
    sb("part_i", [128, 1], I32)
    sb("iota", [128, width], F32)
    sb("part", [128, 1], F32)
    sb("ident", [128, 128], F32)
    sb("identb", [128, 128], BF16)
    sb("before", [128, 128], F32)
    sb("above", [128, 128], F32)
    sb("onesb", [128, 128], BF16)
    sb("ones", [128, 128], F32)
    sb("zerosb", [128, width], BF16)
    sb("ln_eps", [128, 1], F32)
    sb("ln_eps4", [128, 1], F32)
    iota_made = semaphore("iota_made")
    iota_cast = semaphore("iota_cast")
    with nc.Block() as block:
        @block.gpsimd
        def _(pool):
            pool.iota(c["iota_i"][:, :], pattern=[[1, width]], base=0, channel_multiplier=0).then_inc(iota_made, 1)
            pool.iota(c["part_i"][:, :], pattern=[[0, 1]], base=0, channel_multiplier=1).then_inc(iota_made, 1)

        @block.vector
        def _(dve):
            dve.wait_ge(iota_made, 2)
            dve.tensor_copy(c["iota"][:, :], c["iota_i"][:, :]).then_inc(iota_cast, 1)
            dve.tensor_copy(c["part"][:, :], c["part_i"][:, :]).then_inc(iota_cast, 1)
            dve.memset(c["onesb"][:, :], 1.0)
            dve.memset(c["ones"][:, :], 1.0)
            dve.memset(c["zerosb"][:, :], 0.0)
            dve.memset(c["ln_eps"][:, :], LN_EPS)
            dve.memset(c["ln_eps4"][:, :], LN_EPS / 4)
            dve.wait_ge(iota_cast, 2)
            row, col = c["iota"][:, 0:128], c["part"][:, 0:1]
            dve.tensor_scalar(c["ident"][:, :], row, col, None, ALU.is_equal)
            dve.tensor_scalar(c["identb"][:, :], row, col, None, ALU.is_equal)
            dve.tensor_scalar(c["before"][:, :], row, col, None, ALU.is_lt)
            dve.tensor_scalar(c["above"][:, :], row, col, None, ALU.is_gt)
    return c


def sort_positions(nc, c, sh, keys):
    with stage(nc) as (ctx, semaphore):
        hi, et = sh["hi"], sh["et"]
        sorts = []
        for q, (tag, cols, row, pos, count_table) in enumerate(keys):
            def sb(name, shape, dt=F32):
                return ctx.enter_context(nc.sbuf_tensor(f"{tag}_{name}", shape, dt))

            def ps(name):
                return ctx.enter_context(nc.psum_tensor(f"{tag}_{name}", [128, 512], F32))

            b = {"cols": cols, "row": row, "pos": pos, "count_table": count_table}
            for name in ("key_i", "low_i", "high_i"):
                b[name] = sb(name, [128, et], I32)
            for name in ("key", "low", "high", "from_table", "in_tile"):
                b[name] = sb(name, [128, et])
            b["hot_low"] = sb("hot_low", [128, et * 128], BF16)
            b["hot_high"] = sb("hot_high", [128, 2 * GT * hi], BF16)
            b["count"] = sb("count", [128, sh["hc"] * 128])
            b["running"], b["first"], b["before_row"] = sb("running", [128, hi]), sb("first", [128, hi]), sb("before_row", [128, 1])
            b["key_row"], b["low_row"] = sb("key_row", [128, 2, GE], I32), sb("low_row", [128, 2, GE], I32)
            b["hot_row"], b["equal"] = sb("hot_row", [128, 2, GE]), sb("equal", [128, GE])
            b["at_tile"], b["picked"] = sb("at_tile", [128, 2, hi]), sb("picked", [128, 2, hi])
            if count_table is not None:
                b["count_t"] = sb("count_t", [128, sh["hc"], 128])
            b["hist"], b["found"] = ps("hist"), [ps("found0"), ps("found1")]
            for name in ("keys_in", "split", "parts_cast", "hot_made", "counted", "count_out", "scanned", "prefixed",
                         "prefix_out", "first_made", "row_in0", "row_in1", "row_free", "row_low", "row_hot", "again",
                         "table_updated", "table_out", "looked_up", "found_free", "turned_done", "turned_out",
                         "count_stored", "zeroed", "summed"):
                b[name] = semaphore(f"{tag}_{name}")
            b["row_in"] = [b["row_in0"], b["row_in1"]]
            sorts.append(b)
        turned = ctx.enter_context(nc.psum_tensor("sort_turned", [128, 512], F32))
        prefix = ctx.enter_context(nc.psum_tensor("sort_prefix", [128, 512], F32))

        def lows(b, t):
            return b["hot_low"][:, bass.ds(t * 128, 128)]

        def highs(b, slot):
            return b["hot_high"][:, slot * hi:(slot + 1) * hi]

        with nc.Block() as block:
            @block.sync
            def _(sp):
                for b in sorts:
                    sp.dma_start(b["key_i"][:, :], b["cols"]).then_inc(b["keys_in"], 16)

                def load(g, s, r, tiles):
                    w = tiles * 128
                    for b in sorts:
                        sp.wait_ge(b["row_free"], g + 1)
                        sp.dma_start(b["key_row"][:, s, 0:w],
                                     b["row"][bass.ds(g * GE, w)].rearrange("(a n) -> a n", a=1)
                                     .to_broadcast([128, w])).then_inc(b["row_in"][s], 16)
                edge_groups(sp, sh, (0, load))
                for b in sorts:
                    if b["count_table"] is not None:
                        sp.wait_ge(b["turned_out"], 1)
                        sp.dma_start(b["count_table"].rearrange("(c h l) -> h c l", h=128, l=128), b["count_t"][:, :, :]) \
                            .then_inc(b["count_stored"], 16)
                        sp.wait_ge(b["count_stored"], 16)

            @block.tensor
            def _(pe):
                for b in sorts:
                    pe.matmul(b["hist"][:, 0:hi], c["zerosb"][:, 0:128], c["zerosb"][:, 0:hi], start=True, stop=True,
                              skip_group_check=True)

                def add(t, s, r):
                    for b in sorts:
                        pe.wait_ge(b["hot_made"], t + 1)
                        pe.matmul(b["hist"][:, 0:hi], lows(b, t), highs(b, s), start=False, stop=True,
                                  skip_group_check=True).then_inc(b["counted"], 1)
                rounds(pe, et, 2, add)
                for q, b in enumerate(sorts):
                    pe.wait_ge(b["scanned"], 1)
                    pe.matmul(prefix[:, q:q + 1], c["above"][:, :], b["running"][:, hi - 1:hi], start=True, stop=True) \
                        .then_inc(b["prefixed"], 1)
                    pe.wait_ge(b["prefix_out"], 1)
                for b in sorts:
                    if b["count_table"] is not None:
                        pe.wait_ge(b["count_out"], 1)
                        for k in range(sh["hc"]):
                            last = pe.transpose(turned[:, k * 128:(k + 1) * 128], b["count"][:, k * 128:(k + 1) * 128],
                                                c["ident"][:, :])
                        last.then_inc(b["turned_done"], 1)
                    pe.wait_ge(b["first_made"], 1)
                    pe.matmul(b["hist"][:, 0:hi], c["ident"][:, :], b["first"][:, :], start=True, stop=True,
                              skip_group_check=True).then_inc(b["table_updated"], 1)

                def look_up(g, s, r, tiles):
                    for j in range(tiles):
                        t = g * GT + j
                        for b in sorts:
                            if j == 0:
                                pe.wait_ge(b["row_hot"], g + 1)
                                pe.wait_ge(b["again"], g + 1)
                            pe.wait_ge(b["table_out"], t + 1)
                            pe.matmul(b["hist"][:, 0:hi], lows(b, t), highs(b, s * GT + j), start=False, stop=True,
                                      skip_group_check=True).then_inc(b["table_updated"], 1)
                            pe.wait_ge(b["found_free"], t + 1)
                            pe.matmul(b["found"][j % 2][:, 0:hi], b["hot_row"][:, s, j * 128:(j + 1) * 128],
                                      b["at_tile"][:, j % 2, :], start=True, stop=True).then_inc(b["looked_up"], 1)
                edge_groups(pe, sh, (0, look_up))

            @block.scalar
            def _(act):
                for b in sorts:
                    act.wait_ge(b["counted"], et)
                    act.wait_ge(b["zeroed"], 1)
                    act.activation(b["count"][:, 0:hi], b["hist"][:, 0:hi], ACT.Copy).then_inc(b["count_out"], 1)
                for q, b in enumerate(sorts):
                    act.wait_ge(b["prefixed"], 1)
                    act.activation(b["before_row"][:, :], prefix[:, q:q + 1], ACT.Copy, bias=1.0) \
                        .then_inc(b["prefix_out"], 1)
                for b in sorts:
                    if b["count_table"] is not None:
                        act.wait_ge(b["turned_done"], 1)
                        act.activation(flat(b["count_t"][:, :, :]), turned[:, 0:sh["hc"] * 128], ACT.Copy) \
                            .then_inc(b["turned_out"], 1)

                def take(t, s, r):
                    for b in sorts:
                        act.wait_ge(b["table_updated"], t + 1)
                        if not isinstance(t, int) or t >= 2:
                            act.wait_ge(b["looked_up"], t - 1)
                        act.activation(b["at_tile"][:, s, :], b["hist"][:, 0:hi], ACT.Copy).then_inc(b["table_out"], 1)
                take(0, 0, 0)
                take(1, 1, 0)
                rounds(act, et - 2, 2, lambda t, s, r: take(t + 2, s, r))

            @block.vector
            def _(dve):
                for b in sorts:
                    dve.sem_inc(b["row_free"], 2)
                    dve.sem_inc(b["found_free"], 2)
                    dve.memset(b["count"][:, :], 0.0).then_inc(b["zeroed"], 1)
                    dve.wait_ge(b["keys_in"], 16)
                    dve.tensor_copy(b["key"][:, :], b["key_i"][:, :]).then_inc(b["split"], 1)
                    dve.tensor_scalar(b["low_i"][:, :], b["key_i"][:, :], 127, None, ALU.bitwise_and).then_inc(b["split"], 1)
                    dve.tensor_scalar(b["high_i"][:, :], b["key_i"][:, :], 7, None, ALU.arith_shift_right) \
                        .then_inc(b["split"], 1)
                for b in sorts:
                    dve.wait_ge(b["split"], 3)
                    dve.tensor_copy(b["low"][:, :], b["low_i"][:, :]).then_inc(b["parts_cast"], 1)
                    dve.tensor_copy(b["high"][:, :], b["high_i"][:, :]).then_inc(b["parts_cast"], 1)
                for b in sorts:
                    dve.wait_ge(b["parts_cast"], 2)

                def make(t, s, r):
                    for b in sorts:
                        if reused(t, 2):
                            dve.wait_ge(b["counted"], t - 1)
                        dve.tensor_scalar(lows(b, t), c["iota"][:, 0:128], b["low"][:, bass.ds(t, 1)], None, ALU.is_equal)
                        dve.tensor_scalar(highs(b, s), c["iota"][:, 0:hi], b["high"][:, bass.ds(t, 1)], None,
                                          ALU.is_equal).then_inc(b["hot_made"], 1)
                make(0, 0, 0)
                make(1, 1, 0)
                rounds(dve, et - 2, 2, lambda t, s, r: make(t + 2, s, r))
                for b in sorts:
                    dve.wait_ge(b["count_out"], 1)
                    dve.tensor_tensor_scan(b["running"][:, :], c["ones"][:, 0:1].to_broadcast([128, hi]),
                                           b["count"][:, 0:hi], 0.0, ALU.mult, ALU.add).then_inc(b["scanned"], 1)
                for b in sorts:
                    dve.wait_ge(b["prefix_out"], 1)
                    dve.wait_ge(b["scanned"], 1)
                    dve.scalar_tensor_tensor(b["first"][:, :], b["running"][:, :], b["before_row"][:, 0:1],
                                             b["count"][:, 0:hi], ALU.add, ALU.subtract).then_inc(b["first_made"], 1)

                def compare(g, s, r, tiles):
                    w = tiles * 128
                    for b in sorts:
                        dve.wait_ge(b["row_in"][s], r * 16 + 16)
                        dve.tensor_scalar(b["low_row"][:, s, 0:w], b["key_row"][:, s, 0:w], 127, None, ALU.bitwise_and) \
                            .then_inc(b["row_low"], 1)
                    for b in sorts:
                        dve.wait_ge(b["row_low"], g + 1)
                        if reused(g):
                            dve.wait_ge(b["looked_up"], (g - 1) * GT)
                        dve.tensor_scalar(b["hot_row"][:, s, 0:w], b["low_row"][:, s, 0:w], c["part"][:, 0:1], None,
                                          ALU.is_equal).then_inc(b["row_hot"], 1)
                        dve.wait_ge(b["row_free"], g + 2)
                        if reused(g):
                            dve.wait_ge(b["found_free"], (g - 1) * GT + 2)
                            dve.wait_ge(b["table_updated"], (g - 1) * GT + 1)
                        for j in range(tiles):
                            again = dve.tensor_scalar(highs(b, s * GT + j), c["iota"][:, 0:hi],
                                                      b["high"][:, bass.ds(g * GT + j, 1)], None, ALU.is_equal)
                        again.then_inc(b["again"], 1)
                        for j in range(tiles):
                            t = g * GT + j
                            last = dve.scalar_tensor_tensor(
                                b["equal"][:, j * 128:(j + 1) * 128], b["key_row"][:, s, j * 128:(j + 1) * 128],
                                b["key"][:, bass.ds(t, 1)], c["before"][:, :], ALU.is_equal, ALU.mult,
                                accum_out=b["in_tile"][:, bass.ds(t, 1)])
                        last.then_inc(b["row_free"], 1)

                def pick(g, s, r, tiles):
                    for j in range(tiles):
                        t = g * GT + j
                        for b in sorts:
                            dve.wait_ge(b["looked_up"], t + 1)
                            dve.wait_ge(b["found_free"], t + 1)
                            dve.wait_ge(b["again"], g + 1)
                            dve.scalar_tensor_tensor(
                                b["picked"][:, j % 2, :], b["found"][j % 2][:, 0:hi], 1.0, highs(b, s * GT + j),
                                ALU.mult, ALU.mult, accum_out=b["from_table"][:, bass.ds(t, 1)]) \
                                .then_inc(b["found_free"], 1)
                for b in sorts:
                    dve.wait_ge(b["counted"], et)
                edge_groups(dve, sh, (0, compare), (1, pick))
                for b in sorts:
                    dve.wait_ge(b["found_free"], et + 2)
                    dve.wait_ge(b["row_free"], sh["eg"] + (1 if sh["tail_e"] else 0) + 2)
                    dve.tensor_tensor(b["pos"][:, :], b["from_table"][:, :], b["in_tile"][:, :], ALU.add) \
                        .then_inc(b["summed"], 1)
                for b in sorts:
                    dve.wait_ge(b["summed"], 1)


ROW = 388
END = 384


def flat(tile):
    return tile.rearrange("p a b -> p (a b)")


def load_weights(nc, ctx, semaphore, c, sh, t):
    w = {}

    def sb(name, shape, dt=F32):
        w[name] = ctx.enter_context(nc.sbuf_tensor("w_" + name, shape, dt))
        return w[name]

    def sem(name):
        return semaphore("w_" + name)

    squares = ["w0x", "w0s", "w0e", "w1", "w2n", "w2n_t", "w2e_a", "w2e_b", "w2l_a", "w2l_b", "l3w1", "l3w2", "l3w3"]
    columns = ["b2n", "b2e", "l3b1", "bias1", "gamma", "beta", "neg_mu"]
    rows = ["b0", "b2l", "l3b2", "l3b3", "att_s", "att_d"]
    for name in squares:
        sb(name, [128, 128])
    for name in columns:
        sb(name, [128, 1])
    for name in rows:
        sb(name, [128, 128])
    for name in ("b0", "b2l", "l3b2", "l3b3"):
        sb(name + "_m", [128, NT, 128], BF16)
    sb("ws", [128, 128])
    sb("wd", [128, 128])
    sb("wsd", [128, 128])
    sb("w2n_neg", [128, 128])
    sb("part_hi", [128, 128], BF16)
    sb("part_mid", [128, 128], BF16)
    sb("part_lo", [128, 128], BF16)
    sb("rest1", [128, 128])
    sb("rest2", [128, 128])
    sb("weighted", [128, 128])
    sb("per_head", [128, 8])
    loaded, linked = sem("loaded"), sem("linked")
    loads = len(squares) + len(columns) + len(rows)
    with nc.Block() as block:
        @block.sync
        def _(sp):
            for name in squares:
                sp.dma_start(w[name][:, :], t[name]).then_inc(loaded, 16)
            for name in columns:
                sp.dma_start(w[name][:, :], t[name].rearrange("(p a) -> p a", a=1)).then_inc(loaded, 16)
            for name in rows:
                sp.dma_start(w[name][:, :], t[name].rearrange("(a n) -> a n", a=1).to_broadcast([128, 128])) \
                    .then_inc(loaded, 16)

        @block.vector
        def _(dve):
            dve.wait_ge(loaded, 16 * loads)
            done = [0]

            def link(instruction):
                instruction.then_inc(linked, 1)
                done[0] += 1
                dve.wait_ge(linked, done[0])

            for name in ("b0", "b2l", "l3b2", "l3b3"):
                bias_parts(dve, link, w, w[name], w[name + "_m"])
            for att, out in (("att_s", "ws"), ("att_d", "wd")):
                link(dve.tensor_tensor(w["weighted"][:, :], w["w1"][:, :], w[att][:, :], ALU.mult))
                link(dve.tensor_reduce(w["per_head"][:, :], w["weighted"][:, :].rearrange("p (h f) -> p h f", h=8),
                                       AX.X, ALU.add))
                link(dve.tensor_copy(w[out][:, :].rearrange("p (h f) -> p h f", h=8),
                                     w["per_head"][:, :].rearrange("p (h a) -> p h a", a=1).to_broadcast([128, 8, 16])))
            link(dve.tensor_tensor(w["wsd"][:, :], w["ws"][:, :], w["wd"][:, :], ALU.add))
            link(dve.tensor_scalar(w["w2n_neg"][:, :], w["w2n_t"][:, :], -1.0, None, ALU.mult))
    return w


def bias_parts(dve, link, w, row, parts):
    link(dve.tensor_copy(w["part_hi"][:, :], row[:, :]))
    link(dve.tensor_tensor(w["rest1"][:, :], row[:, :], w["part_hi"][:, :], ALU.subtract))
    link(dve.tensor_copy(w["part_mid"][:, :], w["rest1"][:, :]))
    link(dve.tensor_tensor(w["rest2"][:, :], w["rest1"][:, :], w["part_mid"][:, :], ALU.subtract))
    link(dve.tensor_copy(w["part_lo"][:, :], w["rest2"][:, :]))
    link(dve.memset(flat(parts[:, :, :]), 0.0))
    for k, part in enumerate(("part_hi", "part_mid", "part_lo")):
        at = slice(32 * k, 32 * k + 32)
        for j in range(NT):
            last = dve.tensor_scalar(parts[at, j, :], w[part][at, :], 1.0 / 32, None, ALU.mult)
    link(last)


def norm_buffers(nc, ctx, semaphore, tag, eps, slots=2):
    def sb(name, shape):
        return ctx.enter_context(nc.sbuf_tensor(f"{tag}_{name}", shape, F32))

    nm = {"eps": eps, "stats": sb("stats", [128, slots, NT, 6]), "moments": sb("moments", [128, slots, NT, 2]),
          "dev": sb("dev", [128, slots, NT]), "inv": sb("inv", [128, slots, NT])}
    for name in ("stats_made", "moments_made", "dev_made", "inv_made", "carried"):
        nm[name] = semaphore(f"{tag}_{name}")
    return nm


def norm_measure(nm, dve, rows, g, s, p, t):
    norm_stats(nm, dve, rows, s, p, t)
    norm_moments(nm, dve, g, s, p, t)


def norm_stats(nm, dve, rows, s, p, t):
    for j in range(t):
        last = dve.bn_stats(nm["stats"][0:p, s, j, :], rows[:, j, :])
    last.then_inc(nm["stats_made"], 1)


def norm_moments(nm, dve, g, s, p, t):
    dve.wait_ge(nm["stats_made"], g + 1)
    dve.sem_inc(nm["carried"], 1)
    for j in range(t):
        last = dve.bn_aggr(nm["moments"][0:p, s, j, :], nm["stats"][0:p, s, j, :])
    last.then_inc(nm["moments_made"], 1)


def norm_deviation(nm, act, g, s, p, t):
    act.wait_ge(nm["moments_made"], g + 1)
    act.activation(nm["dev"][0:p, s, 0:t], nm["moments"][0:p, s, 0:t, 1], ACT.Sqrt,
                   bias=nm["eps"][0:p, :]).then_inc(nm["dev_made"], 1)


def norm_invert(nm, dve, g, s, p, t):
    dve.wait_ge(nm["dev_made"], g + 1)
    dve.reciprocal(nm["inv"][0:p, s, 0:t], nm["dev"][0:p, s, 0:t]).then_inc(nm["inv_made"], 1)


def norm_scale(nm, dve, out, rows, g, s, p, t):
    dve.wait_ge(nm["inv_made"], g + 1)
    for j in range(t):
        last = dve.tensor_scalar(out[:, j, :], rows[:, j, :], nm["moments"][0:p, s, j, 0:1],
                                 nm["inv"][0:p, s, j:j + 1], ALU.subtract, ALU.mult)
    return last


def edge_rows_stage(nc, ctx, semaphore, c, sh, t, w, pos, pos_s):
    def sb(name, shape, dt=F32):
        return ctx.enter_context(nc.sbuf_tensor("p_" + name, shape, dt))

    def ps(name):
        return ctx.enter_context(nc.psum_tensor("p_" + name, [128, 512], F32))

    def sem(name):
        return semaphore("p_" + name)

    ends_i = sb("ends_i", [128, 2, sh["et"]], I32)
    ends = sb("ends", [128, sh["et"], 2])
    own_i = sb("own_i", [128, sh["et"]], I32)
    other_i = sb("other_i", [128, sh["et"]], I32)
    dist = sb("dist", [128, sh["et"]])
    ramp = sb("ramp", [128, sh["et"]])
    ramp01 = sb("ramp01", [128, sh["et"]])
    cosine = sb("cosine", [128, sh["et"]])
    halved = sb("halved", [128, sh["et"]])
    cut = sb("cut", [128, sh["et"]])
    half_pi = sb("half_pi", [128, 1])
    half = sb("half", [128, 1])
    pad_row = sb("pad_row", [1, ROW])
    own_at, other_at, put_at, pair_at = (sb(k, [128, 4, GT], I32) for k in ("own_at", "other_at", "put_at", "pair_at"))
    pairs, pair = sb("pairs", [128, sh["et"], 2]), sb("pair", [128, 4, GT, 2])
    xs = sb("xs", [128, 4, GT, 128])
    xs_t, ea_t = sb("xs_t", [128, 2, GE]), sb("ea_t", [128, 2, GE])
    ea = sb("ea", [128, 4, GT, 128])
    dist_row = sb("dist_row", [128, 4, GE])
    radial = sb("radial", [128, 2, GE])
    soft1, soft2 = sb("soft1", [128, 2, GE]), sb("soft2", [128, 2, GE])
    hidden = sb("hidden", [128, 2, GE])
    filt = sb("filt", [128, 2, GT, 128])
    row = sb("row", [128, 4, GT, ROW])
    turned_x, turned_e, message = ps("turned_x"), ps("turned_e"), ps("message")
    act1, act2 = ps("act1"), ps("act2")

    ends_in, linked, setup, cos_made, pads_stored = (
        sem(k) for k in ("ends_in", "linked", "setup", "cos_made", "pads_stored"))
    numbers_ready, at_made, put_made, pair_made, issuing = (
        sem(k) for k in ("numbers_ready", "at_made", "put_made", "pair_made", "issuing"))
    gathered, ea_in, dist_in, stored, paired = (
        [sem(f"{name}{k}") for k in range(4)] for name in ("gathered", "ea_in", "dist_in", "stored", "paired"))
    x_turned, x_t_out, message_made, message_out, squared, radial_made = (
        sem(k) for k in ("x_turned", "x_t_out", "message_made", "message_out", "squared", "radial_made"))
    act1_made, abs1, exp1, log1, pos1, hidden_made, act2_made, abs2, exp2, log2, filt_made, row_made = (
        sem(k) for k in ("act1_made", "abs1", "exp1", "log1", "pos1", "hidden_made", "act2_made", "abs2", "exp2",
                         "log2", "filt_made", "row_made"))

    def sync(sp):
        sp.dma_start(ends_i[:, 0, :], t["dst_cols"]).then_inc(ends_in, 16)
        sp.dma_start(ends_i[:, 1, :], t["src_cols"]).then_inc(ends_in, 16)
        sp.dma_start(dist[:, :], t["weight_cols"]).then_inc(ends_in, 16)
        sp.wait_ge(setup, 1)
        sp.dma_start(t["rows_d"][0:1, :], pad_row[:, :]).then_inc(pads_stored, 16)
        sp.dma_start(t["rows_d"][sh["ep"] + 1:sh["ep"] + 2, :], pad_row[:, :]).then_inc(pads_stored, 16)
        sp.dma_start(t["rows_s"][0:1, :], pad_row[:, 0:2]).then_inc(pads_stored, 16)
        sp.dma_start(t["rows_s"][sh["ep"] + 1:sh["ep"] + 2, :], pad_row[:, 0:2]).then_inc(pads_stored, 16)

        def load_distances(g, k, r, tiles):
            n = tiles * 128
            if reused(g, 4):
                sp.wait_ge(squared, g - 3)
            sp.dma_start(dist_row[:, k, 0:n],
                         t["weight_flat"][bass.ds(g * GE, n)].rearrange("(a n) -> a n", a=1)
                         .to_broadcast([128, n])).then_inc(dist_in[k], 16)

        def load_attributes(g, k, r, tiles):
            if reused(g, 4):
                sp.wait_ge(x_turned, g - 3)
                sp.wait_ge(row_made, g - 3)
            sp.dma_start(ea[:, k, 0:tiles, :], edge_rows(t["edge_attr"], g, tiles)).then_inc(ea_in[k], 16)
        return [(0, load_distances, 0), (1, load_attributes, 0)], lambda: sp.wait_ge(pads_stored, 64)

    def gpsimd(pool):
        last_node = pool.to_reg(sh["n"] - 1)
        last_row = pool.to_reg(sh["ep"] + 1)
        pool.wait_ge(numbers_ready, 1)

        def gather(g, k, r, tiles):
            if reused(g, 4):
                pool.wait_ge(gathered[k], r * 32 * GT)
            pool.tensor_copy(own_at[:, k, 0:tiles], own_i[:, bass.ds(g * GT, tiles)]).then_inc(at_made, 1)
            pool.tensor_copy(other_at[:, k, 0:tiles], other_i[:, bass.ds(g * GT, tiles)]).then_inc(at_made, 1)
            pool.wait_ge(at_made, 2 * g + 2)
            if reused(g, 4):
                pool.wait_ge(stored[k], r * 16 * GT)
                pool.wait_ge(x_turned, g - 3)
            pool.sem_inc(issuing, 1)
            for j in range(tiles):
                pool.indirect_dma_start(
                    out=xs[:, k, j, :], out_offset=None, in_=t["x"],
                    in_offset=bass.IndirectOffsetOnAxis(ap=other_at[:, k, j:j + 1], axis=0),
                    bounds_check=last_node, oob_is_err=False).then_inc(gathered[k], 16)
                pool.indirect_dma_start(
                    out=row[:, k, j, 128:256], out_offset=None, in_=t["x"],
                    in_offset=bass.IndirectOffsetOnAxis(ap=own_at[:, k, j:j + 1], axis=0),
                    bounds_check=last_node, oob_is_err=False).then_inc(gathered[k], 16)

        def scatter(g, k, r, tiles):
            if reused(g, 4):
                pool.wait_ge(stored[k], r * 16 * GT)
            pool.tensor_copy(put_at[:, k, 0:tiles], pos[:, bass.ds(g * GT, tiles)]).then_inc(put_made, 1)
            pool.wait_ge(put_made, g + 1)
            pool.wait_ge(row_made, g + 1)
            pool.wait_ge(message_out, g + 1)
            pool.wait_ge(gathered[k], r * 32 * GT + 32 * tiles)
            pool.sem_inc(issuing, 1)
            for j in range(tiles):
                pool.indirect_dma_start(
                    out=t["rows_d"], out_offset=bass.IndirectOffsetOnAxis(ap=put_at[:, k, j:j + 1], axis=0),
                    in_=row[:, k, j, :], in_offset=None,
                    bounds_check=last_row, oob_is_err=False).then_inc(stored[k], 16)

        def put_pairs(g, k, r, tiles):
            if reused(g, 4):
                pool.wait_ge(paired[k], r * 16 * GT)
            pool.tensor_copy(pair_at[:, k, 0:tiles], pos_s[:, bass.ds(g * GT, tiles)]).then_inc(pair_made, 1)
            pool.tensor_copy(pair[:, k, 0:tiles, :], pairs[:, bass.ds(g * GT, tiles), :]).then_inc(pair_made, 1)
            pool.wait_ge(pair_made, 2 * g + 2)
            pool.sem_inc(issuing, 1)
            for j in range(tiles):
                pool.indirect_dma_start(
                    out=t["rows_s"], out_offset=bass.IndirectOffsetOnAxis(ap=pair_at[:, k, j:j + 1], axis=0),
                    in_=pair[:, k, j, :], in_offset=None,
                    bounds_check=last_row, oob_is_err=False).then_inc(paired[k], 16)

        def finish():
            for k in range(4):
                pool.wait_ge(stored[k], 16 * slot_tiles(sh, k, 4))
                pool.wait_ge(paired[k], 16 * slot_tiles(sh, k, 4))
        return [(2, gather, 0), (5, scatter, 0), (5, put_pairs, 0)], finish

    def tensor(pe):
        def filter1(g, k, r, tiles):
            s, n = k % 2, tiles * 128
            pe.wait_ge(radial_made, g + 1)
            if reused(g, 1):
                pe.wait_ge(pos1, g)
            pe.matmul(act1[:, 0:n], w["l3w1"][:, :], radial[:, s, 0:n], start=True, stop=True) \
                .then_inc(act1_made, 1)

        def turn(g, k, r, tiles):
            pe.wait_ge(gathered[k], r * 32 * GT + 32 * tiles)
            pe.wait_ge(ea_in[k], r * 16 + 16)
            if reused(g, 1):
                pe.wait_ge(x_t_out, g)
            for j in range(tiles):
                pe.transpose(turned_x[:, j * 128:(j + 1) * 128], xs[:, k, j, :], c["ident"][:, :])
                last = pe.transpose(turned_e[:, j * 128:(j + 1) * 128], ea[:, k, j, :], c["ident"][:, :])
            last.then_inc(x_turned, 1)

        def project(g, k, r, tiles):
            s = k % 2
            pe.wait_ge(x_t_out, g + 1)
            if reused(g, 1):
                pe.wait_ge(message_out, g)
            for j in range(tiles):
                at = slice(j * 128, (j + 1) * 128)
                pe.matmul(message[:, at], xs_t[:, s, at], w["w0s"][:, :], start=True, stop=False)
                last = pe.matmul(message[:, at], ea_t[:, s, at], w["w0e"][:, :], start=False, stop=True)
            last.then_inc(message_made, 1)

        def filter2(g, k, r, tiles):
            s, n = k % 2, tiles * 128
            pe.wait_ge(hidden_made, g + 1)
            if reused(g, 1):
                pe.wait_ge(filt_made, g)
            pe.matmul(act2[:, 0:n], c["onesb"][:, :], flat(w["l3b2_m"][:, 0:tiles, :]), start=True,
                      stop=False, skip_group_check=True)
            for j in range(tiles):
                at = slice(j * 128, (j + 1) * 128)
                last = pe.matmul(act2[:, at], hidden[:, s, at], w["l3w2"][:, :], start=False, stop=True,
                                 skip_group_check=True)
            last.then_inc(act2_made, 1)
        return [(2, turn, 0), (3, project, 1), (2, filter2, 3), (0, filter1, 3)], None

    def scalar(act):
        act.wait_ge(setup, 1)
        act.activation(cosine[:, :], ramp01[:, :], ACT.Sin, bias=half_pi[:, :], scale=-3.14159265358979) \
            .then_inc(cos_made, 1)

        def radial_part(g, k, r, tiles):
            s, n = k % 2, tiles * 128
            act.wait_ge(dist_in[k], r * 16 + 16)
            if reused(g):
                act.wait_ge(act1_made, g - 1)
            act.activation(radial[:, s, 0:n], dist_row[:, k, 0:n], ACT.Square, bias=w["neg_mu"][:, :]) \
                .then_inc(squared, 1)
            act.wait_ge(squared, g + 1)
            act.activation(radial[:, s, 0:n], radial[:, s, 0:n], ACT.Exp, scale=-float(D)).then_inc(radial_made, 1)

        def decay1(g, k, r, tiles):
            s, n = k % 2, tiles * 128
            act.wait_ge(act1_made, g + 1)
            if reused(g):
                act.wait_ge(hidden_made, g - 1)
            act.activation(soft1[:, s, 0:n], act1[:, 0:n], ACT.Abs, bias=w["l3b1"][:, :]).then_inc(abs1, 1)
            act.wait_ge(abs1, g + 1)
            act.activation(soft1[:, s, 0:n], soft1[:, s, 0:n], ACT.Exp, scale=-1.0).then_inc(exp1, 1)

        def decay2(g, k, r, tiles):
            s, n = k % 2, tiles * 128
            act.wait_ge(act2_made, g + 1)
            if reused(g):
                act.wait_ge(filt_made, g - 1)
            act.activation(soft2[:, s, 0:n], act2[:, 0:n], ACT.Abs).then_inc(abs2, 1)
            act.wait_ge(abs2, g + 1)
            act.activation(soft2[:, s, 0:n], soft2[:, s, 0:n], ACT.Exp, scale=-1.0).then_inc(exp2, 1)

        def logs1(g, k, r, tiles):
            s, n = k % 2, tiles * 128
            act.wait_ge(exp1, g + 1)
            act.activation(soft1[:, s, 0:n], soft1[:, s, 0:n], ACT.Ln, scale=0.5, bias=half[:, :]) \
                .then_inc(log1, 1)

        def logs2(g, k, r, tiles):
            s, n = k % 2, tiles * 128
            act.wait_ge(exp2, g + 1)
            act.activation(soft2[:, s, 0:n], soft2[:, s, 0:n], ACT.Ln, scale=0.5, bias=half[:, :]) \
                .then_inc(log2, 1)

        def copies(g, k, r, tiles):
            s, n = k % 2, tiles * 128
            act.wait_ge(x_turned, g + 1)
            if reused(g):
                act.wait_ge(message_made, g - 1)
            act.activation(xs_t[:, s, 0:n], turned_x[:, 0:n], ACT.Copy)
            act.activation(ea_t[:, s, 0:n], turned_e[:, 0:n], ACT.Copy).then_inc(x_t_out, 1)

        def messages(g, k, r, tiles):
            act.wait_ge(message_made, g + 1)
            if reused(g, 4):
                act.wait_ge(stored[k], r * 16 * GT)
            act.activation(row[:, k, 0:tiles, 0:128], message[:, 0:tiles * 128].rearrange("p (t f) -> p t f", f=128),
                           ACT.Copy).then_inc(message_out, 1)
        return [(4, messages, 0), (1, decay1, 0), (3, decay2, 0), (0, radial_part, 0), (1, logs1, 1), (3, logs2, 1),
                (2, copies, 2)], None

    def vector(dve):
        done = [0]

        def link(instruction):
            instruction.then_inc(linked, 1)
            done[0] += 1
            dve.wait_ge(linked, done[0])
        dve.memset(pad_row[:, :], -1.0)
        dve.memset(half[:, :], 0.5)
        dve.memset(half_pi[:, :], 3.14159265358979 / 2)
        for k in range(4):
            dve.memset(row[:, k, :, 386:388], 0.0)
        dve.wait_ge(ends_in, 48)
        for k in range(2):
            dve.tensor_copy(pairs[:, :, k], ends_i[:, 1 - k, :])
        dve.tensor_scalar(own_i[:, :], ends_i[:, 0, :], sh["n"] - 1, None, ALU.min)
        dve.tensor_scalar(other_i[:, :], ends_i[:, 1, :], sh["n"] - 1, None, ALU.min).then_inc(numbers_ready, 1)
        for k in range(2):
            link(dve.tensor_copy(ends[:, :, k], ends_i[:, k, :]))
        link(dve.tensor_scalar(ramp[:, :], dist[:, :], -0.8, 1.0 / (1.0 - 0.8), ALU.add, ALU.mult))
        dve.tensor_scalar(ramp01[:, :], ramp[:, :], 0.0, 1.0, ALU.max, ALU.min).then_inc(setup, 1)
        dve.wait_ge(cos_made, 1)
        link(dve.tensor_scalar(halved[:, :], cosine[:, :], 0.5, 0.5, ALU.mult, ALU.add))
        link(dve.scalar_tensor_tensor(cut[:, :], dist[:, :], 1.0, halved[:, :], ALU.is_le, ALU.mult))

        def rectify(g, k, r, tiles):
            s, n = k % 2, tiles * 128
            dve.wait_ge(abs1, g + 1)
            if reused(g):
                dve.wait_ge(act2_made, g - 1)
            dve.tensor_scalar(hidden[:, s, 0:n], act1[:, 0:n], w["l3b1"][:, :], 0.0, ALU.add, ALU.max) \
                .then_inc(pos1, 1)

        def hide(g, k, r, tiles):
            s, n = k % 2, tiles * 128
            dve.wait_ge(pos1, g + 1)
            dve.wait_ge(log1, g + 1)
            dve.tensor_tensor(hidden[:, s, 0:n], hidden[:, s, 0:n], soft1[:, s, 0:n], ALU.add) \
                .then_inc(hidden_made, 1)

        def filters(g, k, r, tiles):
            s, n = k % 2, tiles * 128
            dve.wait_ge(log2, g + 1)
            if reused(g):
                dve.wait_ge(row_made, g - 1)
            dve.scalar_tensor_tensor(flat(filt[:, s, 0:tiles, :]), act2[:, 0:n], 0.0, soft2[:, s, 0:n],
                                     ALU.max, ALU.add).then_inc(filt_made, 1)

        def fill(g, k, r, tiles):
            s = k % 2
            dve.wait_ge(filt_made, g + 1)
            dve.wait_ge(ea_in[k], r * 16 + 16)
            if reused(g, 4):
                dve.wait_ge(stored[k], r * 16 * GT)
            for j in range(tiles):
                dve.scalar_tensor_tensor(row[:, k, j, 256:384], ea[:, k, j, :], cut[:, bass.ds(g * GT + j, 1)],
                                         filt[:, s, j, :], ALU.mult, ALU.mult)
            dve.tensor_copy(row[:, k, 0:tiles, END:END + 2], ends[:, bass.ds(g * GT, tiles), :]) \
                .then_inc(row_made, 1)
        return [(1, rectify, 0), (1, hide, 1), (3, filters, 2), (4, fill, 3)], None
    return {"sync": sync, "gpsimd": gpsimd, "tensor": tensor, "scalar": scalar, "vector": vector}


def dense_stage(nc, ctx, semaphore, c, sh, tag, src, dst, weight, bias_m, eps, gram=None):
    def sb(name, shape, dt=F32):
        return ctx.enter_context(nc.sbuf_tensor(f"{tag}_{name}", shape, dt))

    def ps(name):
        return ctx.enter_context(nc.psum_tensor(f"{tag}_{name}", [128, 512], F32))

    def sem(name):
        return semaphore(f"{tag}_{name}")

    groups = sh["full"] + (1 if sh["tail_t"] else 0)
    x = sb("x", [128, LOADS, NT, 128])
    x_t = sb("x_t", [128, 2, ROWS])
    u = sb("u", [128, 4, NT, 128])
    y = sb("y", [128, 4, NT, 128])
    turned, summed = [ps("turned")], [ps("summed")]
    norm = norm_buffers(nc, ctx, semaphore, tag + "_norm", eps, 4)
    x_in = [sem(f"x_in{k}") for k in range(LOADS)]
    y_stored = [sem(f"y_stored{s}") for s in range(LOADS)]
    x_turned, x_t_out, sum_made, u_made, y_made = (
        sem(k) for k in ("x_turned", "x_t_out", "sum_made", "u_made", "y_made"))
    if gram:
        ym = sb("ym", [128, 4, NT, 129])
        kept_inv = sb("kept_inv", [128, 4, NT])
        counts = sb("counts", [128, groups, NT])
        alone = sb("alone", [128, groups, NT])
        gram_ps = ps("gram")
        counts_in, alone_made, kept_made, ym_made, gram_added = (
            sem(k) for k in ("counts_in", "alone_made", "kept_made", "ym_made", "gram_added"))
    else:
        turned.append(ps("turned1"))
        summed.append(ps("summed1"))
    banks = len(turned)

    def view(bank, p, t):
        return bank[:, 0:t * 128].rearrange("p (t f) -> p t f", f=128)[:, :, 0:p]

    def sync(sp):
        if gram:
            n_full = sh["full"] * ROWS
            sp.dma_start(counts[:, 0:sh["full"], :],
                         gram[0][0:n_full].rearrange("(g p r) -> p g r", p=128, r=NT)).then_inc(counts_in, 16)
            if sh["tail_t"]:
                sp.dma_start(counts[0:sh["tail_p"], sh["full"], 0:sh["tail_t"]],
                             gram[0][n_full:sh["n"]].rearrange("(p r) -> p r", r=sh["tail_t"])).then_inc(counts_in, 16)

        def load(g, k, r, size):
            p, t = size
            if reused(g, LOADS):
                sp.wait_ge(u_made, g - LOADS + 1)
            sp.dma_start(x[0:p, k, 0:t, :], node_rows(src, g, size)).then_inc(x_in[k], 16)

        def store(g, k, r, size):
            p, t = size
            sp.wait_ge(y_made, g + 1)
            sp.dma_start(node_rows(dst, g, size), y[0:p, k % 4, 0:t, :]).then_inc(y_stored[k], 16)

        def finish():
            for k in range(LOADS):
                sp.wait_ge(y_stored[k], 16 * len(range(k, groups, LOADS)))
        return [(0, load), (6, store)], finish

    def tensor(pe):
        if gram:
            pe.matmul(gram_ps[:, 0:129], c["zerosb"][:, 0:128], c["zerosb"][:, 0:129], start=True, stop=True,
                      skip_group_check=True)

        def turn(g, k, r, size):
            p, t = size
            pe.wait_ge(x_in[k], r * 16 + 16)
            if reused(g, banks):
                pe.wait_ge(x_t_out, g + 1 - banks)
            bank = turned[k % banks]
            for j in range(t):
                last = pe.transpose(bank[:, j * 128:j * 128 + p], x[0:p, k, j, :], c["ident"][0:p, 0:p])
            last.then_inc(x_turned, 1)

        def project(g, k, r, size):
            p, t = size
            bank = summed[k % banks]
            pe.wait_ge(x_t_out, g + 1)
            if reused(g, banks):
                pe.wait_ge(u_made, g + 1 - banks)
            pe.matmul(bank[0:p, 0:t * 128], c["onesb"][:, 0:p], flat(bias_m[:, 0:t, :]), start=True,
                      stop=False, skip_group_check=True)
            for j in range(t):
                last = pe.matmul(bank[0:p, j * 128:(j + 1) * 128], x_t[:, k % 2, j * 128:j * 128 + p],
                                 weight[:, :], start=False, stop=True, skip_group_check=True)
            last.then_inc(sum_made, 1)

        def add_gram(g, k, r, size):
            p, t = size
            pe.wait_ge(ym_made, g + 1)
            for j in range(t):
                last = pe.matmul(gram_ps[:, 0:129], y[0:p, k % 4, j, :], ym[0:p, k % 4, j, :], start=False, stop=True,
                                 skip_group_check=True)
            last.then_inc(gram_added, 1)
        return [(0, turn), *([(5, add_gram)] if gram else []), (1, project)], None

    def scalar(act):
        def copy(g, k, r, size):
            p, t = size
            act.wait_ge(x_turned, g + 1)
            if reused(g):
                act.wait_ge(sum_made, g - 1)
            act.activation(view(x_t[:, k % 2, :], p, t), view(turned[k % banks], p, t), ACT.Copy).then_inc(x_t_out, 1)

        def deviation(g, k, r, size):
            norm_deviation(norm, act, g, k % 4, *size)

        def finish():
            if gram:
                act.wait_ge(gram_added, groups)
                act.activation(gram[1][:, :], gram_ps[:, 0:129], ACT.Copy).then_inc(x_t_out, 1)
        return [(0, copy), (3, deviation)], finish

    def vector(dve):
        if gram:
            dve.wait_ge(counts_in, 32 if sh["tail_t"] else 16)
            dve.tensor_scalar(flat(alone[:, 0:sh["full"], :]), flat(counts[:, 0:sh["full"], :]), 0.0, None,
                              ALU.is_equal).then_inc(alone_made, 1)
            if sh["tail_t"]:
                dve.tensor_scalar(alone[0:sh["tail_p"], sh["full"], 0:sh["tail_t"]],
                                  counts[0:sh["tail_p"], sh["full"], 0:sh["tail_t"]], 0.0, None,
                                  ALU.is_equal).then_inc(alone_made, 1)
            dve.wait_ge(alone_made, 2 if sh["tail_t"] else 1)

        def add(g, k, r, size):
            p, t = size
            dve.wait_ge(sum_made, g + 1)
            dve.scalar_tensor_tensor(flat(u[0:p, k % 4, 0:t, :]), summed[k % banks][0:p, 0:t * 128], 0.0,
                                     flat(x[0:p, k, 0:t, :]), ALU.max, ALU.add).then_inc(u_made, 1)

        def stats(g, k, r, size):
            p, t = size
            dve.wait_ge(u_made, g + 1)
            norm_stats(norm, dve, u[0:p, k % 4, 0:t, :], k % 4, p, t)

        def moments(g, k, r, size):
            norm_moments(norm, dve, g, k % 4, *size)

        def invert(g, k, r, size):
            norm_invert(norm, dve, g, k % 4, *size)

        def scale(g, k, r, size):
            p, t = size
            s = k % 4
            if reused(g, 4):
                dve.wait_ge(y_stored[(k + 4) % LOADS], (r * 16 if k < 4 else r * 16 + 16))
                if gram:
                    dve.wait_ge(gram_added, g - 3)
            norm_scale(norm, dve, y[0:p, s, 0:t, :], u[0:p, s, 0:t, :], g, s, p, t).then_inc(y_made, 1)
            if gram:
                keep = alone[0:p, bass.ds(g, 1), 0:t].rearrange("p a t -> p (a t)")
                dve.tensor_tensor(kept_inv[0:p, s, 0:t], norm["inv"][0:p, s, 0:t], keep, ALU.mult) \
                    .then_inc(kept_made, 1)

        def mask(g, k, r, size):
            p, t = size
            s = k % 4
            dve.tensor_copy(ym[0:p, s, 0:t, 128], alone[0:p, bass.ds(g, 1), 0:t].rearrange("p a t -> p (a t)"))
            dve.wait_ge(kept_made, g + 1)
            for j in range(t):
                last = dve.tensor_scalar(ym[0:p, s, j, 0:128], u[0:p, s, j, :], norm["moments"][0:p, s, j, 0:1],
                                         kept_inv[0:p, s, j:j + 1], ALU.subtract, ALU.mult)
            last.then_inc(ym_made, 1)
        return [(2, add), (4, invert), (2, stats), (4, scale), (2, moments), *([(4, mask)] if gram else [])], None
    return {"sync": sync, "tensor": tensor, "scalar": scalar, "vector": vector}


def last_dense_stage(nc, ctx, semaphore, c, sh, w, src, table):
    def sb(name, shape, dt=F32):
        return ctx.enter_context(nc.sbuf_tensor("d2_" + name, shape, dt))

    def ps(name):
        return ctx.enter_context(nc.psum_tensor("d2_" + name, [128, 512], F32))

    def sem(name):
        return semaphore("d2_" + name)

    groups = sh["full"] + (1 if sh["tail_t"] else 0)
    x = sb("x", [128, LOADS, NT, 128])
    x_t = sb("x_t", [128, 2, ROWS])
    both, u2 = sb("both", [128, 4, NT, 2 * D]), sb("u2", [128, 4, NT, 128])
    y, y2 = both[:, :, :, 0:D], both[:, :, :, D:2 * D]
    squares = sb("squares", [128, 2, NT, 128])
    power, dev, inv, power2, dev2, inv2 = (sb(k, [128, 4, NT]) for k in ("power", "dev", "inv", "power2", "dev2", "inv2"))
    turned, summed, row_ps = [ps("turned0"), ps("turned1")], [ps(f"summed{k}") for k in range(4)], ps("row")
    x_in, stored = ([sem(f"{name}{k}") for k in range(LOADS)] for name in ("x_in", "stored"))
    (row_made, x_turned, x_t_out, sum_made, power_made, dev_made, inv_made, y_made, u2_made, power2_made, dev2_made,
     inv2_made, y2_made) = (sem(k) for k in (
         "row_made", "x_turned", "x_t_out", "sum_made", "power_made", "dev_made", "inv_made", "y_made", "u2_made",
         "power2_made", "dev2_made", "inv2_made", "y2_made"))

    def view(bank, p, t):
        return bank[:, 0:t * 128].rearrange("p (t f) -> p t f", f=128)[:, :, 0:p]

    def sync(sp):
        def load(g, k, r, size):
            p, t = size
            if reused(g, LOADS):
                sp.wait_ge(x_turned, g - LOADS + 1)
            sp.dma_start(x[0:p, k, 0:t, :], node_rows(src, g, size)).then_inc(x_in[k], 16)

        def store(g, k, r, size):
            p, t = size
            sp.wait_ge(y_made, g + 1)
            sp.wait_ge(y2_made, g + 1)
            sp.dma_start(node_rows(table, g, size), both[0:p, k % 4, 0:t, :]).then_inc(stored[k], 16)

        def finish():
            for k in range(LOADS):
                sp.wait_ge(stored[k], 16 * len(range(k, groups, LOADS)))
        return [(0, load), (6, store)], finish

    def tensor(pe):
        pe.matmul(row_ps[:, :], c["onesb"][:, :], flat(w["lone_mc"][:, :, :]), start=True, stop=True) \
            .then_inc(row_made, 1)

        def turn(g, k, r, size):
            p, t = size
            pe.wait_ge(x_in[k], r * 16 + 16)
            if reused(g):
                pe.wait_ge(x_t_out, g - 1)
            for j in range(t):
                last = pe.transpose(turned[k % 2][:, j * 128:j * 128 + p], x[0:p, k, j, :], c["ident"][0:p, 0:p])
            last.then_inc(x_turned, 1)

        def project(g, k, r, size):
            p, t = size
            bank = summed[k % 4]
            pe.wait_ge(x_t_out, g + 1)
            if reused(g, 4):
                pe.wait_ge(y_made, g - 3)
            pe.matmul(bank[0:p, 0:t * 128], c["onesb"][:, 0:p], flat(w["bz_mc"][:, 0:t, :]), start=True,
                      stop=False, skip_group_check=True)
            for j in range(t):
                last = pe.matmul(bank[0:p, j * 128:(j + 1) * 128], x_t[:, k % 2, j * 128:j * 128 + p],
                                 w["wz"][:, :], start=False, stop=True, skip_group_check=True)
            last.then_inc(sum_made, 1)
        return [(0, turn), (1, project)], None

    def scalar(act):
        def copy(g, k, r, size):
            p, t = size
            act.wait_ge(x_turned, g + 1)
            if reused(g):
                act.wait_ge(sum_made, g - 1)
            act.activation(view(x_t[:, k % 2, :], p, t), view(turned[k % 2], p, t), ACT.Copy).then_inc(x_t_out, 1)

        def measure(g, k, r, size):
            p, t = size
            s = k % 4
            act.wait_ge(sum_made, g + 1)
            if reused(g, 1):
                act.wait_ge(power_made, g)
            for j in range(t):
                last = act.activation(squares[0:p, 0, j, :], summed[s][0:p, j * 128:(j + 1) * 128], ACT.Square,
                                      accum_out=power[0:p, s, j:j + 1])
            last.then_inc(power_made, 1)

        def measure2(g, k, r, size):
            p, t = size
            s = k % 4
            act.wait_ge(u2_made, g + 1)
            if reused(g, 1):
                act.wait_ge(power2_made, g)
            for j in range(t):
                last = act.activation(squares[0:p, 1, j, :], u2[0:p, s, j, :], ACT.Square,
                                      accum_out=power2[0:p, s, j:j + 1])
            last.then_inc(power2_made, 1)

        def deviation(g, k, r, size):
            p, t = size
            act.wait_ge(power_made, g + 1)
            act.activation(dev[0:p, k % 4, 0:t], power[0:p, k % 4, 0:t], ACT.Sqrt, bias=c["ln_eps"][0:p, :],
                           scale=1.0 / D).then_inc(dev_made, 1)

        def deviation2(g, k, r, size):
            p, t = size
            act.wait_ge(power2_made, g + 1)
            act.activation(dev2[0:p, k % 4, 0:t], power2[0:p, k % 4, 0:t], ACT.Sqrt, bias=c["ln_eps"][0:p, :],
                           scale=1.0 / D).then_inc(dev2_made, 1)
        return [(2, measure), (0, copy), (2, deviation), (4, measure2), (4, deviation2)], None

    def vector(dve):
        dve.wait_ge(row_made, 1)

        def invert(g, k, r, size):
            p, t = size
            dve.wait_ge(dev_made, g + 1)
            dve.reciprocal(inv[0:p, k % 4, 0:t], dev[0:p, k % 4, 0:t]).then_inc(inv_made, 1)

        def scale(g, k, r, size):
            p, t = size
            s = k % 4
            if reused(g, 4):
                dve.wait_ge(stored[(k + 4) % LOADS], (r * 16 if k < 4 else r * 16 + 16))
                dve.wait_ge(u2_made, g - 3)
            dve.wait_ge(inv_made, g + 1)
            for j in range(t):
                last = dve.tensor_scalar(y[0:p, s, j, :], summed[s][0:p, j * 128:(j + 1) * 128],
                                         inv[0:p, s, j:j + 1], None, ALU.mult)
            last.then_inc(y_made, 1)

        def add(g, k, r, size):
            p, t = size
            s = k % 4
            dve.wait_ge(y_made, g + 1)
            if reused(g, 4):
                dve.wait_ge(y2_made, g - 3)
            dve.tensor_tensor(u2[0:p, s, 0:t, :], row_ps[0:p, 0:t * 128].rearrange("p (t f) -> p t f", f=D),
                              y[0:p, s, 0:t, :], ALU.add) \
                .then_inc(u2_made, 1)

        def invert2(g, k, r, size):
            p, t = size
            dve.wait_ge(dev2_made, g + 1)
            dve.reciprocal(inv2[0:p, k % 4, 0:t], dev2[0:p, k % 4, 0:t]).then_inc(inv2_made, 1)

        def scale2(g, k, r, size):
            p, t = size
            s = k % 4
            if reused(g, 4):
                dve.wait_ge(stored[(k + 4) % LOADS], (r * 16 if k < 4 else r * 16 + 16))
            dve.wait_ge(inv2_made, g + 1)
            for j in range(t):
                last = dve.tensor_scalar(y2[0:p, s, j, :], u2[0:p, s, j, :], inv2[0:p, s, j:j + 1], None, ALU.mult)
            last.then_inc(y2_made, 1)
        return [(3, invert), (5, invert2), (3, scale), (5, scale2), (3, add)], None
    return {"sync": sync, "tensor": tensor, "scalar": scalar, "vector": vector}


def order_buffers(nc, ctx, sh, tag):
    o = {"joined": ctx.enter_context(nc.sbuf_tensor(tag + "_joined", [128, sh["ep"] + 1], BF16))}
    for name in ("store_at", "own_at", "other_at"):
        o[name] = ctx.enter_context(nc.sbuf_tensor(f"{tag}_{name}", [128, sh["et"]], I32))
    return o


def order_stage(nc, inner, semaphore, c, sh, tag, o, table, first_column):
    def sb(name, shape, dt=F32):
        return inner.enter_context(nc.sbuf_tensor(f"{tag}o_{name}", shape, dt))

    def sem(name):
        return semaphore(f"{tag}o_{name}")

    near = [sb(f"near{k}", [128, sh["et"], 2]) for k in range(3)]
    joined_col = sb("joined_col", [128, sh["et"]], BF16)
    more = sb("more", [128, sh["et"]])
    store_f = sb("store_f", [128, sh["et"]])
    bank = inner.enter_context(nc.psum_tensor(f"{tag}o_bank", [128, 512], F32))
    rows_in, linked, columns_made, spread, copied = (
        sem(k) for k in ("rows_in", "linked", "columns_made", "spread", "copied"))

    def sync(sp):
        for k in range(3):
            sp.dma_start(near[k][:, :, :], table[k:k + sh["ep"], first_column:first_column + 2]
                         .rearrange("(t p) f -> p t f", p=128)).then_inc(rows_in, 16)
        return [], None

    def vector(dve):
        def finish():
            done = [0]

            def link(instruction):
                instruction.then_inc(linked, 1)
                done[0] += 1
                dve.wait_ge(linked, done[0])
            dve.wait_ge(rows_in, 48)
            own = near[1][:, :, 0]
            dve.tensor_tensor(joined_col[:, :], near[0][:, :, 0], own, ALU.is_equal).then_inc(columns_made, 1)
            link(dve.tensor_tensor(more[:, :], near[2][:, :, 0], own, ALU.is_equal))
            link(dve.scalar_tensor_tensor(store_f[:, :], more[:, :], SKIP, own, ALU.mult, ALU.add))
            dve.tensor_copy(o["store_at"][:, :], store_f[:, :])
            dve.tensor_scalar(o["own_at"][:, :], own, float(sh["n"] - 1), None, ALU.min)
            dve.tensor_scalar(o["other_at"][:, :], near[1][:, :, 1], float(sh["n"] - 1), None, ALU.min)
            link(dve.memset(o["joined"][:, sh["ep"]:sh["ep"] + 1], 1.0 if sh["pads"] else 0.0))
        return [], finish

    def tensor(pe):
        def finish():
            pe.wait_ge(columns_made, 1)

            def spread_out(g, s, r, tiles):
                if reused(g, 1):
                    pe.wait_ge(copied, g)
                for j in range(tiles):
                    last = pe.matmul(bank[:, j * 128:(j + 1) * 128],
                                     joined_col[:, bass.ds(g * GT + j, 1)].to_broadcast([128, 128]),
                                     c["identb"][:, :], start=True, stop=True)
                last.then_inc(spread, 1)
            edge_groups(pe, sh, (0, spread_out))
        return [], finish

    def scalar(act):
        def finish():
            def copy(g, s, r, tiles):
                act.wait_ge(spread, g + 1)
                act.activation(o["joined"][:, bass.ds(g * GE, tiles * 128)], bank[:, 0:tiles * 128],
                               ACT.Copy).then_inc(copied, 1)
            edge_groups(act, sh, (0, copy))
        return [], finish

    return {"sync": sync, "vector": vector, "tensor": tensor, "scalar": scalar}


def layer0_ends(nc, c, sh, t, w, o):
    with stage(nc) as (ctx, semaphore):
        def sb(name, shape, dt=F32):
            return ctx.enter_context(nc.sbuf_tensor("e0_" + name, shape, dt))

        def sem(name):
            return semaphore("e0_" + name)

        rows = sb("rows", [128, 4, GT, 256])
        total = sb("total", [128, 2, GE])
        x_t = sb("x_t", [128, 2, GE])
        u = sb("u", [128, 2, GT, 128])
        y = sb("y", [128, 4, GT, 128])
        at = sb("at", [128, 4, GT], I32)
        message_t0, message_t1, turned0, turned1, summed0, summed1 = (ctx.enter_context(nc.psum_tensor("e0_" + k, [128, 512], F32))
                                               for k in ("message_t0", "message_t1", "turned0", "turned1", "summed0", "summed1"))
        message_t, turned, summed = [message_t0, message_t1], [turned0, turned1], [summed0, summed1]
        norm = norm_buffers(nc, ctx, semaphore, "e0_norm", c["ln_eps"])
        rows_in = [sem(f"rows_in{k}") for k in range(4)]
        kept = [sem(f"kept{k}") for k in range(4)]
        scattered = [sem(f"scattered{k}") for k in range(4)]
        message_turned, x_turned, total_made, x_t_out, sum_made, u_made, y_made, at_made, issuing = (
            sem(k) for k in ("message_turned", "x_turned", "total_made", "x_t_out", "sum_made", "u_made", "y_made",
                             "at_made", "issuing"))

        with nc.Block() as block:
            @block.sync
            def _(sp):
                def load(g, k, r, tiles):
                    if reused(g, 4):
                        sp.wait_ge(u_made, g - 3)
                    sp.dma_start(rows[:, k, 0:tiles, :], edge_rows(t["rows_d"], g, tiles, 1, slice(0, 256))) \
                        .then_inc(rows_in[k], 16)

                def keep(g, k, r, tiles):
                    sp.wait_ge(y_made, g + 1)
                    sp.dma_start(edge_rows(t["x1_ends"], g, tiles), y[:, k, 0:tiles, :]).then_inc(kept[k], 16)
                edge_rings(sp, sh, (0, load), (4, keep))
                for k in range(4):
                    sp.wait_ge(kept[k], 16 * slot_groups(sh, k, 4))

            @block.gpsimd
            def _(pool):
                last_node = pool.to_reg(sh["n"] - 1)

                def scatter(g, k, r, tiles):
                    if reused(g, 4):
                        pool.wait_ge(scattered[k], r * 16 * GT)
                    row_numbers(pool, at, k, tiles, o["store_at"], g, at_made)
                    pool.wait_ge(at_made, g + 1)
                    pool.wait_ge(y_made, g + 1)
                    pool.sem_inc(issuing, 1)
                    for j in range(tiles):
                        pool.indirect_dma_start(
                            out=t["x1"], out_offset=bass.IndirectOffsetOnAxis(ap=at[:, k, j:j + 1], axis=0),
                            in_=y[:, k, j, :], in_offset=None, bounds_check=last_node, oob_is_err=False) \
                            .then_inc(scattered[k], 16)
                edge_rings(pool, sh, (0, scatter))
                for k in range(4):
                    pool.wait_ge(scattered[k], 16 * slot_tiles(sh, k, 4))

            @block.tensor
            def _(pe):
                def turn(g, k, r, tiles):
                    s = k % 2
                    pe.wait_ge(rows_in[k], r * 16 + 16)
                    if reused(g):
                        pe.wait_ge(total_made, g - 1)
                    for j in range(tiles):
                        last = pe.transpose(message_t[s][:, j * 128:(j + 1) * 128], rows[:, k, j, 0:128], c["ident"][:, :])
                    last.then_inc(message_turned, 1)
                    if reused(g):
                        pe.wait_ge(x_t_out, g - 1)
                    for j in range(tiles):
                        last = pe.transpose(turned[s][:, j * 128:(j + 1) * 128], rows[:, k, j, 128:256], c["ident"][:, :])
                    last.then_inc(x_turned, 1)

                def project(g, k, r, tiles):
                    s = k % 2
                    pe.wait_ge(x_t_out, g + 1)
                    pe.wait_ge(total_made, g + 1)
                    if reused(g):
                        pe.wait_ge(u_made, g - 1)
                    pe.matmul(summed[s][:, 0:tiles * 128], c["onesb"][:, :], flat(w["b0_m"][:, 0:tiles, :]), start=True,
                              stop=False, skip_group_check=True)
                    for j in range(tiles):
                        cols = slice(j * 128, (j + 1) * 128)
                        pe.matmul(summed[s][:, cols], x_t[:, s, cols], w["w0x"][:, :], start=False, stop=True,
                                  skip_group_check=True)
                        last = pe.matmul(summed[s][:, cols], total[:, s, cols], c["ident"][:, :], start=False, stop=True,
                                         skip_group_check=True)
                    last.then_inc(sum_made, 1)

                edge_rings(pe, sh, (0, turn), (1, project))

            @block.scalar
            def _(act):
                def copy(g, k, r, tiles):
                    s = k % 2
                    n = tiles * 128
                    act.wait_ge(x_turned, g + 1)
                    if reused(g):
                        act.wait_ge(sum_made, g - 1)
                    act.activation(x_t[:, s, 0:n], turned[s][:, 0:n], ACT.Copy).then_inc(x_t_out, 1)

                edge_rings(act, sh, (0, copy), (2, lambda g, k, r, tiles: norm_deviation(norm, act, g, k % 2, 128, tiles)))

            @block.vector
            def _(dve):
                def sum_up(g, k, r, tiles):
                    s = k % 2
                    n = tiles * 128
                    dve.wait_ge(message_turned, g + 1)
                    if reused(g, 1):
                        dve.wait_ge(total_made, g)
                    if reused(g):
                        dve.wait_ge(sum_made, g - 1)
                    dve.tensor_tensor_scan(
                        total[:, s, 0:n], o["joined"][:, bass.ds(g * GE, n)], message_t[s][:, 0:n],
                        total[:, 1 - s, GE - 1:GE] if reused(g, 1) else 0.0, ALU.mult, ALU.add).then_inc(total_made, 1)

                def measure(g, k, r, tiles):
                    s = k % 2
                    dve.wait_ge(sum_made, g + 1)
                    if reused(g):
                        dve.wait_ge(y_made, g - 1)
                    dve.scalar_tensor_tensor(
                        u[:, s, 0:tiles, :], summed[s][:, 0:tiles * 128].rearrange("p (t f) -> p t f", f=128), 0.0,
                        rows[:, k, 0:tiles, 128:256], ALU.max, ALU.add).then_inc(u_made, 1)
                    dve.wait_ge(u_made, g + 1)
                    norm_measure(norm, dve, u[:, s, 0:tiles, :], g, s, 128, tiles)

                def scale(g, k, r, tiles):
                    s = k % 2
                    if reused(g, 4):
                        dve.wait_ge(kept[k], r * 16)
                        dve.wait_ge(scattered[k], r * 16 * GT)
                    norm_invert(norm, dve, g, s, 128, tiles)
                    norm_scale(norm, dve, y[:, k, 0:tiles, :], u[:, s, 0:tiles, :], g, s, 128, tiles).then_inc(y_made, 1)
                edge_rings(dve, sh, (0, sum_up), (2, scale), (1, measure))


def slot_groups(sh, s, slots=2):
    return len(range(s, sh["eg"] + (1 if sh["tail_e"] else 0), slots))


def slot_tiles(sh, s, slots=2):
    return sum(sh["tail_e"] if g == sh["eg"] else GT for g in range(s, sh["eg"] + (1 if sh["tail_e"] else 0), slots))


def attention(nc, c, sh, t, w, o, mixed_all, sums):
    with stage(nc) as (ctx, semaphore):
        def sb(name, shape=None, dt=F32):
            return ctx.enter_context(nc.sbuf_tensor("at_" + name, shape or [128, 2, GE], dt))

        def sem(name):
            return semaphore("at_" + name)

        groups = sh["eg"] + (1 if sh["tail_e"] else 0)
        own_at, other_at = (sb(k, [128, 4, GT], I32) for k in ("own_at", "other_at"))
        xa, xb = sb("xa", [128, 4, GT, 128]), sb("xb", [128, 4, GT, 128])
        xa_t, xb_t = sb("xa_t"), sb("xb_t")
        restart, logit, own, lift = (sb(k) for k in ("restart", "logit", "own", "lift"))
        peak = sb("peak", [128, 2, GE + 1])
        fall = sb("fall", [128, GE])
        step, below, up, down = (sb(k) for k in ("step", "below", "up", "down"))
        total, mixed, scaled = sb("total"), sb("mixed"), sb("scaled")
        weighted, mine = sb("weighted"), sb("mine", [128, GE])
        squares = sb("squares", [128, GE])
        last = sb("last", [128, 4, GE], BF16)
        decay, p, keep_old, keep_own = step, below, up, down
        whole = inverse = scaled
        old = both = result = weighted
        sum_parts, square_parts = sb("sum_parts", [128, groups]), sb("square_parts", [128, groups])
        turned_a, turned_b, score, own_score, value0, value1, own_value0, own_value1 = (
            ctx.enter_context(nc.psum_tensor("at_" + k, [128, 512], F32))
            for k in ("turned_a", "turned_b", "score", "own_score", "value0", "value1", "own_value0", "own_value1"))
        value, own_value = [value0, value1], [own_value0, own_value1]
        gathered = [sem(f"gathered{k}") for k in range(4)]
        names = ("at_made leaks_made x_turned x_t_out score_made value_made own_score_made logit_made own_made restart_made "
                 "peak_made carry_made fall_made step_made decay_made below_made p_made total_made weighted_made "
                 "mixed_made lift_made up_made keeps_made scaled_made whole_made inverse_made log_made old_made mine_made "
                 "both_made result_made last_made summed squared issuing finished")
        S = {k: sem(k) for k in names.split()}

        with nc.Block() as block:
            @block.gpsimd
            def _(pool):
                last_node = pool.to_reg(sh["n"] - 1)

                def gather(g, k, r, tiles):
                    if reused(g, 4):
                        pool.wait_ge(gathered[k], r * 32 * GT)
                    row_numbers(pool, own_at, k, tiles, o["own_at"], g, S["at_made"])
                    row_numbers(pool, other_at, k, tiles, o["other_at"], g, S["at_made"])
                    pool.wait_ge(S["at_made"], 2 * g + 2)
                    if reused(g, 4):
                        pool.wait_ge(S["x_turned"], g - 3)
                    pool.sem_inc(S["issuing"], 1)
                    for j in range(tiles):
                        for to, numbers in ((xa, own_at), (xb, other_at)):
                            pool.indirect_dma_start(
                                out=to[:, k, j, :], out_offset=None, in_=t["x1"],
                                in_offset=bass.IndirectOffsetOnAxis(ap=numbers[:, k, j:j + 1], axis=0),
                                bounds_check=last_node, oob_is_err=False).then_inc(gathered[k], 16)
                edge_rings(pool, sh, (0, gather))

            @block.tensor
            def _(pe):
                def turn(g, k, r, tiles):
                    pe.wait_ge(gathered[k], r * 32 * GT + 32 * tiles)
                    if reused(g, 1):
                        pe.wait_ge(S["x_t_out"], g)
                    for j in range(tiles):
                        pe.transpose(turned_a[:, j * 128:(j + 1) * 128], xa[:, k, j, :], c["ident"][:, :])
                        last_ = pe.transpose(turned_b[:, j * 128:(j + 1) * 128], xb[:, k, j, :], c["ident"][:, :])
                    last_.then_inc(S["x_turned"], 1)

                def project(g, k, r, tiles):
                    s, n = k % 2, tiles * 128
                    pe.wait_ge(S["x_t_out"], g + 1)
                    if reused(g, 1):
                        pe.wait_ge(S["logit_made"], g)
                    pe.matmul(score[:, 0:n], w["ws"][:, :], xb_t[:, s, 0:n], start=True, stop=False)
                    pe.matmul(score[:, 0:n], w["wd"][:, :], xa_t[:, s, 0:n], start=False, stop=True) \
                        .then_inc(S["score_made"], 1)
                    if reused(g, 1):
                        pe.wait_ge(S["own_made"], g)
                    pe.matmul(own_score[:, 0:n], w["wsd"][:, :], xa_t[:, s, 0:n], start=True, stop=True) \
                        .then_inc(S["own_score_made"], 1)
                    if reused(g):
                        pe.wait_ge(S["mine_made"], g - 1)
                    pe.matmul(value[s][:, 0:n], w["w1"][:, :], xb_t[:, s, 0:n], start=True, stop=True)
                    pe.matmul(own_value[s][:, 0:n], w["w1"][:, :], xa_t[:, s, 0:n], start=True, stop=True) \
                        .then_inc(S["value_made"], 1)
                edge_rings(pe, sh, (0, turn), (1, project))

            @block.scalar
            def _(act):
                def copies(g, k, r, tiles):
                    s, n = k % 2, tiles * 128
                    act.wait_ge(S["x_turned"], g + 1)
                    if reused(g):
                        act.wait_ge(S["value_made"], g - 1)
                    act.activation(xa_t[:, s, 0:n], turned_a[:, 0:n], ACT.Copy)
                    act.activation(xb_t[:, s, 0:n], turned_b[:, 0:n], ACT.Copy).then_inc(S["x_t_out"], 1)

                def masks(g, k, r, tiles):
                    s, n = k % 2, tiles * 128
                    if reused(g):
                        act.wait_ge(S["step_made"], g - 1)
                    if reused(g, 4):
                        act.wait_ge(S["summed"], g - 3)
                    act.activation(restart[:, s, 0:n], o["joined"][:, bass.ds(g * GE, n)], ACT.Copy, scale=-NEG, bias=NEG) \
                        .then_inc(S["restart_made"], 1)
                    act.activation(last[:, k, 0:n], o["joined"][:, bass.ds(g * GE + 1, n)], ACT.Copy, scale=-1.0, bias=1.0) \
                        .then_inc(S["last_made"], 1)

                def leaks(g, k, r, tiles):
                    s, n = k % 2, tiles * 128
                    act.wait_ge(S["score_made"], g + 1)
                    act.wait_ge(S["own_score_made"], g + 1)
                    if reused(g):
                        act.wait_ge(S["below_made"], g - 1)
                        act.wait_ge(S["lift_made"], g - 1)
                    act.activation(logit[:, s, 0:n], score[:, 0:n], ACT.Copy, scale=SLOPE)
                    act.activation(own[:, s, 0:n], own_score[:, 0:n], ACT.Copy, scale=SLOPE).then_inc(S["leaks_made"], 1)

                def exps(g, k, r, tiles):
                    s, n = k % 2, tiles * 128
                    act.wait_ge(S["step_made"], g + 1)
                    act.activation(decay[:, s, 0:n], step[:, s, 0:n], ACT.Exp).then_inc(S["decay_made"], 1)
                    act.wait_ge(S["below_made"], g + 1)
                    act.activation(p[:, s, 0:n], below[:, s, 0:n], ACT.Exp).then_inc(S["p_made"], 1)
                    act.wait_ge(S["lift_made"], g + 1)
                    if reused(g):
                        act.wait_ge(S["old_made"], g - 1)
                        act.wait_ge(S["whole_made"], g - 1)
                    act.activation(up[:, s, 0:n], lift[:, s, 0:n], ACT.Relu)
                    act.activation(down[:, s, 0:n], lift[:, s, 0:n], ACT.Relu, scale=-1.0).then_inc(S["up_made"], 1)
                    act.wait_ge(S["up_made"], g + 1)
                    act.activation(keep_old[:, s, 0:n], up[:, s, 0:n], ACT.Exp, scale=-1.0)
                    act.activation(keep_own[:, s, 0:n], down[:, s, 0:n], ACT.Exp, scale=-1.0).then_inc(S["keeps_made"], 1)

                def logs(g, k, r, tiles):
                    s, n = k % 2, tiles * 128
                    act.wait_ge(S["whole_made"], g + 1)
                    act.activation(whole[:, s, 0:n], whole[:, s, 0:n], ACT.Ln).then_inc(S["log_made"], 1)

                def invert(g, k, r, tiles):
                    s, n = k % 2, tiles * 128
                    act.wait_ge(S["log_made"], g + 1)
                    act.activation(inverse[:, s, 0:n], whole[:, s, 0:n], ACT.Exp, scale=-1.0).then_inc(S["inverse_made"], 1)

                def square(g, k, r, tiles):
                    act.wait_ge(S["summed"], g + 1)
                    if reused(g, 1):
                        act.wait_ge(S["squared"], g)
                    act.activation(squares[:, 0:tiles * 128], mixed_all[:, bass.ds(g * GE, tiles * 128)], ACT.Square,
                                   accum_out=square_parts[:, bass.ds(g, 1)]).then_inc(S["squared"], 1)
                edge_rings(act, sh, (0, copies), (1, leaks), (3, logs), (3, invert), (2, exps), (0, masks), (5, square))

            @block.vector
            def _(dve):
                def weigh(g, k, r, tiles):
                    s, n = k % 2, tiles * 128
                    dve.wait_ge(S["leaks_made"], g + 1)
                    dve.tensor_tensor(logit[:, s, 0:n], score[:, 0:n], logit[:, s, 0:n], ALU.max) \
                        .then_inc(S["logit_made"], 1)
                    dve.tensor_tensor(own[:, s, 0:n], own_score[:, 0:n], own[:, s, 0:n], ALU.max) \
                        .then_inc(S["own_made"], 1)
                    dve.wait_ge(S["restart_made"], g + 1)
                    dve.wait_ge(S["logit_made"], g + 1)
                    if reused(g, 1):
                        dve.wait_ge(S["carry_made"], g + 1)
                    else:
                        dve.memset(peak[:, 0, 0:1], 0.0).then_inc(S["carry_made"], 1)
                        dve.wait_ge(S["carry_made"], 1)
                    dve.tensor_tensor_scan(peak[:, s, 1:n + 1], restart[:, s, 0:n], logit[:, s, 0:n], peak[:, s, 0:1],
                                           ALU.add, ALU.max).then_inc(S["peak_made"], 1)
                    dve.wait_ge(S["peak_made"], g + 1)
                    dve.tensor_copy(peak[:, 1 - s, 0:1], peak[:, s, n:n + 1]).then_inc(S["carry_made"], 1)
                    if reused(g, 1):
                        dve.wait_ge(S["step_made"], g)
                    if reused(g):
                        dve.wait_ge(S["mixed_made"], g - 1)
                    dve.tensor_tensor(fall[:, 0:n], peak[:, s, 0:n], peak[:, s, 1:n + 1], ALU.subtract) \
                        .then_inc(S["fall_made"], 1)
                    dve.tensor_tensor(below[:, s, 0:n], logit[:, s, 0:n], peak[:, s, 1:n + 1], ALU.subtract) \
                        .then_inc(S["below_made"], 1)
                    if reused(g):
                        dve.wait_ge(S["up_made"], g - 1)
                    dve.wait_ge(S["own_made"], g + 1)
                    dve.tensor_tensor(lift[:, s, 0:n], own[:, s, 0:n], peak[:, s, 1:n + 1], ALU.subtract) \
                        .then_inc(S["lift_made"], 1)
                    dve.wait_ge(S["fall_made"], g + 1)
                    dve.tensor_tensor(step[:, s, 0:n], fall[:, 0:n], restart[:, s, 0:n], ALU.add) \
                        .then_inc(S["step_made"], 1)

                def mix(g, k, r, tiles):
                    s, n = k % 2, tiles * 128
                    if reused(g, 1):
                        dve.wait_ge(S["both_made"], g)
                    if reused(g):
                        dve.wait_ge(S["summed"], g - 1)
                    dve.wait_ge(S["p_made"], g + 1)
                    dve.wait_ge(S["value_made"], g + 1)
                    dve.tensor_tensor(weighted[:, s, 0:n], value[s][:, 0:n], p[:, s, 0:n], ALU.mult) \
                        .then_inc(S["weighted_made"], 1)
                    dve.wait_ge(S["decay_made"], g + 1)
                    dve.tensor_tensor_scan(total[:, s, 0:n], decay[:, s, 0:n], p[:, s, 0:n],
                                           total[:, 1 - s, GE - 1:GE] if reused(g, 1) else 0.0, ALU.mult, ALU.add) \
                        .then_inc(S["total_made"], 1)
                    dve.wait_ge(S["weighted_made"], g + 1)
                    dve.tensor_tensor_scan(mixed[:, s, 0:n], decay[:, s, 0:n], weighted[:, s, 0:n],
                                           mixed[:, 1 - s, GE - 1:GE] if reused(g, 1) else 0.0, ALU.mult, ALU.add) \
                        .then_inc(S["mixed_made"], 1)
                    dve.wait_ge(S["keeps_made"], g + 1)
                    dve.tensor_tensor(mine[:, 0:n], own_value[s][:, 0:n], keep_own[:, s, 0:n], ALU.mult) \
                        .then_inc(S["mine_made"], 1)
                    dve.wait_ge(S["total_made"], g + 1)
                    dve.tensor_tensor(scaled[:, s, 0:n], total[:, s, 0:n], keep_old[:, s, 0:n], ALU.mult) \
                        .then_inc(S["scaled_made"], 1)
                    dve.wait_ge(S["mixed_made"], g + 1)
                    dve.tensor_tensor(old[:, s, 0:n], mixed[:, s, 0:n], keep_old[:, s, 0:n], ALU.mult) \
                        .then_inc(S["old_made"], 1)
                    dve.wait_ge(S["scaled_made"], g + 1)
                    dve.scalar_tensor_tensor(whole[:, s, 0:n], scaled[:, s, 0:n], SOFTMAX_EPS, keep_own[:, s, 0:n],
                                             ALU.add, ALU.add).then_inc(S["whole_made"], 1)
                    dve.wait_ge(S["old_made"], g + 1)
                    dve.wait_ge(S["mine_made"], g + 1)
                    dve.tensor_tensor(both[:, s, 0:n], old[:, s, 0:n], mine[:, 0:n], ALU.add).then_inc(S["both_made"], 1)

                def divide(g, k, r, tiles):
                    s, n = k % 2, tiles * 128
                    dve.wait_ge(S["both_made"], g + 1)
                    dve.wait_ge(S["inverse_made"], g + 1)
                    dve.tensor_tensor(result[:, s, 0:n], both[:, s, 0:n], inverse[:, s, 0:n], ALU.mult) \
                        .then_inc(S["result_made"], 1)
                    dve.wait_ge(S["result_made"], g + 1)
                    dve.wait_ge(S["last_made"], g + 1)
                    dve.scalar_tensor_tensor(mixed_all[:, bass.ds(g * GE, n)], result[:, s, 0:n], 1.0, last[:, k, 0:n],
                                             ALU.mult, ALU.mult, accum_out=sum_parts[:, bass.ds(g, 1)]) \
                        .then_inc(S["summed"], 1)
                edge_rings(dve, sh, (0, weigh), (2, divide), (1, mix))
                dve.wait_ge(S["summed"], groups)
                dve.wait_ge(S["squared"], groups)
                dve.tensor_reduce(sums[:, 0:1], sum_parts[:, :], AX.X, ALU.add)
                dve.tensor_reduce(sums[:, 1:2], square_parts[:, :], AX.X, ALU.add).then_inc(S["finished"], 1)


def batch_norm(nc, c, sh, w, gram, sums, out):
    with stage(nc) as (ctx, semaphore):
        def sb(name, shape):
            return ctx.enter_context(nc.sbuf_tensor("bn_" + name, shape, F32))

        def sem(name):
            return semaphore("bn_" + name)

        gw, mean, squares, mean2, var = sb("gw", [128, 128]), *(sb(k, [128, 1]) for k in ("mean", "squares", "mean2", "var"))
        total, total2, dev, inv = (sb(k, [128, 1]) for k in ("total", "total2", "dev", "inv"))
        moved, centre, scale, shift, bn_eps = (sb(k, [128, 1]) for k in ("moved", "centre", "scale", "shift", "bn_eps"))
        scale_all, shift_all, shift_row = sb("scale_all", [128, 128]), sb("shift_all", [128, 128]), sb("shift_row", [128, 128])
        a, b = (ctx.enter_context(nc.psum_tensor("bn_" + k, [128, 512], F32)) for k in ("a", "b"))
        linked, product, product_out, reduced, reduced_out, var_made, dev_made, columns, spread = (
            sem(k) for k in ("linked", "product", "product_out", "reduced", "reduced_out", "var_made", "dev_made", "columns", "spread"))
        with nc.Block() as block:
            @block.tensor
            def _(pe):
                pe.matmul(a[:, 0:128], gram[:, 0:128], w["w1"][:, :], start=True, stop=True).then_inc(product, 1)
                pe.wait_ge(product_out, 1)
                pe.matmul(b[:, 0:1], gw[:, :], c["ones"][:, 0:1], start=True, stop=True)
                pe.matmul(b[:, 1:2], w["w1"][:, :], gram[:, 128:129], start=True, stop=True).then_inc(reduced, 1)
                pe.wait_ge(columns, 1)
                pe.matmul(a[:, 128:256], scale_all[:, :], c["ident"][:, :], start=True, stop=True)
                pe.matmul(a[:, 256:384], shift_all[:, :], c["ident"][:, :], start=True, stop=True).then_inc(spread, 1)

            @block.scalar
            def _(act):
                act.wait_ge(var_made, 1)
                act.activation(dev[:, :], var[:, :], ACT.Sqrt, bias=bn_eps[:, :]).then_inc(dev_made, 1)

            @block.vector
            def _(dve):
                done = [0]

                def link(instruction):
                    instruction.then_inc(linked, 1)
                    done[0] += 1
                    dve.wait_ge(linked, done[0])
                dve.memset(bn_eps[:, :], BN_EPS)
                dve.wait_ge(product, 1)
                dve.tensor_tensor(gw[:, :], a[:, 0:128], w["w1"][:, :], ALU.mult).then_inc(product_out, 1)
                dve.wait_ge(reduced, 1)
                dve.tensor_tensor(total[:, :], b[:, 1:2], sums[:, 0:1], ALU.add)
                link(dve.tensor_tensor(total2[:, :], b[:, 0:1], sums[:, 1:2], ALU.add))
                dve.tensor_scalar(mean[:, :], total[:, :], 1.0 / sh["n"], None, ALU.mult)
                link(dve.tensor_scalar(squares[:, :], total2[:, :], 1.0 / sh["n"], None, ALU.mult))
                link(dve.tensor_tensor(mean2[:, :], mean[:, :], mean[:, :], ALU.mult))
                link(dve.tensor_tensor(centre[:, :], squares[:, :], mean2[:, :], ALU.subtract))
                dve.tensor_scalar(var[:, :], centre[:, :], 0.0, None, ALU.max).then_inc(var_made, 1)
                dve.wait_ge(dev_made, 1)
                link(dve.reciprocal(inv[:, :], dev[:, :]))
                link(dve.tensor_tensor(scale[:, :], inv[:, :], w["gamma"][:, :], ALU.mult))
                link(dve.tensor_tensor(moved[:, :], mean[:, :], w["bias1"][:, :], ALU.add))
                link(dve.tensor_tensor(mean2[:, :], w["bias1"][:, :], moved[:, :], ALU.subtract))
                link(dve.scalar_tensor_tensor(shift[:, :], mean2[:, :], scale[:, 0:1], w["beta"][:, :], ALU.mult, ALU.add))
                dve.tensor_scalar(out["scale"][:, :], scale[:, :], 0.5, None, ALU.mult)
                link(dve.tensor_scalar(out["shift"][:, :], shift[:, :], 0.5, None, ALU.mult))
                dve.tensor_scalar(scale_all[:, :], c["ones"][:, :], out["scale"][:, :], None, ALU.mult)
                dve.tensor_scalar(shift_all[:, :], c["ones"][:, :], out["shift"][:, :], None, ALU.mult) \
                    .then_inc(columns, 1)
                dve.wait_ge(spread, 1)
                link(dve.tensor_tensor(out["w1"][:, :], a[:, 128:256], w["w1"][:, :], ALU.mult))
                link(dve.tensor_copy(shift_row[:, :], a[:, 256:384]))
                bias_parts(dve, link, w, shift_row, out["shift_m"])


def layer1_ends(nc, c, sh, t, o, mixed, bn):
    with stage(nc) as (ctx, semaphore):
        def sb(name, shape, dt=F32):
            return ctx.enter_context(nc.sbuf_tensor("e1_" + name, shape, dt))

        def sem(name):
            return semaphore("e1_" + name)

        rows = sb("rows", [128, 2, GT, 128])
        active = sb("active", [128, 2, GE])
        u, y = sb("u", [128, 2, GT, 128]), sb("y", [128, 2, GT, 128])
        at = sb("at", [128, 2, GT], I32)
        turned = [ctx.enter_context(nc.psum_tensor(f"e1_turned{k}", [128, 512], F32)) for k in range(2)]
        norm = norm_buffers(nc, ctx, semaphore, "e1_norm", c["ln_eps4"])
        rows_in = [sem("rows_in0"), sem("rows_in1")]
        scattered = [sem("scattered0"), sem("scattered1")]
        active_made, turn_made, u_made, y_made, at_made, issuing = (
            sem(k) for k in ("active_made", "turn_made", "u_made", "y_made", "at_made", "issuing"))
        with nc.Block() as block:
            @block.sync
            def _(sp):
                def load(g, s, r, tiles):
                    if reused(g):
                        sp.wait_ge(u_made, g - 1)
                    sp.dma_start(rows[:, s, 0:tiles, :], edge_rows(t["x1_ends"], g, tiles)).then_inc(rows_in[s], 16)
                edge_groups(sp, sh, (0, load))

            @block.scalar
            def _(act):
                def activate(g, s, r, tiles):
                    n = tiles * 128
                    if reused(g):
                        act.wait_ge(turn_made, g - 1)
                    act.activation(active[:, s, 0:n], mixed[:, bass.ds(g * GE, n)], ACT.Relu,
                                   bias=bn["shift"][:, :], scale=bn["scale"][:, :]).then_inc(active_made, 1)
                edge_groups(act, sh, (0, activate), (1, lambda g, s, r, tiles: norm_deviation(norm, act, g, s, 128, tiles)))

            @block.tensor
            def _(pe):
                def turn(g, s, r, tiles):
                    pe.wait_ge(active_made, g + 1)
                    if reused(g):
                        pe.wait_ge(u_made, g - 1)
                    for j in range(tiles):
                        last = pe.transpose(turned[s][:, j * 128:(j + 1) * 128], active[:, s, j * 128:(j + 1) * 128],
                                            c["ident"][:, :])
                    last.then_inc(turn_made, 1)
                edge_groups(pe, sh, (0, turn))

            @block.vector
            def _(dve):
                def measure(g, s, r, tiles):
                    dve.wait_ge(turn_made, g + 1)
                    dve.wait_ge(rows_in[s], r * 16 + 16)
                    if reused(g):
                        dve.wait_ge(y_made, g - 1)
                    dve.tensor_tensor(flat(u[:, s, 0:tiles, :]), turned[s][:, 0:tiles * 128],
                                      flat(rows[:, s, 0:tiles, :]), ALU.add).then_inc(u_made, 1)
                    dve.wait_ge(u_made, g + 1)
                    norm_measure(norm, dve, u[:, s, 0:tiles, :], g, s, 128, tiles)

                def scale(g, s, r, tiles):
                    if reused(g):
                        dve.wait_ge(scattered[s], r * 16 * GT)
                    dve.tensor_copy(at[:, s, 0:tiles], o["store_at"][:, bass.ds(g * GT, tiles)]).then_inc(at_made, 1)
                    norm_invert(norm, dve, g, s, 128, tiles)
                    norm_scale(norm, dve, y[:, s, 0:tiles, :], u[:, s, 0:tiles, :], g, s, 128, tiles).then_inc(y_made, 1)
                edge_groups(dve, sh, (0, measure), (1, scale))

            @block.gpsimd
            def _(pool):
                scatter_rows(pool, sh, t["x2"], y, at, y_made, at_made, issuing, scattered)


def scatter_rows(pool, sh, table, y, at, y_made, at_made, issuing, scattered):
    last_node = pool.to_reg(sh["n"] - 1)

    def scatter(g, s, r, tiles):
        pool.wait_ge(at_made, g + 1)
        pool.wait_ge(y_made, g + 1)
        pool.sem_inc(issuing, 1)
        for j in range(tiles):
            pool.indirect_dma_start(
                out=table, out_offset=bass.IndirectOffsetOnAxis(ap=at[:, s, j:j + 1], axis=0),
                in_=y[:, s, j, :], in_offset=None, bounds_check=last_node, oob_is_err=False) \
                .then_inc(scattered[s], 16)
    edge_groups(pool, sh, (0, scatter))
    for s in range(2):
        pool.wait_ge(scattered[s], 16 * slot_tiles(sh, s))


def compose_buffers(nc, ctx, w):
    for name in ("bz_mc", "lone_m", "lone_mc"):
        w[name] = ctx.enter_context(nc.sbuf_tensor("w_" + name, [128, NT, 128], BF16))
    for name in ("wz", "w2l_r"):
        w[name] = ctx.enter_context(nc.sbuf_tensor("w_" + name, [128, 128], F32))


def compose_stage(nc, inner, semaphore, c, w):
    def sb(name):
        return inner.enter_context(nc.sbuf_tensor("co_" + name, [128, 128], F32))

    def sem(name):
        return semaphore("co_" + name)

    spread, bz, z, size, decayed, logged, lone, whole, centred = (
        sb(k) for k in ("spread", "bz", "z", "size", "decayed", "logged", "lone", "whole", "centred"))
    total = inner.enter_context(nc.sbuf_tensor("co_total", [128, 1], F32))
    half = inner.enter_context(nc.sbuf_tensor("co_half", [128, 1], F32))
    products = inner.enter_context(nc.psum_tensor("co_products", [128, 512], F32))
    linked, spread_made, product, z_made, log_made, chained = (
        sem(k) for k in ("linked", "spread_made", "product", "z_made", "log_made", "chained"))
    def tensor(pe):
        pe.matmul(products[:, 0:128], w["w2n"][:, :], w["w2l_b"][:, :], start=True, stop=True)
        pe.matmul(products[:, 128:256], c["ones"][:, :], w["l3w3"][:, :], start=True, stop=True)
        pe.wait_ge(spread_made, 1)
        pe.matmul(products[:, 256:384], spread[:, :], w["w2l_b"][:, :], start=True, stop=True) \
            .then_inc(product, 1)
        return [], None

    def scalar(act):
        act.wait_ge(z_made, 1)
        act.activation(size[:, :], z[:, :], ACT.Abs).then_inc(chained, 1)
        act.wait_ge(chained, 1)
        act.activation(decayed[:, :], size[:, :], ACT.Exp, scale=-1.0).then_inc(chained, 1)
        act.wait_ge(chained, 2)
        act.activation(logged[:, :], decayed[:, :], ACT.Ln, scale=0.5, bias=half[:, :]).then_inc(log_made, 1)
        return [], None

    def vector(dve):
        done = [0]

        def link(instruction):
            instruction.then_inc(linked, 1)
            done[0] += 1
            dve.wait_ge(linked, done[0])
        dve.memset(half[:, :], 0.5)
        dve.tensor_scalar(spread[:, :], c["ones"][:, :], w["b2n"][:, :], None, ALU.mult).then_inc(spread_made, 1)
        dve.wait_ge(product, 1)
        dve.tensor_tensor(z[:, :], products[:, 128:256], w["l3b3"][:, :], ALU.add).then_inc(z_made, 1)
        link(dve.tensor_tensor(w["w2l_r"][:, :], w["w2l_a"][:, :], c["ident"][:, :], ALU.add))
        link(dve.tensor_tensor(whole[:, :], products[:, 0:128], w["w2l_r"][:, :], ALU.add))
        link(dve.tensor_tensor(bz[:, :], products[:, 256:384], w["b2l"][:, :], ALU.add))

        def centre(out, rows):
            link(dve.tensor_reduce(total[:, :], rows[:, :], AX.X, ALU.add))
            link(dve.tensor_scalar(total[:, :], total[:, :], 1.0 / D, None, ALU.mult))
            link(dve.tensor_scalar(out[:, :], rows[:, :], total[:, 0:1], None, ALU.subtract))
        centre(w["wz"], whole)
        centre(centred, bz)
        bias_parts(dve, link, w, centred, w["bz_mc"])
        dve.wait_ge(log_made, 1)
        link(dve.scalar_tensor_tensor(lone[:, :], z[:, :], 0.0, logged[:, :], ALU.max, ALU.add))
        bias_parts(dve, link, w, lone, w["lone_m"])
        centre(centred, lone)
        bias_parts(dve, link, w, centred, w["lone_mc"])
        return [], None
    return {"tensor": tensor, "scalar": scalar, "vector": vector}


def layer2_ends(nc, c, sh, t, w, o):
    with stage(nc) as (ctx, semaphore):
        def sb(name, shape, dt=F32):
            return ctx.enter_context(nc.sbuf_tensor("e2_" + name, shape, dt))

        def sem(name):
            return semaphore("e2_" + name)

        own_at, other_at, at = (sb(k, [128, 4, GT], I32) for k in ("own_at", "other_at", "at"))
        xa, xb = sb("xa", [128, 4, GT, 128]), sb("xb", [128, 4, GT, 128])
        xa_t, xb_t = sb("xa_t", [128, 2, GE]), sb("xb_t", [128, 2, GE])
        h_other, gap, new_h = sb("h_other", [128, GE]), sb("gap", [128, GE]), sb("new_h", [128, GE])
        seg_sum, count = sb("seg_sum", [128, 2, GE]), sb("count", [128, 2, GE])
        numerator, inverse, log_count = (sb(k, [128, GE]) for k in ("numerator", "inverse", "log_count"))
        mean = sb("mean", [128, 2, GE])
        u, u2, rows = sb("u", [128, 2, GT, 128]), sb("u2", [128, 2, GT, 128]), sb("rows", [128, 4, GT, 2 * D])
        y, y2 = rows[:, :, :, 0:D], rows[:, :, :, D:2 * D]
        turned_a, turned_b, h_ps, gap_ps, own_ps, new_ps, out_ps, lone_ps = (
            ctx.enter_context(nc.psum_tensor("e2_" + k, [128, 512], F32))
            for k in ("turned_a", "turned_b", "h_ps", "gap_ps", "own_ps", "new_ps", "out_ps", "lone_ps"))
        norm, norm2 = norm_buffers(nc, ctx, semaphore, "e2_norm", c["ln_eps"]), norm_buffers(nc, ctx, semaphore, "e2_norm2", c["ln_eps"])
        gathered = [sem(f"gathered{k}") for k in range(4)]
        scattered = [sem(f"scattered{k}") for k in range(4)]
        (at_made, x_turned, x_t_out, h_made, h_out, new_made, new_out, seg_made, count_made, num_made, inv_made,
         mean_made, out_made, u_made, y_made, u2_made, y2_made, lone_made, put_made, issuing) = (sem(k) for k in (
             "at_made", "x_turned", "x_t_out", "h_made", "h_out", "new_made", "new_out", "seg_made", "count_made",
             "num_made", "inv_made", "mean_made", "out_made", "u_made", "y_made", "u2_made", "y2_made", "lone_made",
             "put_made", "issuing"))
        log_made, own_made = sem("log_made"), sem("own_made")

        with nc.Block() as block:
            @block.gpsimd
            def _(pool):
                last_node = pool.to_reg(sh["n"] - 1)

                def gather(g, k, r, tiles):
                    if reused(g, 4):
                        pool.wait_ge(gathered[k], r * 32 * GT)
                    row_numbers(pool, own_at, k, tiles, o["own_at"], g, at_made)
                    row_numbers(pool, other_at, k, tiles, o["other_at"], g, at_made)
                    pool.wait_ge(at_made, 2 * g + 2)
                    if reused(g, 4):
                        pool.wait_ge(x_turned, g - 3)
                    pool.sem_inc(issuing, 1)
                    for j in range(tiles):
                        for to, numbers in ((xa, own_at), (xb, other_at)):
                            pool.indirect_dma_start(
                                out=to[:, k, j, :], out_offset=None, in_=t["x2"],
                                in_offset=bass.IndirectOffsetOnAxis(ap=numbers[:, k, j:j + 1], axis=0),
                                bounds_check=last_node, oob_is_err=False).then_inc(gathered[k], 16)

                def scatter(g, k, r, tiles):
                    if reused(g, 4):
                        pool.wait_ge(scattered[k], r * 16 * GT)
                    row_numbers(pool, at, k, tiles, o["store_at"], g, put_made)
                    pool.wait_ge(put_made, g + 1)
                    pool.wait_ge(y_made, g + 1)
                    pool.wait_ge(y2_made, g + 1)
                    pool.sem_inc(issuing, 1)
                    for j in range(tiles):
                        pool.indirect_dma_start(
                            out=t["last"], out_offset=bass.IndirectOffsetOnAxis(ap=at[:, k, j:j + 1], axis=0),
                            in_=rows[:, k, j, :], in_offset=None, bounds_check=last_node, oob_is_err=False) \
                            .then_inc(scattered[k], 16)
                edge_rings(pool, sh, (0, gather), (6, scatter))
                for k in range(4):
                    pool.wait_ge(scattered[k], 16 * slot_tiles(sh, k, 4))

            @block.tensor
            def _(pe):
                pe.matmul(lone_ps[:, :], c["onesb"][:, :], flat(w["lone_m"][:, :, :]), start=True, stop=True) \
                    .then_inc(lone_made, 1)

                def turn(g, k, r, tiles):
                    s = k % 2
                    pe.wait_ge(gathered[k], r * 32 * GT + 32 * tiles)
                    if reused(g, 1):
                        pe.wait_ge(x_t_out, g)
                    for j in range(tiles):
                        pe.transpose(turned_a[:, j * 128:(j + 1) * 128], xa[:, k, j, :], c["ident"][:, :])
                        last = pe.transpose(turned_b[:, j * 128:(j + 1) * 128], xb[:, k, j, :], c["ident"][:, :])
                    last.then_inc(x_turned, 1)

                def project(g, k, r, tiles):
                    s = k % 2
                    n = tiles * 128
                    pe.wait_ge(x_t_out, g + 1)
                    if reused(g, 1):
                        pe.wait_ge(h_out, g)
                    pe.matmul(h_ps[:, 0:n], w["w2n_t"][:, :], xb_t[:, s, 0:n], start=True, stop=True)
                    pe.matmul(gap_ps[:, 0:n], w["w2n_t"][:, :], xa_t[:, s, 0:n], start=True, stop=False)
                    pe.matmul(gap_ps[:, 0:n], w["w2n_neg"][:, :], xb_t[:, s, 0:n], start=False, stop=True) \
                        .then_inc(h_made, 1)
                    if reused(g, 1):
                        pe.wait_ge(num_made, g)
                    pe.matmul(own_ps[:, 0:n], w["w2n_t"][:, :], xa_t[:, s, 0:n], start=True, stop=True) \
                        .then_inc(own_made, 1)

                def edge(g, k, r, tiles):
                    s = k % 2
                    n = tiles * 128
                    pe.wait_ge(h_out, g + 1)
                    if reused(g, 1):
                        pe.wait_ge(new_out, g)
                    pe.matmul(new_ps[:, 0:n], w["w2e_a"][:, :], h_other[:, 0:n], start=True, stop=False)
                    pe.matmul(new_ps[:, 0:n], w["w2e_b"][:, :], gap[:, 0:n], start=False, stop=True) \
                        .then_inc(new_made, 1)

                def combine(g, k, r, tiles):
                    s = k % 2
                    pe.wait_ge(mean_made, g + 1)
                    if reused(g, 1):
                        pe.wait_ge(u_made, g)
                    pe.matmul(out_ps[:, 0:tiles * 128], c["onesb"][:, :], flat(w["b2l_m"][:, 0:tiles, :]), start=True,
                              stop=False, skip_group_check=True)
                    for j in range(tiles):
                        cols = slice(j * 128, (j + 1) * 128)
                        pe.matmul(out_ps[:, cols], xa_t[:, s, cols], w["w2l_r"][:, :], start=False, stop=True,
                                  skip_group_check=True)
                        last = pe.matmul(out_ps[:, cols], mean[:, s, cols], w["w2l_b"][:, :], start=False, stop=True,
                                         skip_group_check=True)
                    last.then_inc(out_made, 1)
                edge_rings(pe, sh, (0, turn), (1, project), (2, combine), (1, edge))

            @block.scalar
            def _(act):
                def copies(g, k, r, tiles):
                    s = k % 2
                    n = tiles * 128
                    act.wait_ge(x_turned, g + 1)
                    if reused(g):
                        act.wait_ge(out_made, g - 1)
                    act.activation(xa_t[:, s, 0:n], turned_a[:, 0:n], ACT.Copy)
                    act.activation(xb_t[:, s, 0:n], turned_b[:, 0:n], ACT.Copy).then_inc(x_t_out, 1)

                def logs(g, k, r, tiles):
                    s, n = k % 2, tiles * 128
                    act.wait_ge(count_made, g + 1)
                    if reused(g, 1):
                        act.wait_ge(inv_made, g)
                    act.activation(log_count[:, 0:n], count[:, s, 0:n], ACT.Ln).then_inc(log_made, 1)

                def invert(g, k, r, tiles):
                    n = tiles * 128
                    act.wait_ge(log_made, g + 1)
                    if reused(g, 1):
                        act.wait_ge(mean_made, g)
                    act.activation(inverse[:, 0:n], log_count[:, 0:n], ACT.Exp, scale=-1.0).then_inc(inv_made, 1)

                def edge(g, k, r, tiles):
                    n = tiles * 128
                    act.wait_ge(h_made, g + 1)
                    if reused(g, 1):
                        act.wait_ge(new_made, g)
                    act.activation(h_other[:, 0:n], h_ps[:, 0:n], ACT.Identity, bias=w["b2n"][:, :])
                    act.activation(gap[:, 0:n], gap_ps[:, 0:n], ACT.Abs).then_inc(h_out, 1)
                    act.wait_ge(new_made, g + 1)
                    if reused(g, 1):
                        act.wait_ge(seg_made, g)
                    act.activation(new_h[:, 0:n], new_ps[:, 0:n], ACT.Identity, bias=w["b2e"][:, :]).then_inc(new_out, 1)
                edge_rings(act, sh, (0, copies), (1, edge), (1, logs), (1, invert),
                           (3, lambda g, k, r, tiles: norm_deviation(norm, act, g, k % 2, 128, tiles)),
                           (4, lambda g, k, r, tiles: norm_deviation(norm2, act, g, k % 2, 128, tiles)))

            @block.vector
            def _(dve):
                dve.wait_ge(lone_made, 1)

                def aggregate(g, k, r, tiles):
                    s = k % 2
                    n = tiles * 128
                    joined = o["joined"][:, bass.ds(g * GE, n)]
                    if reused(g, 1):
                        dve.wait_ge(count_made, g)
                        dve.wait_ge(mean_made, g)
                    if reused(g):
                        dve.wait_ge(log_made, g - 1)
                    dve.tensor_tensor_scan(count[:, s, 0:n], joined, c["ones"][:, 0:1].to_broadcast([128, n]),
                                           count[:, 1 - s, GE - 1:GE] if reused(g, 1) else 0.0,
                                           ALU.mult, ALU.add).then_inc(count_made, 1)
                    dve.wait_ge(new_out, g + 1)
                    if reused(g, 1):
                        dve.wait_ge(seg_made, g)
                    dve.tensor_tensor_scan(seg_sum[:, s, 0:n], joined, new_h[:, 0:n],
                                           seg_sum[:, 1 - s, GE - 1:GE] if reused(g, 1) else 0.0,
                                           ALU.mult, ALU.add).then_inc(seg_made, 1)
                    dve.wait_ge(seg_made, g + 1)
                    dve.wait_ge(own_made, g + 1)
                    dve.scalar_tensor_tensor(numerator[:, 0:n], own_ps[:, 0:n], w["b2n"][:, :], seg_sum[:, s, 0:n],
                                             ALU.add, ALU.add).then_inc(num_made, 1)
                    dve.wait_ge(num_made, g + 1)
                    dve.wait_ge(inv_made, g + 1)
                    if reused(g):
                        dve.wait_ge(out_made, g - 1)
                    dve.tensor_tensor(mean[:, s, 0:n], numerator[:, 0:n], inverse[:, 0:n], ALU.mult) \
                        .then_inc(mean_made, 1)

                def measure(g, k, r, tiles):
                    s = k % 2
                    dve.wait_ge(out_made, g + 1)
                    if reused(g):
                        dve.wait_ge(y_made, g - 1)
                    dve.tensor_copy(flat(u[:, s, 0:tiles, :]), out_ps[:, 0:tiles * 128]).then_inc(u_made, 1)
                    dve.wait_ge(u_made, g + 1)
                    norm_measure(norm, dve, u[:, s, 0:tiles, :], g, s, 128, tiles)

                def scale(g, k, r, tiles):
                    s = k % 2
                    if reused(g):
                        dve.wait_ge(u2_made, g - 1)
                    if reused(g, 4):
                        dve.wait_ge(scattered[k], r * 16 * GT)
                    norm_invert(norm, dve, g, s, 128, tiles)
                    norm_scale(norm, dve, y[:, k, 0:tiles, :], u[:, s, 0:tiles, :], g, s, 128, tiles).then_inc(y_made, 1)

                def measure2(g, k, r, tiles):
                    s = k % 2
                    dve.wait_ge(y_made, g + 1)
                    if reused(g):
                        dve.wait_ge(y2_made, g - 1)
                    dve.tensor_tensor(u2[:, s, 0:tiles, :], lone_ps[:, 0:tiles * 128].rearrange("p (t f) -> p t f", f=D),
                                      y[:, k, 0:tiles, :], ALU.add).then_inc(u2_made, 1)
                    dve.wait_ge(u2_made, g + 1)
                    norm_measure(norm2, dve, u2[:, s, 0:tiles, :], g, s, 128, tiles)

                def scale2(g, k, r, tiles):
                    s = k % 2
                    if reused(g, 4):
                        dve.wait_ge(scattered[k], r * 16 * GT)
                    norm_invert(norm2, dve, g, s, 128, tiles)
                    norm_scale(norm2, dve, y2[:, k, 0:tiles, :], u2[:, s, 0:tiles, :], g, s, 128, tiles).then_inc(y2_made, 1)
                edge_rings(dve, sh, (0, aggregate), (1, measure), (2, scale), (2, measure2), (3, scale2))


def layer3_ends(nc, c, sh, t, w, o):
    with stage(nc) as (ctx, semaphore):
        def sb(name, shape, dt=F32):
            return ctx.enter_context(nc.sbuf_tensor("e3_" + name, shape, dt))

        def sem(name):
            return semaphore("e3_" + name)

        own_at, other_at, at = (sb(k, [128, 4, GT], I32) for k in ("own_at", "other_at", "at"))
        xa, xb = sb("xa", [128, 4, GT, 128]), sb("xb", [128, 4, GT, 128])
        factor, message = sb("factor", [128, 4, GT, 128]), sb("message", [128, 2, GT, 128])
        times, restart = sb("times", [128, GE]), sb("restart", [128, GE])
        product = sb("product", [128, 2, GE])
        size, decayed, logged = sb("size", [128, GE]), sb("decayed", [128, GE]), sb("logged", [128, GE])
        z, u, y = sb("z", [128, 2, GT, 128]), sb("u", [128, 2, GT, 128]), sb("y", [128, 4, GT, 128])
        half = sb("half", [128, 1])
        turned, out_ps = (ctx.enter_context(nc.psum_tensor("e3_" + k, [128, 512], F32)) for k in ("turned", "out_ps"))
        norm = norm_buffers(nc, ctx, semaphore, "e3_norm", c["ln_eps"])
        halves = t["last"].rearrange("n (h f) -> (n h) f", h=2)
        own, other, store = (sb(k, [128, sh["et"]], I32) for k in ("own", "other", "store"))
        doubled = sem("doubled")
        gathered = [sem(f"gathered{k}") for k in range(4)]
        factor_in = [sem(f"factor_in{k}") for k in range(4)]
        scattered = [sem(f"scattered{k}") for k in range(4)]
        (at_made, half_made, message_made, message_turned, times_made, restart_made, product_made, out_made, size_made,
         decay_made, log_made, z_made, u_made, y_made, put_made, issuing) = (sem(k) for k in (
             "at_made", "half_made", "message_made", "message_turned", "times_made", "restart_made", "product_made",
             "out_made", "size_made", "decay_made", "log_made", "z_made", "u_made", "y_made", "put_made", "issuing"))

        with nc.Block() as block:
            @block.sync
            def _(sp):
                def load(g, k, r, tiles):
                    if reused(g, 4):
                        sp.wait_ge(message_made, g - 3)
                    sp.dma_start(factor[:, k, 0:tiles, :], edge_rows(t["rows_d"], g, tiles, 1, slice(256, 384))) \
                        .then_inc(factor_in[k], 16)
                edge_rings(sp, sh, (0, load))

            @block.gpsimd
            def _(pool):
                last_half = pool.to_reg(2 * sh["n"] - 1)
                pool.wait_ge(doubled, 3)

                def gather(g, k, r, tiles):
                    if reused(g, 4):
                        pool.wait_ge(gathered[k], r * 32 * GT)
                    row_numbers(pool, own_at, k, tiles, own, g, at_made)
                    row_numbers(pool, other_at, k, tiles, other, g, at_made)
                    pool.wait_ge(at_made, 2 * g + 2)
                    if reused(g, 4):
                        pool.wait_ge(message_made, g - 3)
                        pool.wait_ge(u_made, g - 3)
                    pool.sem_inc(issuing, 1)
                    for j in range(tiles):
                        for to, numbers in ((xa, own_at), (xb, other_at)):
                            pool.indirect_dma_start(
                                out=to[:, k, j, :], out_offset=None, in_=halves,
                                in_offset=bass.IndirectOffsetOnAxis(ap=numbers[:, k, j:j + 1], axis=0),
                                bounds_check=last_half, oob_is_err=False).then_inc(gathered[k], 16)

                def scatter(g, k, r, tiles):
                    if reused(g, 4):
                        pool.wait_ge(scattered[k], r * 16 * GT)
                    row_numbers(pool, at, k, tiles, store, g, put_made)
                    pool.wait_ge(put_made, g + 1)
                    pool.wait_ge(y_made, g + 1)
                    pool.sem_inc(issuing, 1)
                    for j in range(tiles):
                        pool.indirect_dma_start(
                            out=halves, out_offset=bass.IndirectOffsetOnAxis(ap=at[:, k, j:j + 1], axis=0),
                            in_=y[:, k, j, :], in_offset=None, bounds_check=last_half, oob_is_err=False) \
                            .then_inc(scattered[k], 16)
                edge_rings(pool, sh, (0, gather), (5, scatter))
                for k in range(4):
                    pool.wait_ge(scattered[k], 16 * slot_tiles(sh, k, 4))

            @block.tensor
            def _(pe):
                def turn(g, k, r, tiles):
                    s = k % 2
                    pe.wait_ge(message_made, g + 1)
                    if reused(g, 1):
                        pe.wait_ge(product_made, g)
                    for j in range(tiles):
                        last = pe.transpose(turned[:, j * 128:(j + 1) * 128], message[:, s, j, :], c["ident"][:, :])
                    last.then_inc(message_turned, 1)

                def project(g, k, r, tiles):
                    s = k % 2
                    pe.wait_ge(product_made, g + 1)
                    if reused(g, 1):
                        pe.wait_ge(z_made, g)
                    pe.matmul(out_ps[:, 0:tiles * 128], c["onesb"][:, :], flat(w["l3b3_m"][:, 0:tiles, :]), start=True,
                              stop=False, skip_group_check=True)
                    for j in range(tiles):
                        cols = slice(j * 128, (j + 1) * 128)
                        last = pe.matmul(out_ps[:, cols], product[:, s, cols], w["l3w3"][:, :], start=False, stop=True,
                                         skip_group_check=True)
                    last.then_inc(out_made, 1)
                edge_rings(pe, sh, (0, turn), (1, project))

            @block.scalar
            def _(act):
                act.wait_ge(half_made, 1)

                def softplus(g, k, r, tiles):
                    n = tiles * 128
                    act.wait_ge(out_made, g + 1)
                    if reused(g, 1):
                        act.wait_ge(decay_made, g)
                    act.activation(size[:, 0:n], out_ps[:, 0:n], ACT.Abs).then_inc(size_made, 1)
                    act.wait_ge(size_made, g + 1)
                    if reused(g, 1):
                        act.wait_ge(log_made, g)
                    act.activation(decayed[:, 0:n], size[:, 0:n], ACT.Exp, scale=-1.0).then_inc(decay_made, 1)
                    act.wait_ge(decay_made, g + 1)
                    if reused(g, 1):
                        act.wait_ge(z_made, g)
                    act.activation(logged[:, 0:n], decayed[:, 0:n], ACT.Ln, scale=0.5, bias=half[:, :]) \
                        .then_inc(log_made, 1)
                edge_rings(act, sh, (0, softplus), (2, lambda g, k, r, tiles: norm_deviation(norm, act, g, k % 2, 128, tiles)))

            @block.vector
            def _(dve):
                dve.tensor_scalar(own[:, :], o["own_at"][:, :], 2.0, None, ALU.mult).then_inc(doubled, 1)
                dve.tensor_scalar(other[:, :], o["other_at"][:, :], 2.0, None, ALU.mult).then_inc(doubled, 1)
                dve.tensor_scalar(store[:, :], o["store_at"][:, :], 2.0, 1.0, ALU.mult, ALU.add).then_inc(doubled, 1)
                dve.memset(half[:, :], 0.5).then_inc(half_made, 1)

                def multiply(g, k, r, tiles):
                    s = k % 2
                    dve.wait_ge(gathered[k], r * 32 * GT + 32 * tiles)
                    dve.wait_ge(factor_in[k], r * 16 + 16)
                    if reused(g):
                        dve.wait_ge(message_turned, g - 1)
                    dve.tensor_tensor(flat(message[:, s, 0:tiles, :]), flat(xb[:, k, 0:tiles, :]),
                                      flat(factor[:, k, 0:tiles, :]), ALU.mult).then_inc(message_made, 1)

                def product_up(g, k, r, tiles):
                    s = k % 2
                    n = tiles * 128
                    dve.wait_ge(message_turned, g + 1)
                    if reused(g, 1):
                        dve.wait_ge(product_made, g)
                    dve.tensor_tensor(times[:, 0:n], turned[:, 0:n], o["joined"][:, bass.ds(g * GE, n)], ALU.mult) \
                        .then_inc(times_made, 1)
                    dve.wait_ge(times_made, g + 1)
                    dve.tensor_tensor(restart[:, 0:n], turned[:, 0:n], times[:, 0:n], ALU.subtract) \
                        .then_inc(restart_made, 1)
                    dve.wait_ge(restart_made, g + 1)
                    if reused(g):
                        dve.wait_ge(out_made, g - 1)
                    dve.tensor_tensor_scan(product[:, s, 0:n], times[:, 0:n], restart[:, 0:n],
                                           product[:, 1 - s, GE - 1:GE] if reused(g, 1) else 1.0,
                                           ALU.mult, ALU.add).then_inc(product_made, 1)

                def measure(g, k, r, tiles):
                    s = k % 2
                    dve.wait_ge(out_made, g + 1)
                    dve.wait_ge(log_made, g + 1)
                    if reused(g):
                        dve.wait_ge(u_made, g - 1)
                    dve.scalar_tensor_tensor(flat(z[:, s, 0:tiles, :]), out_ps[:, 0:tiles * 128], 0.0,
                                             logged[:, 0:tiles * 128], ALU.max, ALU.add).then_inc(z_made, 1)
                    dve.wait_ge(z_made, g + 1)
                    if reused(g):
                        dve.wait_ge(y_made, g - 1)
                    dve.tensor_tensor(flat(u[:, s, 0:tiles, :]), flat(z[:, s, 0:tiles, :]),
                                      flat(xa[:, k, 0:tiles, :]), ALU.add).then_inc(u_made, 1)
                    dve.wait_ge(u_made, g + 1)
                    norm_measure(norm, dve, u[:, s, 0:tiles, :], g, s, 128, tiles)

                def scale(g, k, r, tiles):
                    s = k % 2
                    if reused(g, 4):
                        dve.wait_ge(scattered[k], r * 16 * GT)
                    norm_invert(norm, dve, g, s, 128, tiles)
                    norm_scale(norm, dve, y[:, k, 0:tiles, :], u[:, s, 0:tiles, :], g, s, 128, tiles).then_inc(y_made, 1)
                edge_rings(dve, sh, (0, multiply), (1, product_up), (2, measure), (3, scale))


def program(nc, t, n, edge_tiles, pads):
    sh = shapes(n, edge_tiles, pads)
    with stage(nc) as (ctx, semaphore):
        c = constants(nc, ctx, semaphore, sh)
        w = load_weights(nc, ctx, semaphore, c, sh, t)
        pos_d = ctx.enter_context(nc.sbuf_tensor("pos_d", [128, sh["et"]], I32))
        pos_s = ctx.enter_context(nc.sbuf_tensor("pos_s", [128, sh["et"]], I32))
        gram = ctx.enter_context(nc.sbuf_tensor("gram", [128, 129], F32))
        sums = ctx.enter_context(nc.sbuf_tensor("sums", [128, 2], F32))
        bn = {"scale": ctx.enter_context(nc.sbuf_tensor("scale", [128, 1], F32)),
              "shift": ctx.enter_context(nc.sbuf_tensor("shift", [128, 1], F32)),
              "w1": ctx.enter_context(nc.sbuf_tensor("w1_scaled", [128, 128], F32)),
              "shift_m": ctx.enter_context(nc.sbuf_tensor("shift_m", [128, NT, 128], BF16))}
        sort_positions(nc, c, sh, [("by_dst", t["dst_cols"], t["dst_flat"], pos_d, t["cnt"]),
                                   ("by_src", t["src_cols"], t["src_flat"], pos_s, None)])
        with stage(nc) as (inner, inner_semaphore):
            run_stages(nc, sh, edge_rows_stage(nc, inner, inner_semaphore, c, sh, t, w, pos_d, pos_s),
                       dense_stage(nc, inner, inner_semaphore, c, sh, "d0", t["x"], t["x1"], w["w0x"], w["b0_m"],
                                   c["ln_eps"], gram=(t["cnt"], gram)))
        compose_buffers(nc, ctx, w)
        o = order_buffers(nc, ctx, sh, "by_end")
        with stage(nc) as (inner, inner_semaphore):
            run_stages(nc, sh, order_stage(nc, inner, inner_semaphore, c, sh, "od", o, t["rows_d"], END),
                       compose_stage(nc, inner, inner_semaphore, c, w))
        with stage(nc) as (inner, semaphore):
            mixed = inner.enter_context(nc.sbuf_tensor("mixed", [128, sh["ep"]], F32))
            layer0_ends(nc, c, sh, t, w, o)
            attention(nc, c, sh, t, w, o, mixed, sums)
            batch_norm(nc, c, sh, w, gram, sums, bn)
            with stage(nc) as (inner2, inner_semaphore):
                run_stages(nc, sh, node_stage=dense_stage(nc, inner2, inner_semaphore, c, sh, "d1", t["x1"], t["x2"],
                                                          bn["w1"], bn["shift_m"], c["ln_eps4"]))
            layer1_ends(nc, c, sh, t, o, mixed, bn)
        with stage(nc) as (outer, _):
            o_start = order_buffers(nc, outer, sh, "by_start")
            with stage(nc) as (inner, inner_semaphore):
                run_stages(nc, sh, order_stage(nc, inner, inner_semaphore, c, sh, "os", o_start, t["rows_s"], 0),
                           last_dense_stage(nc, inner, inner_semaphore, c, sh, w, t["x2"], t["last"]))
            layer2_ends(nc, c, sh, t, w, o_start)
        layer3_ends(nc, c, sh, t, w, o)


def kernel(**inputs):
    import numpy as _np
    import concourse.bacc as _bacc
    from concourse import mybir as _mybir
    from concourse.bass_utils import run_bass_kernel_spmd as _run

    nc = _bacc.Bacc("TRN2", target_bir_lowering=False, num_devices=1)
    a = {k: _np.asarray(v) for k, v in inputs.items()}
    n, e = a["x"].shape[0], a["dst"].shape[0]
    tiles = -(-e // 128)
    pad = tiles * 128 - e
    f32 = _mybir.dt.float32
    arrays, t = {}, {}

    def put(name, array):
        arrays[name] = _np.ascontiguousarray(array)
        t[name] = nc.dram_tensor(name, arrays[name].shape, _mybir.dt.from_np(arrays[name].dtype),
                                 kind="ExternalInput").ap()

    beyond = n // 128 * 128 + 127
    for name in ("dst", "src"):
        flat_ = _np.concatenate([a[name], _np.full((pad,), beyond, a[name].dtype)])
        put(name + "_flat", flat_)
        put(name + "_cols", flat_.reshape(tiles, 128).T)
    weight = _np.concatenate([a["edge_weight"], _np.zeros((pad,), a["edge_weight"].dtype)])
    put("weight_flat", weight)
    put("weight_cols", weight.reshape(tiles, 128).T)
    put("edge_attr", _np.concatenate([a["edge_attr_128"], _np.zeros((pad, 128), a["edge_attr_128"].dtype)]))
    put("x", a["x"])
    w0, wl, we = a["L0_gnn_W"].T, a["L2_gnn_W_lin"].T, a["L2_gnn_W_edge"].T
    squares = {"w0x": w0[0:128], "w0s": w0[128:256], "w0e": w0[256:384], "w1": a["L1_gnn_W"],
               "w2n": a["L2_gnn_W_neigh"], "w2n_t": a["L2_gnn_W_neigh"].T, "w2e_a": we[0:128], "w2e_b": we[128:256],
               "w2l_a": wl[0:128], "w2l_b": wl[128:256],
               "l3w1": a["L3_gnn_W1"], "l3w2": a["L3_gnn_W2"], "l3w3": a["L3_gnn_W3"]}
    vectors = {"b0": "L0_gnn_b", "b2n": "L2_gnn_b_neigh", "b2e": "L2_gnn_b_edge", "b2l": "L2_gnn_b_lin",
               "l3b1": "L3_gnn_b1", "l3b2": "L3_gnn_b2", "l3b3": "L3_gnn_b3", "bias1": "L1_gnn_bias",
               "gamma": "L1_gnn_bn_gamma", "beta": "L1_gnn_bn_beta"}
    for name, array in squares.items():
        put(name, array)
    for name, key in vectors.items():
        put(name, a[key])
    put("att_s", a["L1_gnn_att_src"].reshape(128))
    put("att_d", a["L1_gnn_att_dst"].reshape(128))
    put("neg_mu", -_np.linspace(0.0, 1.0, 128, dtype=_np.float32))
    sh = shapes(n, tiles, pad)

    def scratch(name, shape, kind="Internal"):
        t[name] = nc.dram_tensor(name, shape, f32, kind=kind).ap()

    scratch("last", [n, 256], "ExternalOutput")
    for name in ("x1", "x2"):
        scratch(name, [n, 128])
    scratch("x1_ends", [sh["ep"], 128])
    scratch("cnt", [sh["hc"] * 128 * 128])
    scratch("rows_d", [sh["ep"] + 2, ROW])
    scratch("rows_s", [sh["ep"] + 2, 2])
    program(nc, t, n, tiles, pad)
    r = _run(nc, [arrays], core_ids=[0])
    return _np.ascontiguousarray(r.results[0]["last"][:, 128:256])
```
